# Optimizing a Trainium2 kernel written in Bass

```python
import numpy as np
import jax
import jax.numpy as jnp

def _softmax(x, axis=-1):
    return jax.nn.softmax(x, axis=axis)

def _gelu(x):
    return jax.nn.gelu(x, approximate=True)

def _silu(x):
    return jax.nn.silu(x)

def _sigmoid(x):
    return jax.nn.sigmoid(x)

def _layernorm(x, axis=-1, eps=1e-05):
    m = jnp.mean(x, axis=axis, keepdims=True)
    v = jnp.var(x, axis=axis, keepdims=True)
    return (x - m) / jnp.sqrt(v + eps)

def _scatter_add(tgt, idx, src, axis=0):
    return tgt.at[idx].add(src)

def _segment_sum(src, seg, n):
    return jax.ops.segment_sum(src, seg, n)
kernel_name = 'mk_gnn_ffn_d2_gnn_r32_d09f75'

def setup_inputs(seed: int=0):
    np.random.seed(seed)
    _w = jnp.asarray

    def _rec_inputs():
        import jax
        import jax.numpy as jnp
        _gk = jax.random.key(seed)
        x = -0.0002117 + 1 * jax.random.normal(jax.random.fold_in(_gk, 1), (3125, 256), jnp.float32)
        src = jax.random.randint(jax.random.fold_in(_gk, 2), (50000,), 0, 3125, jnp.int32)
        dst = jax.random.randint(jax.random.fold_in(_gk, 3), (50000,), 0, 3125, jnp.int32)
        _o = jnp.argsort(dst, stable=True)
        src = src[_o]
        dst = dst[_o]
        edge_weight = jax.random.uniform(jax.random.fold_in(_gk, 13), (50000,), jnp.float32, 0.0, 1)
        return (x, src, dst, edge_weight)
    x, src, dst, edge_weight = _rec_inputs()

    def _L0_gnn_setup():
        import jax, jax.numpy as jnp
        import numpy as np
        N_NODES = 3125
        N_EDGES = 100000
        D = 256

        def _graph_conv(x, W, edge_src, edge_dst, edge_weight, n_nodes):
            support = x @ W
            msg = support[edge_src] * edge_weight[:, None]
            return jax.ops.segment_sum(msg, edge_dst, num_segments=n_nodes)
        key = jax.random.key(seed)
        k1, k2, k3, k4, k5, k6 = jax.random.split(key, 6)
        scale = 1.0 / np.sqrt(D)
        return {'features': jax.random.normal(k1, (N_NODES, D), dtype=jnp.float32), 'edge_weight': jax.random.uniform(k2, (N_EDGES,), dtype=jnp.float32), 'W1': jax.random.normal(k3, (D, D), dtype=jnp.float32) * scale, 'W2': jax.random.normal(k4, (D, D), dtype=jnp.float32) * scale, 'edge_src': jax.random.randint(k5, (N_EDGES,), 0, N_NODES, dtype=jnp.int32), 'edge_dst': jax.random.randint(k6, (N_EDGES,), 0, N_NODES, dtype=jnp.int32)}
    _L0_gnn_all = _L0_gnn_setup()
    _L0_gnn_in = {k: v for k, v in _L0_gnn_all.items() if k in ('W1', 'W2')}
    del _L0_gnn_all

    def _L0_ffn_setup():
        import math
        import jax, jax.numpy as jnp
        import numpy as np
        CAPACITY_FACTOR = 1.25
        key = jax.random.key(seed)
        ks = jax.random.split(key, 5)
        B, L, D, F, E = (8, 256, 256, 1024, 8)
        h = jax.random.normal(ks[0], (B, L, D), dtype=jnp.float32)
        gate_w = jax.random.normal(ks[1], (D, E), dtype=jnp.float32) * 0.02
        gate_b = jnp.zeros((E,), dtype=jnp.float32)
        w1 = jax.random.normal(ks[2], (E, D, F), dtype=jnp.float32) * (1.0 / math.sqrt(D))
        b1 = jnp.zeros((E, F), dtype=jnp.float32)
        w2 = jax.random.normal(ks[3], (E, F, D), dtype=jnp.float32) * (1.0 / math.sqrt(F))
        b2 = jnp.zeros((E, D), dtype=jnp.float32)
        return {'h': h, 'gate_w': gate_w, 'gate_b': gate_b, 'w1': w1, 'b1': b1, 'w2': w2, 'b2': b2}
    _L0_ffn_all = _L0_ffn_setup()
    _L0_ffn_in = {k: v for k, v in _L0_ffn_all.items() if k in ('gate_w', 'gate_b', 'w1', 'b1', 'w2', 'b2')}
    del _L0_ffn_all

    def _L1_gnn_setup():
        import jax, jax.numpy as jnp
        import numpy as np
        N = 625
        E = 10000
        D_IN = 256
        HID = 64
        HEADS = 4
        D_OUT = 256
        EPS = 1e-05
        SLOPE = 0.2

        def _gat(x, src, dst, W, a_src, a_dst, b, heads, ch, concat):
            n = x.shape[0]
            h = (x @ W).reshape(n, heads, ch)
            es = (h * a_src).sum(-1)
            ed = (h * a_dst).sum(-1)
            e = jax.nn.leaky_relu(es[src] + ed[dst], SLOPE)
            m = jax.ops.segment_max(e, dst, num_segments=n)
            w = jnp.exp(e - m[dst])
            den = jax.ops.segment_sum(w, dst, num_segments=n)
            alpha = w / den[dst]
            msg = h[src] * alpha[:, :, None]
            out = jax.ops.segment_sum(msg, dst, num_segments=n)
            out = out.reshape(n, heads * ch) if concat else out.mean(axis=1)
            return out + b

        def _layernorm(x, g, b):
            mu = x.mean(-1, keepdims=True)
            v = ((x - mu) ** 2).mean(-1, keepdims=True)
            return (x - mu) * jax.lax.rsqrt(v + EPS) * g + b
        key = jax.random.key(seed)
        ks = jax.random.split(key, 10)

        def glorot(k, shape):
            fan_in, fan_out = (shape[0], int(np.prod(shape[1:])))
            s = np.sqrt(2.0 / (fan_in + fan_out)).astype(np.float32)
            return jax.random.normal(k, shape, dtype=jnp.float32) * s
        x = jax.random.normal(ks[0], (N, D_IN), dtype=jnp.float32)
        edge_index = jax.random.randint(ks[1], (2, E), 0, N, dtype=jnp.int64)
        return {'x': x, 'edge_index': edge_index, 'W1': glorot(ks[2], (D_IN, HEADS * HID)), 'a1_src': glorot(ks[3], (HEADS, HID)), 'a1_dst': glorot(ks[4], (HEADS, HID)), 'b1': jnp.zeros((HEADS * HID,), jnp.float32), 'ln_g': jnp.ones((HEADS * HID,), jnp.float32), 'ln_b': jnp.zeros((HEADS * HID,), jnp.float32), 'W2': glorot(ks[5], (HEADS * HID, D_OUT)), 'a2_src': glorot(ks[6], (1, D_OUT)), 'a2_dst': glorot(ks[7], (1, D_OUT)), 'b2': jnp.zeros((D_OUT,), jnp.float32)}
    _L1_gnn_all = _L1_gnn_setup()
    _L1_gnn_in = {k: v for k, v in _L1_gnn_all.items() if k in ('W1', 'a1_src', 'a1_dst', 'b1', 'ln_g', 'ln_b', 'W2', 'a2_src', 'a2_dst', 'b2')}
    del _L1_gnn_all

    def _L1_ffn_setup():
        import jax, jax.numpy as jnp
        import numpy as np
        B, N, D = (16, 128, 256)
        NUM_EXPERTS, TOP_K, HEADS = (4, 2, 4)
        N_EDGES = 32768
        LN_EPS = 1e-05

        def _layernorm(x, g, b):
            mu = x.mean(-1, keepdims=True)
            var = ((x - mu) ** 2).mean(-1, keepdims=True)
            return (x - mu) * jax.lax.rsqrt(var + LN_EPS) * g + b

        def _forward(x, edge_index, W_gat, att_src, att_dst, b_gat, ln_gamma, ln_beta, W1, b1, W2, b2):
            Bc, Nc, Dc = x.shape
            M = Bc * Nc
            x_flat = x.reshape(M, Dc)
            h = (x_flat @ W_gat).reshape(M, HEADS, NUM_EXPERTS)
            loops = jnp.arange(M, dtype=edge_index.dtype)
            src = jnp.concatenate([edge_index[0], loops])
            dst = jnp.concatenate([edge_index[1], loops])
            a_src = (h * att_src).sum(-1)
            a_dst = (h * att_dst).sum(-1)
            e = jax.nn.leaky_relu(a_src[src] + a_dst[dst], negative_slope=0.2)
            e_max = jax.ops.segment_max(e, dst, num_segments=M)
            ee = jnp.exp(e - e_max[dst])
            denom = jax.ops.segment_sum(ee, dst, num_segments=M)
            alpha = ee / (denom[dst] + 1e-16)
            msg = h[src] * alpha[:, :, None]
            agg = jax.ops.segment_sum(msg, dst, num_segments=M).reshape(M, HEADS * NUM_EXPERTS) + b_gat
            scores = _layernorm(agg, ln_gamma, ln_beta).reshape(M, HEADS, NUM_EXPERTS).mean(1)
            scores = scores.reshape(Bc, Nc, NUM_EXPERTS)
            topk_s, topk_i = jax.lax.top_k(scores, TOP_K)
            w = jax.nn.softmax(topk_s, axis=-1)
            out = jnp.zeros_like(x)
            for ei in range(NUM_EXPERTS):
                g = jnp.where(topk_i == ei, w, 0.0).sum(-1)
                hh = jax.nn.gelu(x @ W1[ei] + b1[ei], approximate=False)
                out = out + g[..., None] * (hh @ W2[ei] + b2[ei])
            return out
        key = jax.random.key(seed)
        ks = jax.random.split(key, 8)
        s = 0.05
        return {'x': jax.random.normal(ks[0], (B, N, D), jnp.float32), 'W_gat': jax.random.normal(ks[1], (D, HEADS * NUM_EXPERTS), jnp.float32) * s, 'att_src': jax.random.normal(ks[2], (HEADS, NUM_EXPERTS), jnp.float32) * s, 'att_dst': jax.random.normal(ks[3], (HEADS, NUM_EXPERTS), jnp.float32) * s, 'b_gat': jnp.zeros((HEADS * NUM_EXPERTS,), jnp.float32), 'ln_gamma': jnp.ones((HEADS * NUM_EXPERTS,), jnp.float32), 'ln_beta': jnp.zeros((HEADS * NUM_EXPERTS,), jnp.float32), 'W1': jax.random.normal(ks[4], (NUM_EXPERTS, D, 2 * D), jnp.float32) * s, 'b1': jnp.zeros((NUM_EXPERTS, 2 * D), jnp.float32), 'W2': jax.random.normal(ks[5], (NUM_EXPERTS, 2 * D, D), jnp.float32) * s, 'b2': jnp.zeros((NUM_EXPERTS, D), jnp.float32), 'edge_index': jax.random.randint(ks[6], (2, N_EDGES), 0, B * N, jnp.int32)}
    _L1_ffn_all = _L1_ffn_setup()
    _L1_ffn_in = {k: v for k, v in _L1_ffn_all.items() if k in ('W_gat', 'att_src', 'att_dst', 'b_gat', 'ln_gamma', 'ln_beta', 'W1', 'b1', 'W2', 'b2', 'edge_index')}
    del _L1_ffn_all
    return {'x': x, 'src': src, 'dst': dst, 'edge_weight': edge_weight, 'L0_gnn_W1': _L0_gnn_in['W1'], 'L0_gnn_W2': _L0_gnn_in['W2'], 'L0_ffn_gate_w': _L0_ffn_in['gate_w'], 'L0_ffn_gate_b': _L0_ffn_in['gate_b'], 'L0_ffn_w1': _L0_ffn_in['w1'], 'L0_ffn_b1': _L0_ffn_in['b1'], 'L0_ffn_w2': _L0_ffn_in['w2'], 'L0_ffn_b2': _L0_ffn_in['b2'], 'L1_gnn_W1': _L1_gnn_in['W1'], 'L1_gnn_a1_src': _L1_gnn_in['a1_src'], 'L1_gnn_a1_dst': _L1_gnn_in['a1_dst'], 'L1_gnn_b1': _L1_gnn_in['b1'], 'L1_gnn_ln_g': _L1_gnn_in['ln_g'], 'L1_gnn_ln_b': _L1_gnn_in['ln_b'], 'L1_gnn_W2': _L1_gnn_in['W2'], 'L1_gnn_a2_src': _L1_gnn_in['a2_src'], 'L1_gnn_a2_dst': _L1_gnn_in['a2_dst'], 'L1_gnn_b2': _L1_gnn_in['b2'], 'L1_ffn_W_gat': _L1_ffn_in['W_gat'], 'L1_ffn_att_src': _L1_ffn_in['att_src'], 'L1_ffn_att_dst': _L1_ffn_in['att_dst'], 'L1_ffn_b_gat': _L1_ffn_in['b_gat'], 'L1_ffn_ln_gamma': _L1_ffn_in['ln_gamma'], 'L1_ffn_ln_beta': _L1_ffn_in['ln_beta'], 'L1_ffn_W1': _L1_ffn_in['W1'], 'L1_ffn_b1': _L1_ffn_in['b1'], 'L1_ffn_W2': _L1_ffn_in['W2'], 'L1_ffn_b2': _L1_ffn_in['b2'], 'L1_ffn_edge_index': _L1_ffn_in['edge_index']}

def reference(x, src, dst, edge_weight, L0_gnn_W1, L0_gnn_W2, L0_ffn_gate_w, L0_ffn_gate_b, L0_ffn_w1, L0_ffn_b1, L0_ffn_w2, L0_ffn_b2, L1_gnn_W1, L1_gnn_a1_src, L1_gnn_a1_dst, L1_gnn_b1, L1_gnn_ln_g, L1_gnn_ln_b, L1_gnn_W2, L1_gnn_a2_src, L1_gnn_a2_dst, L1_gnn_b2, L1_ffn_W_gat, L1_ffn_att_src, L1_ffn_att_dst, L1_ffn_b_gat, L1_ffn_ln_gamma, L1_ffn_ln_beta, L1_ffn_W1, L1_ffn_b1, L1_ffn_W2, L1_ffn_b2, L1_ffn_edge_index):
    import jax
    import jax.numpy as jnp

    def _L0_gnn_ref(features, edge_weight, W1, W2, edge_src, edge_dst):
        import jax, jax.numpy as jnp
        import numpy as np
        N_NODES = 3125
        N_EDGES = 100000
        D = 256

        def _graph_conv(x, W, edge_src, edge_dst, edge_weight, n_nodes):
            support = x @ W
            msg = support[edge_src] * edge_weight[:, None]
            return jax.ops.segment_sum(msg, edge_dst, num_segments=n_nodes)
        n = features.shape[0]
        h = _graph_conv(features, W1, edge_src, edge_dst, edge_weight, n)
        out = _graph_conv(h, W2, edge_src, edge_dst, edge_weight, n)
        return out

    def _L0_ffn_ref(h, gate_w, gate_b, w1, b1, w2, b2):
        import math
        import jax, jax.numpy as jnp
        import numpy as np
        CAPACITY_FACTOR = 1.25
        B, L, D = h.shape
        E = gate_w.shape[1]
        T = B * L
        C = max(1, math.ceil(CAPACITY_FACTOR * T / E))
        x = h.reshape(T, D)
        logits = x @ gate_w + gate_b
        probs = jax.nn.softmax(logits, axis=-1)
        idx = jnp.argmax(probs, axis=-1)
        prb = jnp.take_along_axis(probs, idx[:, None], axis=1)[:, 0]
        one_hot = jax.nn.one_hot(idx, E, dtype=jnp.float32)
        pos = (jnp.cumsum(one_hot, axis=0) * one_hot).sum(-1).astype(jnp.int32) - 1
        kept = pos < C
        pos_safe = jnp.where(kept, pos, C)
        buf = jnp.zeros((E, C, D), dtype=h.dtype).at[idx, pos_safe].set(x, mode='drop')
        hmid = jax.nn.relu(jnp.einsum('ecd,edf->ecf', buf, w1) + b1[:, None, :])
        ybuf = jnp.einsum('ecf,efd->ecd', hmid, w2) + b2[:, None, :]
        pos_g = jnp.minimum(pos, C - 1)
        y_tok = ybuf[idx, pos_g] * (prb * kept)[:, None]
        y = y_tok.reshape(B, L, D)
        y = jnp.nan_to_num(y, nan=0.0, posinf=10000.0, neginf=-10000.0)
        return y

    def _L1_gnn_ref(x, edge_index, W1, a1_src, a1_dst, b1, ln_g, ln_b, W2, a2_src, a2_dst, b2):
        import jax, jax.numpy as jnp
        import numpy as np
        N = 625
        E = 10000
        D_IN = 256
        HID = 64
        HEADS = 4
        D_OUT = 256
        EPS = 1e-05
        SLOPE = 0.2

        def _gat(x, src, dst, W, a_src, a_dst, b, heads, ch, concat):
            n = x.shape[0]
            h = (x @ W).reshape(n, heads, ch)
            es = (h * a_src).sum(-1)
            ed = (h * a_dst).sum(-1)
            e = jax.nn.leaky_relu(es[src] + ed[dst], SLOPE)
            m = jax.ops.segment_max(e, dst, num_segments=n)
            w = jnp.exp(e - m[dst])
            den = jax.ops.segment_sum(w, dst, num_segments=n)
            alpha = w / den[dst]
            msg = h[src] * alpha[:, :, None]
            out = jax.ops.segment_sum(msg, dst, num_segments=n)
            out = out.reshape(n, heads * ch) if concat else out.mean(axis=1)
            return out + b

        def _layernorm(x, g, b):
            mu = x.mean(-1, keepdims=True)
            v = ((x - mu) ** 2).mean(-1, keepdims=True)
            return (x - mu) * jax.lax.rsqrt(v + EPS) * g + b
        loops = jnp.arange(N, dtype=edge_index.dtype)
        src = jnp.concatenate([edge_index[0], loops])
        dst = jnp.concatenate([edge_index[1], loops])
        h = _gat(x, src, dst, W1, a1_src, a1_dst, b1, HEADS, HID, True)
        h = jax.nn.relu(_layernorm(h, ln_g, ln_b))
        out = _gat(h, src, dst, W2, a2_src, a2_dst, b2, 1, D_OUT, False)
        return out

    def _L1_ffn_ref(x, W_gat, att_src, att_dst, b_gat, ln_gamma, ln_beta, W1, b1, W2, b2, edge_index):
        import jax, jax.numpy as jnp
        import numpy as np
        B, N, D = (16, 128, 256)
        NUM_EXPERTS, TOP_K, HEADS = (4, 2, 4)
        N_EDGES = 32768
        LN_EPS = 1e-05

        def _layernorm(x, g, b):
            mu = x.mean(-1, keepdims=True)
            var = ((x - mu) ** 2).mean(-1, keepdims=True)
            return (x - mu) * jax.lax.rsqrt(var + LN_EPS) * g + b

        def _forward(x, edge_index, W_gat, att_src, att_dst, b_gat, ln_gamma, ln_beta, W1, b1, W2, b2):
            Bc, Nc, Dc = x.shape
            M = Bc * Nc
            x_flat = x.reshape(M, Dc)
            h = (x_flat @ W_gat).reshape(M, HEADS, NUM_EXPERTS)
            loops = jnp.arange(M, dtype=edge_index.dtype)
            src = jnp.concatenate([edge_index[0], loops])
            dst = jnp.concatenate([edge_index[1], loops])
            a_src = (h * att_src).sum(-1)
            a_dst = (h * att_dst).sum(-1)
            e = jax.nn.leaky_relu(a_src[src] + a_dst[dst], negative_slope=0.2)
            e_max = jax.ops.segment_max(e, dst, num_segments=M)
            ee = jnp.exp(e - e_max[dst])
            denom = jax.ops.segment_sum(ee, dst, num_segments=M)
            alpha = ee / (denom[dst] + 1e-16)
            msg = h[src] * alpha[:, :, None]
            agg = jax.ops.segment_sum(msg, dst, num_segments=M).reshape(M, HEADS * NUM_EXPERTS) + b_gat
            scores = _layernorm(agg, ln_gamma, ln_beta).reshape(M, HEADS, NUM_EXPERTS).mean(1)
            scores = scores.reshape(Bc, Nc, NUM_EXPERTS)
            topk_s, topk_i = jax.lax.top_k(scores, TOP_K)
            w = jax.nn.softmax(topk_s, axis=-1)
            out = jnp.zeros_like(x)
            for ei in range(NUM_EXPERTS):
                g = jnp.where(topk_i == ei, w, 0.0).sum(-1)
                hh = jax.nn.gelu(x @ W1[ei] + b1[ei], approximate=False)
                out = out + g[..., None] * (hh @ W2[ei] + b2[ei])
            return out
        return _forward(x, edge_index, W_gat, att_src, att_dst, b_gat, ln_gamma, ln_beta, W1, b1, W2, b2)
    edge_index = jnp.stack([src, dst])
    x = x + _L0_gnn_ref(_layernorm(x, axis=-1), edge_weight, L0_gnn_W1, L0_gnn_W2, src, dst)
    x = x + _L0_ffn_ref(_layernorm(x, axis=-1)[None], L0_ffn_gate_w, L0_ffn_gate_b, L0_ffn_w1, L0_ffn_b1, L0_ffn_w2, L0_ffn_b2)[0]
    x = x + _L1_gnn_ref(_layernorm(x, axis=-1), edge_index, L1_gnn_W1, L1_gnn_a1_src, L1_gnn_a1_dst, L1_gnn_b1, L1_gnn_ln_g, L1_gnn_ln_b, L1_gnn_W2, L1_gnn_a2_src, L1_gnn_a2_dst, L1_gnn_b2)
    x = x + _L1_ffn_ref(_layernorm(x, axis=-1)[None], L1_ffn_W_gat, L1_ffn_att_src, L1_ffn_att_dst, L1_ffn_b_gat, L1_ffn_ln_gamma, L1_ffn_ln_beta, L1_ffn_W1, L1_ffn_b1, L1_ffn_W2, L1_ffn_b2, L1_ffn_edge_index)[0]
    return x

_drawn_inputs = setup_inputs


def setup_inputs(seed=0):
    import zlib

    import numpy as np

    out = dict(_drawn_inputs(seed))
    spreads = {'L0_ffn_gate_b': (0.0, 0.438),
     'L0_ffn_b1': (0.0, 2.0),
     'L0_ffn_b2': (0.0, 2.0),
     'L1_gnn_b1': (0.0, 0.299),
     'L1_gnn_ln_g': (1.0, 0.6),
     'L1_gnn_ln_b': (0.0, 0.766),
     'L1_gnn_b2': (0.0, 0.398),
     'L1_ffn_b_gat': (0.0, 0.275),
     'L1_ffn_ln_gamma': (1.0, 0.594),
     'L1_ffn_ln_beta': (0.0, 0.468),
     'L1_ffn_b1': (0.0, 0.79),
     'L1_ffn_b2': (0.0, 0.594)}
    factors = {'L0_ffn_w1': 2.95,
     'L1_gnn_a1_dst': 74.222,
     'L1_gnn_a2_src': 3.885,
     'L1_gnn_a2_dst': 8.0,
     'L1_ffn_att_src': 8.0,
     'L1_ffn_att_dst': 88.176}
    for name, (base, spread) in spreads.items():
        noise = np.random.default_rng([zlib.crc32(name.encode()), seed]).standard_normal(out[name].shape)
        drawn = base * np.exp(spread * noise) if base else spread * noise
        out[name] = jnp.asarray(drawn.astype(out[name].dtype))
    for name, factor in factors.items():
        out[name] = (out[name] * factor).astype(out[name].dtype)
    return out
```

```python
from contextlib import ExitStack

import concourse.bass as bass
from concourse import mybir

P = 128
D = 256
N = 3125
T = 25
NP_ = T * P
TAIL = N - (T - 1) * P
U = 5
TURNS = T // U

E0 = 50000
B = 7
NBLK = 56
EPAD = NBLK * B * P
ROWE = B * P

E1 = 32768
FB = 8
FNBLK = E1 // (FB * P)

NEXP = 8
CAP = 489
HID = 1024
KEXP = 4
HID2 = 512
GH = 4
EPS = 1e-5
SLOPE = 0.2
LOOPS = 625
NEG = -1.0e30
FMAX = 3.4028234663852886e38

ALU = mybir.AluOpType
ACT = mybir.ActivationFunctionType
F32 = mybir.dt.float32
I32 = mybir.dt.int32
U32 = mybir.dt.uint32
X_ = mybir.AxisListType.X
ds = bass.ds


class Steps:

    def __init__(self, eng, sem, start=0):
        self.eng, self.sem, self.at = eng, sem, start

    def __call__(self, ins):
        ins.then_inc(self.sem, 1)
        self.at = self.at + 1
        self.eng.wait_ge(self.sem, self.at)


class Phase:

    def __init__(self, nc, name):
        self.nc, self.name, self.ctx, self.sems = nc, name, ExitStack(), []

    def __enter__(self):
        return self

    def __exit__(self, *a):
        self.ctx.close()
        self.nc.clear_and_free_semaphores(self.sems)
        self.nc.all_engine_barrier()

    def sb(self, name, shape, dt=F32):
        return self.ctx.enter_context(self.nc.sbuf_tensor(f"{self.name}_{name}", shape, dt))

    def sem(self, name):
        self.sems.append(self.nc.alloc_semaphore(f"{self.name}_{name}"))
        return self.sems[-1]


class Memory:
    pass


def dup(ap, k):
    p, a = ap.shape
    return ap.rearrange("p (a o) -> p a o", o=1).broadcast_to([p, a, k])


def alloc(nc, ctx, m):
    def sb(name, shape, dt=F32):
        return ctx.enter_context(nc.sbuf_tensor(name, shape, dt))

    m.X = sb("X", [P, T, D])
    m.ACC = sb("ACC", [P, T, D + GH])
    m.XN = sb("XN", [P, T, D])
    m.iota = sb("iota", [P, NP_])
    m.pcol = sb("pcol", [P, 1])
    m.ident = sb("ident", [P, P])
    m.upper = sb("upper", [P, P])
    m.ones = sb("ones", [P, P])
    m.pen = sb("pen", [P, 1])
    m.own = sb("own", [P, 1])
    m.src = sb("src_t", [P, B, NBLK], U32)
    m.dsti = sb("dsti_t", [P, B, NBLK], U32)
    m.dstf = sb("dstf_t", [P, B, NBLK])
    m.wgt = sb("wgt_t", [P, B, NBLK])
    m.pack = sb("pack", [1, NBLK], I32)
    m.fsrc = sb("fsrc", [P, FB, FNBLK], U32)
    m.fdst = sb("fdst", [P, FB, FNBLK], U32)
    m.flo = sb("flo", [P, FB, FNBLK])
    m.fhi = sb("fhi", [P, FB, FNBLK])
    m.mean = sb("mean", [P, T])
    m.rstd = sb("rstd", [P, T])
    m.XT = m.XN[:].rearrange("p t d -> p (t d)").rearrange("p (k n) -> p k n", k=2)
    m.vec = sb("vec", [P, 2, D])
    m.gscale = sb("gscale", [P, T])
    m.gidx = sb("gidx", [P, T], U32)
    m.gate = sb("gate", [P, T, KEXP])
    m.EDU = sb("EDU", [P, T, 2 * GH])
    m.W = {k: sb(f"W_{k}", [P, 2, n]) for k, n in
           (("c1", D), ("c2", D), ("g1", D + 8), ("g2", D + 2), ("gate", 8), ("gat", 24))}
    m.ps = ctx.enter_context(nc.psum_tensor("ps", [P, 8, 512], F32))


def prepare(nc, m, A):
    with Phase(nc, "prep") as f:
        raw = f.sb("raw", [NBLK, 2, ROWE], I32)
        rawf = f.sb("rawf", [NBLK, 3, ROWE])
        fraw = f.sb("fraw", [FNBLK, 2, FB * P], I32)
        frawf = f.sb("frawf", [FNBLK, 4, FB * P])
        bi = f.sb("bi", [NBLK, 2], I32)
        bf = f.sb("bf", [NBLK, 2])
        row = f.sb("row", [1, 4, NBLK])
        one = f.sb("one", [1, NBLK])
        att = f.sb("att", [P, 4 * D + 32])
        prod = f.sb("prod", [P, 4 * D + 32])
        s_in = f.sem("in")
        s_fill = f.sem("fill")
        s_edge = f.sem("edge")
        s_iota = f.sem("iota")
        s_v = f.sem("v")
        s_tr = f.sem("tr")
        s_cp = f.sem("cp")
        s_row = f.sem("row")
        s_zero = f.sem("zero")
        full = E0 // ROWE
        rest = E0 - full * ROWE
        zrow = 15 * P
        with nc.Block() as block:

            @block.sync
            def _(sp):
                sp.dma_start(m.W["c1"][:], A["L0_gnn_W1"].rearrange("(k p) n -> p k n", p=P)).then_inc(s_in, 16)
                sp.dma_start(m.W["c2"][:], A["L0_gnn_W2"].rearrange("(k p) n -> p k n", p=P)).then_inc(s_in, 16)
                sp.dma_start(m.W["g1"][:, :, 0:D], A["L1_gnn_W1"].rearrange("(k p) n -> p k n", p=P)).then_inc(s_in, 16)
                sp.dma_start(m.W["g2"][:, :, 0:D], A["L1_gnn_W2"].rearrange("(k p) n -> p k n", p=P)).then_inc(s_in, 16)
                sp.dma_start(m.W["gate"][:], A["L0_ffn_gate_w"].rearrange("(k p) n -> p k n", p=P)).then_inc(s_in, 16)
                sp.dma_start(m.W["gat"][:, :, 0:16], A["L1_ffn_W_gat"].rearrange("(k p) n -> p k n", p=P)).then_inc(s_in, 16)
                for k, name in enumerate(("L1_gnn_a1_src", "L1_gnn_a1_dst", "L1_gnn_a2_src", "L1_gnn_a2_dst")):
                    sp.dma_start(att[:, k * D:(k + 1) * D],
                                 A[name].rearrange("a b -> (a b)").partition_broadcast(P)).then_inc(s_in, 16)
                for k, name in enumerate(("L1_ffn_att_src", "L1_ffn_att_dst")):
                    sp.dma_start(att[:, 4 * D + 16 * k:4 * D + 16 * k + 16],
                                 A[name].rearrange("a b -> (a b)").partition_broadcast(P)).then_inc(s_in, 16)
                sp.wait_ge(s_fill, 3)
                for k, name in enumerate(("src", "dst")):
                    sp.dma_start(raw[0:full, k, :], A[name][0:full * ROWE].rearrange("(b e) -> b e", e=ROWE)).then_inc(s_edge, 16)
                    sp.dma_start(raw[full:full + 1, k, 0:rest], A[name][full * ROWE:E0].rearrange("(b e) -> b e", b=1)).then_inc(s_edge, 16)
                sp.dma_start(rawf[0:full, 2, :], A["edge_weight"][0:full * ROWE].rearrange("(b e) -> b e", e=ROWE)).then_inc(s_edge, 16)
                sp.dma_start(rawf[full:full + 1, 2, 0:rest], A["edge_weight"][full * ROWE:E0].rearrange("(b e) -> b e", b=1)).then_inc(s_edge, 16)
                for k in range(2):
                    sp.dma_start(fraw[:, k, :], A["L1_ffn_edge_index"][k].rearrange("(b e) -> b e", e=FB * P)).then_inc(s_edge, 16)
                sp.wait_ge(s_in, 12 * 16)
                sp.wait_ge(s_edge, 8 * 16)

            @block.scalar
            def _(act):
                act.wait_ge(s_fill, 4)
                act.dma_start(m.X[:, 0:T - 1, :], A["x"][0:(T - 1) * P, :].rearrange("(t p) d -> p t d", p=P)).then_inc(s_zero, 16)
                act.dma_start(m.X[0:TAIL, T - 1, :], A["x"][(T - 1) * P:N, :]).then_inc(s_zero, 16)
                act.wait_ge(s_fill, 5)
                zero = m.XN[:, 0:15, :]
                for k in range(2):
                    act.dma_start(m.slots[k * zrow:(k + 1) * zrow, :].rearrange("(p a) d -> p a d", p=P), zero).then_inc(s_zero, 16)
                act.dma_start(m.slots[2 * zrow:2 * zrow + P, :], m.XN[:, 0, :]).then_inc(s_zero, 16)
                act.wait_ge(s_zero, 5 * 16)

            @block.gpsimd
            def _(pool):
                pool.iota(m.iota[:], [[1, NP_]], base=0, channel_multiplier=0,
                          allow_small_or_imprecise_dtypes=True).then_inc(s_iota, 1)
                pool.iota(m.pcol[:], [[0, 1]], base=0, channel_multiplier=1,
                          allow_small_or_imprecise_dtypes=True).then_inc(s_iota, 1)

            @block.vector
            def _(v):
                v.memset(raw[:, 0, :], 0).then_inc(s_fill, 1)
                v.memset(raw[:, 1, :], NP_ - 1).then_inc(s_fill, 1)
                v.memset(rawf[:, 2, :], 0.0).then_inc(s_fill, 1)
                v.memset(m.X[:, T - 1, :], 0.0).then_inc(s_fill, 1)
                v.memset(m.XN[:], 0.0).then_inc(s_fill, 1)
                step = Steps(v, s_v)
                v.memset(one[:], 1.0).then_inc(s_fill, 1)
                v.memset(m.ones[:], 1.0).then_inc(s_fill, 1)
                v.wait_ge(s_iota, 2)
                step(v.tensor_scalar(m.ident[:], m.iota[:, 0:P], m.pcol[:, 0:1], None, ALU.is_equal))
                step(v.tensor_scalar(m.upper[:], m.iota[:, 0:P], m.pcol[:, 0:1], None, ALU.is_ge))
                step(v.tensor_scalar(m.pen[:], m.pcol[:], float(TAIL), NEG, ALU.is_ge, ALU.mult))
                step(v.tensor_scalar(m.own[:], m.pcol[:], float(LOOPS % P), NEG, ALU.is_ge, ALU.mult))
                v.wait_ge(s_in, 12 * 16)
                for k in range(2):
                    for name, heads, base in (("g1", 4, 0), ("g2", 1, 2 * D)):
                        w = m.W[name]
                        for a in range(2):
                            step(v.tensor_tensor(prod[:, 0:D], w[:, k, 0:D], att[:, base + a * D:base + (a + 1) * D], ALU.mult))
                            step(v.tensor_reduce(w[:, k, D + a * heads:D + (a + 1) * heads],
                                                 prod[:, 0:D].rearrange("p (h c) -> p h c", h=heads), X_, ALU.add))
                    for a in range(2):
                        w = m.W["gat"]
                        step(v.tensor_tensor(prod[:, 0:16], w[:, k, 0:16], att[:, 4 * D + 16 * a:4 * D + 16 * a + 16], ALU.mult))
                        step(v.tensor_reduce(w[:, k, 16 + 4 * a:20 + 4 * a],
                                             prod[:, 0:16].rearrange("p (h c) -> p h c", h=4), X_, ALU.add))
                v.wait_ge(s_edge, 8 * 16)
                step(v.tensor_copy(rawf[:, 0:2, :], raw[:]))
                step(v.tensor_reduce(bf[:, 0:1], rawf[:, 1, :], X_, ALU.min))
                step(v.tensor_reduce(bf[:, 1:2], rawf[:, 1, :], X_, ALU.max))
                step(v.tensor_copy(bi[:], bf[:]))
                step(v.tensor_scalar(bi[:], bi[:], 7, None, ALU.logical_shift_right))
                step(v.tensor_copy(bf[:], bi[:]))
                step(v.tensor_copy(frawf[:, 0:2, :], fraw[:]))
                step(v.tensor_scalar(fraw[:, 0, :], fraw[:, 1, :], 7, None, ALU.logical_shift_right))
                step(v.tensor_scalar(fraw[:, 1, :], fraw[:, 1, :], P - 1, None, ALU.bitwise_and))
                step(v.tensor_copy(frawf[:, 2:4, :], fraw[:]))
                v.sem_inc(s_row, 1)
                n = 0
                for k, out in ((0, m.src), (1, m.dsti), (1, m.dstf), (2, m.wgt)):
                    n += 1
                    v.wait_ge(s_tr, n)
                    v.tensor_copy(out[:], m.ps[:, 0, 0:B * NBLK].rearrange("p (j b) -> p j b", j=B)).then_inc(s_cp, 1)
                for k, out in enumerate((m.fsrc, m.fdst, m.fhi, m.flo)):
                    n += 1
                    v.wait_ge(s_tr, n)
                    v.tensor_copy(out[:], m.ps[:, 0, 0:FB * FNBLK].rearrange("p (j b) -> p j b", j=FB)).then_inc(s_cp, 1)
                v.wait_ge(s_tr, 9)
                step(v.tensor_copy(row[:, 0:2, :], m.ps[0:1, 0, 0:2 * NBLK].rearrange("p (a b) -> p a b", a=2)))
                step(v.tensor_tensor(row[:, 2, :], row[:, 1, :], row[:, 0, :], ALU.subtract))
                step(v.tensor_scalar(row[:, 2, :], row[:, 2, :], 1.0, None, ALU.add))
                step(v.tensor_tensor_scan(row[:, 3, :], one[:], row[:, 2, :], 0.0, ALU.mult, ALU.add))
                step(v.tensor_tensor(row[:, 3, :], row[:, 3, :], row[:, 2, :], ALU.subtract))
                step(v.scalar_tensor_tensor(out=row[:, 1, :], in0=row[:, 2, :], scalar=32.0, in1=row[:, 0, :], op0=ALU.mult, op1=ALU.add))
                step(v.scalar_tensor_tensor(out=row[:, 2, :], in0=row[:, 3, :], scalar=1024.0, in1=row[:, 1, :], op0=ALU.mult, op1=ALU.add))
                step(v.tensor_copy(m.pack[:], row[:, 2, :]))

            @block.tensor
            def _(pe):
                pe.wait_ge(s_row, 1)
                n = 0
                for k in (0, 1, 1, 2):
                    if n:
                        pe.wait_ge(s_cp, n)
                    for j in range(B):
                        last = pe.transpose(m.ps[:, 0, j * NBLK:(j + 1) * NBLK], rawf[:, k, j * P:(j + 1) * P],
                                            m.ident[0:NBLK, 0:NBLK])
                    last.then_inc(s_tr, 1)
                    n += 1
                for k in range(4):
                    pe.wait_ge(s_cp, n)
                    for j in range(FB):
                        last = pe.transpose(m.ps[:, 0, j * FNBLK:(j + 1) * FNBLK], frawf[:, k, j * P:(j + 1) * P],
                                            m.ident[0:FNBLK, 0:FNBLK])
                    last.then_inc(s_tr, 1)
                    n += 1
                pe.wait_ge(s_cp, n)
                for k in range(2):
                    last = pe.transpose(m.ps[0:1, 0, k * NBLK:(k + 1) * NBLK], bf[:, k:k + 1], m.ident[0:NBLK, 0:NBLK])
                last.then_inc(s_tr, 1)


def row_moments(nc, m, name, src):
    with Phase(nc, name) as f:
        st = f.sb("st", [P, U, 6])
        mv = f.sb("mv", [P, U, 2])
        s_st = f.sem("st")
        s_mv = f.sem("mv")
        s_cp = f.sem("cp")
        s_v = f.sem("v")
        s_sq = f.sem("sq")
        s_turn = f.sem("turn")
        with nc.Block() as block:

            @block.vector
            def _(v):
                with v.Fori(0, TURNS) as i:
                    for j in range(U):
                        v.bn_stats(st[:, j, :], src[:, ds(U * i + j, 1), :]).then_inc(s_st, 1)
                    v.wait_ge(s_cp, 2 * i)
                    for j in range(U):
                        v.wait_ge(s_st, U * i + j + 1)
                        v.sem_inc(s_turn, 1)
                        v.bn_aggr(mv[:, j, :], st[:, j, :]).then_inc(s_mv, 1)
                    v.wait_ge(s_mv, U * i + U)
                    v.tensor_copy(m.mean[:, ds(U * i, U)], mv[:, :, 0]).then_inc(s_cp, 1)
                    v.tensor_scalar(m.rstd[:, ds(U * i, U)], mv[:, :, 1], EPS, None, ALU.add).then_inc(s_cp, 1)
                v.wait_ge(s_sq, 1)
                v.reciprocal(m.rstd[:], m.rstd[:]).then_inc(s_v, 1)

            @block.scalar
            def _(act):
                act.wait_ge(s_cp, 2 * TURNS)
                act.activation(m.rstd[:], m.rstd[:], ACT.Sqrt).then_inc(s_sq, 1)


def project(nc, m, name, kind, w, cols, heads=0, table=None, vecs=None):
    full = cols + heads
    with Phase(nc, name) as f:
        xs = f.sb("xs", [P, U, D])
        xt = f.sb("xt", [P, U, 2, P])
        s_xs = f.sem("xs")
        s_tr = f.sem("tr")
        s_xt = f.sem("xt")
        s_mm = f.sem("mm")
        s_out = f.sem("out")
        s_keep = f.sem("keep")
        s_dma = f.sem("dma")
        s_v = f.sem("v")
        keep_x = name == "route"
        keep_xt = name == "gatep"

        def p_turn(j):
            return m.ps[:, j, 0:2 * P]

        with nc.Block() as block:

            @block.sync
            def _(sp):
                if table is not None:
                    with sp.Fori(0, TURNS) as i:
                        sp.wait_ge(s_out, U * i + 2 * U)
                        sp.sem_inc(s_keep, 1)
                        sp.dma_start(table.rearrange("(t p) c -> p t c", p=P)[:, ds(U * i, U), :],
                                     m.ACC[:, ds(U * i, U), 0:cols]).then_inc(s_dma, 16)
                    sp.wait_ge(s_dma, 16 * TURNS)

            @block.vector
            def _(v):
                step = Steps(v, s_v)
                with v.Fori(0, TURNS) as i:
                    for j in range(U):
                        t = U * i + j
                        v.wait_ge(s_tr, t + 1)
                        if keep_x:
                            v.wait_ge(s_keep, t + 1)
                        if kind == "acc":
                            v.tensor_copy(xs[:, j, :], m.ACC[:, ds(t, 1), 0:D]).then_inc(s_xs, 1)
                            continue
                        src = m.X[:, ds(t, 1), :] if kind == "ln" else m.ACC[:, ds(t, 1), 0:D]
                        ins = v.tensor_scalar(xs[:, j, :], src, m.mean[:, ds(t, 1)], m.rstd[:, ds(t, 1)],
                                              ALU.subtract, ALU.mult)
                        if kind == "relu":
                            base = 3 * t
                            ins.then_inc(s_v, 1)
                            v.wait_ge(s_v, base + 1)
                            v.tensor_tensor(xs[:, j, :], xs[:, j, :], vecs[0], ALU.mult).then_inc(s_v, 1)
                            v.wait_ge(s_v, base + 2)
                            v.tensor_tensor(xs[:, j, :], xs[:, j, :], vecs[1], ALU.add).then_inc(s_v, 1)
                            v.wait_ge(s_v, base + 3)
                            ins = v.tensor_scalar(xs[:, j, :], xs[:, j, :], 0.0, None, ALU.max)
                        ins.then_inc(s_xs, 1)

            @block.scalar
            def _(act):
                act.sem_inc(s_xt, U)
                act.sem_inc(s_out, U)
                if keep_x:
                    act.sem_inc(s_keep, U)
                with act.Fori(0, TURNS) as i:
                    for j in range(U):
                        t = U * i + j
                        if keep_x:
                            act.wait_ge(s_xs, t + 1)
                            act.copy(m.XN[:, ds(t, 1), :], xs[:, j, :]).then_inc(s_keep, 1)
                        act.wait_ge(s_tr, U + t + 1)
                        act.wait_ge(s_mm, t + 1)
                        pt = p_turn(j).rearrange("p (k n) -> p k n", k=2)
                        if keep_xt:
                            act.copy(m.XT[:, :, ds(P * t, P)], pt)
                        act.copy(xt[:, j, :, :], pt).then_inc(s_xt, 1)
                    for j in range(U):
                        t = U * i + j
                        act.wait_ge(s_mm, U + t + 1)
                        if heads:
                            act.copy(m.EDU[:, ds(t, 1), 0:heads], m.ps[:, j, cols:full])
                        act.copy(m.ACC[:, ds(t, 1), 0:cols], m.ps[:, j, 0:cols]).then_inc(s_out, 1)

            @block.tensor
            def _(pe):
                pe.sem_inc(s_tr, U)
                pe.sem_inc(s_mm, U)
                with pe.Fori(0, TURNS) as i:
                    for j in range(U):
                        t = U * i + j
                        pe.wait_ge(s_xs, t + 1)
                        pe.wait_ge(s_out, t + 1)
                        for k in range(2):
                            ins = pe.transpose(p_turn(j)[:, k * P:(k + 1) * P], xs[:, j, k * P:(k + 1) * P], m.ident[:])
                        ins.then_inc(s_tr, 1)
                    for j in range(U):
                        t = U * i + j
                        pe.wait_ge(s_xt, U + t + 1)
                        for k in range(2):
                            ins = pe.matmul(m.ps[:, j, 0:full], xt[:, j, k, :], w[:, k, 0:full],
                                            start=(k == 0), stop=(k == 1))
                        ins.then_inc(s_mm, 1)


def visits(nc, eng, m, b):
    packed = eng.value_load(m.pack[0:1, ds(b, 1)], min_val=0, max_val=(1 << 22) - 1)
    first = eng.snap(packed % 32)
    count = eng.snap(packed // 32 % 32)
    before = eng.snap(packed // 1024)

    def tile(q):
        return nc.s_assert_within(q - before + first, 0, T - 1,
                                  skip_runtime_bounds_check_because="tiles of nodes below 3200")

    return before, eng.snap(before + count), tile


def convolve(nc, m, name, table):
    with Phase(nc, name) as f:
        G = f.sb("G", [P, 2, B, D])
        ix = f.sb("ix", [P, 2, B], U32)
        dd = f.sb("dd", [P, 2, B])
        ww = f.sb("ww", [P, 2, B])
        S = f.sb("S", [P, B, P])
        s_zero = f.sem("zero")
        s_stage = f.sem("stage")
        s_rows = [f.sem(f"rows{q}") for q in range(2)]
        s_S = f.sem("S")
        s_mm = f.sem("mm")
        s_add = f.sem("add")
        s_blk = f.sem("blk")
        s_turn = f.sem("turn")
        with nc.Block() as block:

            @block.scalar
            def _(act):
                with act.Fori(0, NBLK // 2) as i:
                    for q in range(2):
                        b = 2 * i + q
                        act.wait_ge(s_blk, b + 1)
                        act.copy(ix[:, q, :], m.src[:, :, ds(b, 1)]).then_inc(s_stage, 1)
                        act.copy(dd[:, q, :], m.dstf[:, :, ds(b, 1)]).then_inc(s_stage, 1)
                        act.copy(ww[:, q, :], m.wgt[:, :, ds(b, 1)]).then_inc(s_stage, 1)

            @block.gpsimd
            def _(pool):
                with pool.Fori(0, NBLK // 2) as i:
                    for q in range(2):
                        pool.wait_ge(s_stage, 3 * (2 * i + q) + 3)
                        pool.sem_inc(s_turn, 1)
                        for j in range(B):
                            pool.indirect_dma_start(
                                out=G[:, q, j, :], out_offset=None, in_=table[:, :],
                                in_offset=bass.IndirectOffsetOnAxis(ap=ix[:, q, j:j + 1], axis=0),
                            ).then_inc(s_rows[q], 16)

            @block.vector
            def _(v):
                v.sem_inc(s_add, 1)
                v.memset(m.ACC[:], 0.0).then_inc(s_zero, 1)
                v.wait_ge(s_zero, 1)
                with v.Fori(0, NBLK // 2) as i:
                    for q in range(2):
                        b = 2 * i + q
                        begin, end, tile = visits(nc, v, m, b)
                        v.wait_ge(s_stage, 3 * b + 3)
                        with v.Fori(begin, end) as n:
                            t = tile(n)
                            for j in range(B):
                                v.wait_ge(s_mm, B * n + j + 1)
                                v.tensor_scalar(S[:, j, :], m.iota[:, ds(P * t, P)], dd[:, q, j:j + 1],
                                                ww[:, q, j:j + 1], ALU.is_equal, ALU.mult).then_inc(s_S, 1)
                            v.wait_ge(s_mm, B * n + 2 * B)
                            v.wait_ge(s_add, n + 1)
                            v.tensor_tensor(m.ACC[:, ds(t, 1), 0:D], m.ACC[:, ds(t, 1), 0:D],
                                            m.ps[:, 0:1, 0:D], ALU.add).then_inc(s_add, 1)

            @block.tensor
            def _(pe):
                pe.sem_inc(s_blk, 2)
                pe.sem_inc(s_mm, B)
                with pe.Fori(0, NBLK // 2) as i:
                    for q in range(2):
                        begin, end, tile = visits(nc, pe, m, 2 * i + q)
                        pe.wait_ge(s_rows[q], 16 * B * (i + 1))
                        with pe.Fori(begin, end) as n:
                            pe.wait_ge(s_add, n + 1)
                            for j in range(B):
                                pe.wait_ge(s_S, B * n + j + 1)
                                pe.matmul(m.ps[:, 0, 0:D], S[:, j, :], G[:, q, j, :],
                                          start=(j == 0), stop=(j == B - 1)).then_inc(s_mm, 1)
                        pe.drain().then_inc(s_blk, 1)


def self_loops(nc, m, name, hc, H, edu_table, loops):
    with Phase(nc, name) as f:
        es = f.sb("es", [P, T, H])
        top = f.sb("top", [P, H])
        tops = f.sb("tops", [P, H])
        sc = f.sb("sc", [P, T, H])
        s_v = f.sem("v")
        s_top = f.sem("top")
        s_tops = f.sem("tops")
        s_edu = f.sem("edu")
        s_sc = f.sem("sc")
        s_w = f.sem("w")
        s_dma = f.sem("dma")
        ed = m.EDU[:, :, 0:H]
        bound = m.EDU[:, :, H:2 * H]
        with nc.Block() as block:

            @block.vector
            def _(v):
                step = Steps(v, s_v)
                step(v.tensor_copy(es[:], m.ACC[:, :, hc:hc + H]))
                step(v.tensor_scalar(es[:, T - 1, :], es[:, T - 1, :], m.pen[:, 0:1], None, ALU.add))
                v.tensor_reduce(top[:], es[:].rearrange("p t h -> p h t"), X_, ALU.max).then_inc(s_top, 1)
                v.wait_ge(s_tops, 1)
                big = tops[:].rearrange("p (o h) -> p o h", o=1).broadcast_to([P, T, H])
                step(v.tensor_tensor(bound, ed, big, ALU.add))
                step(v.scalar_tensor_tensor(out=bound, in0=bound, scalar=SLOPE, in1=bound, op0=ALU.mult, op1=ALU.max))
                v.sem_inc(s_edu, 1)
                step(v.tensor_tensor(sc[:], m.ACC[:, :, hc:hc + H], ed, ALU.add))
                step(v.scalar_tensor_tensor(out=sc[:], in0=sc[:], scalar=SLOPE, in1=sc[:], op0=ALU.mult, op1=ALU.max))
                step(v.tensor_tensor(sc[:], sc[:], bound, ALU.subtract))
                step(v.tensor_scalar(sc[:], sc[:], 0.0, None, ALU.min))
                if loops < N:
                    at = loops // P
                    step(v.tensor_scalar(sc[:, at, :], sc[:, at, :], m.own[:, 0:1], None, ALU.add))
                    step(v.memset(sc[:, at + 1:T, :], NEG))
                v.sem_inc(s_sc, 1)
                v.wait_ge(s_w, 1)
                w4 = m.ACC[:, :, hc:hc + H].rearrange("p t (h o) -> p t h o", o=1).broadcast_to([P, T, H, hc // H])
                h4 = m.ACC[:, :, 0:hc].rearrange("p t (h c) -> p t h c", h=H)
                step(v.tensor_tensor(h4, h4, w4, ALU.mult))

            @block.gpsimd
            def _(pool):
                pool.wait_ge(s_top, 1)
                pool.partition_all_reduce(tops[:], top[:], P, bass.bass_isa.ReduceOp.max).then_inc(s_tops, 1)

            @block.scalar
            def _(act):
                act.wait_ge(s_sc, 1)
                act.activation(m.ACC[:, :, hc:hc + H], sc[:], ACT.Exp).then_inc(s_w, 1)

            @block.sync
            def _(sp):
                sp.wait_ge(s_edu, 1)
                sp.dma_start(edu_table.rearrange("(t p) c -> p t c", p=P), m.EDU[:, :, 0:2 * H]).then_inc(s_dma, 16)
                sp.wait_ge(s_dma, 16)


def edge_weights(v, act_sem, exp_sem, step, z, g_es, d_ed, d_bound):
    step(v.tensor_tensor(z, g_es, d_ed, ALU.add))
    step(v.scalar_tensor_tensor(out=z, in0=z, scalar=SLOPE, in1=z, op0=ALU.mult, op1=ALU.max))
    v.tensor_tensor(z, z, d_bound, ALU.subtract).then_inc(act_sem, 1)


def attend(nc, m, name, H, table, edu_table):
    W = D + H
    with Phase(nc, name) as f:
        G = f.sb("G", [P, 2, B, W])
        DD = f.sb("DD", [P, 2, B, 2 * H])
        z = f.sb("z", [P, B, H])
        ixs = f.sb("ixs", [P, 2, B], U32)
        ixd = f.sb("ixd", [P, 2, B], U32)
        dd = f.sb("dd", [P, 2, B])
        S = f.sb("S", [P, B, P])
        s_stage = f.sem("stage")
        s_rows = [f.sem(f"rows{q}") for q in range(2)]
        s_z = f.sem("z")
        s_w = f.sem("w")
        s_S = f.sem("S")
        s_msg = f.sem("msg")
        s_mm = f.sem("mm")
        s_add = f.sem("add")
        s_blk = f.sem("blk")
        s_turn = f.sem("turn")
        s_v = f.sem("v")
        with nc.Block() as block:

            @block.scalar
            def _(act):
                def stage(b, q):
                    act.wait_ge(s_blk, b + 1)
                    act.copy(ixs[:, q, :], m.src[:, :, ds(b, 1)]).then_inc(s_stage, 1)
                    act.copy(ixd[:, q, :], m.dsti[:, :, ds(b, 1)]).then_inc(s_stage, 1)
                    act.copy(dd[:, q, :], m.dstf[:, :, ds(b, 1)]).then_inc(s_stage, 1)

                def weights(b, q):
                    act.wait_ge(s_z, b + 1)
                    act.activation(G[:, q, :, D:W], z[:], ACT.Exp).then_inc(s_w, 1)

                stage(0, 0)
                stage(1, 1)
                with act.Fori(0, NBLK // 2 - 1) as i:
                    for q in range(2):
                        weights(2 * i + q, q)
                        stage(2 * i + q + 2, q)
                for q in range(2):
                    weights(NBLK - 2 + q, q)

            @block.gpsimd
            def _(pool):
                with pool.Fori(0, NBLK // 2) as i:
                    for q in range(2):
                        pool.wait_ge(s_stage, 3 * (2 * i + q) + 3)
                        pool.sem_inc(s_turn, 1)
                        for j in range(B):
                            pool.indirect_dma_start(
                                out=G[:, q, j, :], out_offset=None, in_=table[:, :],
                                in_offset=bass.IndirectOffsetOnAxis(ap=ixs[:, q, j:j + 1], axis=0),
                            ).then_inc(s_rows[q], 16)
                            pool.indirect_dma_start(
                                out=DD[:, q, j, :], out_offset=None, in_=edu_table[:, :],
                                in_offset=bass.IndirectOffsetOnAxis(ap=ixd[:, q, j:j + 1], axis=0),
                            ).then_inc(s_rows[q], 16)

            @block.vector
            def _(v):
                v.sem_inc(s_add, 1)
                with v.Fori(0, NBLK // 2) as i:
                    for q in range(2):
                        b = 2 * i + q
                        begin, end, tile = visits(nc, v, m, b)
                        v.wait_ge(s_rows[q], 32 * B * (i + 1))
                        edge_weights(v, s_z, s_w, Steps(v, s_v, 2 * b), z[:], G[:, q, :, D:W],
                                     DD[:, q, :, 0:H], DD[:, q, :, H:2 * H])
                        v.wait_ge(s_w, b + 1)
                        g4 = G[:, q, :, 0:D].rearrange("p j (h c) -> p j h c", h=H)
                        w4 = G[:, q, :, D:W].rearrange("p j (h o) -> p j h o", o=1).broadcast_to([P, B, H, D // H])
                        v.tensor_tensor(g4, g4, w4, ALU.mult).then_inc(s_msg, 1)
                        v.wait_ge(s_stage, 3 * b + 3)
                        with v.Fori(begin, end) as n:
                            t = tile(n)
                            v.wait_ge(s_mm, B * n + B)
                            io = m.iota[:, ds(P * t, P)].rearrange("p (o c) -> p o c", o=1).broadcast_to([P, B, P])
                            v.tensor_tensor(S[:], io, dup(dd[:, q, :], P), ALU.is_equal).then_inc(s_S, 1)
                            v.wait_ge(s_mm, B * n + 2 * B)
                            v.wait_ge(s_add, n + 1)
                            v.tensor_tensor(m.ACC[:, ds(t, 1), 0:W], m.ACC[:, ds(t, 1), 0:W],
                                            m.ps[:, 0:1, 0:W], ALU.add).then_inc(s_add, 1)

            @block.tensor
            def _(pe):
                pe.sem_inc(s_blk, 2)
                pe.sem_inc(s_mm, B)
                with pe.Fori(0, NBLK // 2) as i:
                    for q in range(2):
                        b = 2 * i + q
                        begin, end, tile = visits(nc, pe, m, b)
                        pe.wait_ge(s_msg, b + 1)
                        with pe.Fori(begin, end) as n:
                            pe.wait_ge(s_add, n + 1)
                            pe.wait_ge(s_S, n + 1)
                            for j in range(B):
                                pe.matmul(m.ps[:, 0, 0:W], S[:, j, :], G[:, q, j, :],
                                          start=(j == 0), stop=(j == B - 1)).then_inc(s_mm, 1)
                        pe.drain().then_inc(s_blk, 1)


def finish_attention(nc, m, name, H, bias_ap, to_x):
    with Phase(nc, name) as f:
        bias = f.sb("bias", [P, D])
        none = f.sb("none", [P, T, H])
        s_dma = f.sem("dma")
        s_v = f.sem("v")
        with nc.Block() as block:

            @block.sync
            def _(sp):
                sp.dma_start(bias[:], bias_ap.partition_broadcast(P)).then_inc(s_dma, 16)
                sp.wait_ge(s_dma, 16)

            @block.vector
            def _(v):
                step = Steps(v, s_v)
                den = m.ACC[:, :, D:D + H]
                a = m.ACC[:, :, 0:D]
                step(v.tensor_scalar(none[:], den, 0.0, None, ALU.is_equal))
                step(v.tensor_tensor(den, den, none[:], ALU.add))
                step(v.reciprocal(den, den))
                a4 = a.rearrange("p t (h c) -> p t h c", h=H)
                r4 = den.rearrange("p t (h o) -> p t h o", o=1).broadcast_to([P, T, H, D // H])
                step(v.tensor_tensor(a4, a4, r4, ALU.mult))
                v.wait_ge(s_dma, 16)
                step(v.tensor_tensor(a, a, bias[:].rearrange("p (o d) -> p o d", o=1).broadcast_to([P, T, D]), ALU.add))
                if to_x:
                    step(v.tensor_tensor(m.X[:], m.X[:], a, ALU.add))


def route(nc, m, A):
    with Phase(nc, "rt") as f:
        bias = f.sb("bias", [P, NEXP])
        L = f.sb("L", [P, T, NEXP])
        OH = f.sb("OH", [P, T, NEXP])
        tmp = f.sb("tmp", [P, T, NEXP])
        tot = f.sb("tot", [P, T, NEXP])
        top = f.sb("top", [P, T])
        node = f.sb("node", [P, T])
        pos = f.sb("pos", [P, T])
        ex = f.sb("ex", [P, T])
        kept = f.sb("kept", [P, T])
        a = f.sb("a", [P, T])
        idx = f.sb("idx", [P, T], U32)
        s_dma = f.sem("dma")
        s_v = f.sem("v")
        s_io = f.sem("io")
        s_l = f.sem("l")
        s_e = f.sem("e")
        s_oh = f.sem("oh")
        s_mm = f.sem("mm")
        s_idx = f.sem("idx")
        s_put = f.sem("put")
        with nc.Block() as block:

            @block.sync
            def _(sp):
                sp.dma_start(bias[:], A["L0_ffn_gate_b"].partition_broadcast(P)).then_inc(s_dma, 16)

            @block.gpsimd
            def _(pool):
                pool.iota(node[:], [[P, T]], base=NEXP * CAP, channel_multiplier=1,
                          allow_small_or_imprecise_dtypes=True).then_inc(s_io, 1)
                pool.wait_ge(s_idx, 1)
                for t in range(T):
                    pool.indirect_dma_start(
                        out=m.slots[:, :], out_offset=bass.IndirectOffsetOnAxis(ap=idx[:, t:t + 1], axis=0),
                        in_=m.XN[:, t, :], in_offset=None).then_inc(s_put, 16)
                pool.wait_ge(s_put, 16 * T)

            @block.scalar
            def _(act):
                act.wait_ge(s_l, 1)
                act.activation(tmp[:], L[:], ACT.Exp).then_inc(s_e, 1)

            @block.tensor
            def _(pe):
                pe.wait_ge(s_oh, 1)
                oh = OH[:].rearrange("p t e -> p (t e)")
                pe.matmul(m.ps[:, 0, 0:T * NEXP], m.upper[:], oh, start=True, stop=True).then_inc(s_mm, 1)
                pe.matmul(m.ps[:, 1, 0:T * NEXP], m.ones[:], oh, start=True, stop=True).then_inc(s_mm, 1)

            @block.vector
            def _(v):
                step = Steps(v, s_v)
                v.wait_ge(s_dma, 16)
                eb = [P, T, NEXP]
                step(v.tensor_tensor(L[:], m.ACC[:, :, 0:NEXP],
                                     bias[:].rearrange("p (o e) -> p o e", o=1).broadcast_to(eb), ALU.add))
                step(v.tensor_reduce(top[:], L[:], X_, ALU.max))
                step(v.tensor_tensor(OH[:], L[:], dup(top[:], NEXP), ALU.is_equal))
                io8 = m.iota[:, 0:NEXP].rearrange("p (o e) -> p o e", o=1).broadcast_to(eb)
                step(v.scalar_tensor_tensor(out=OH[:], in0=OH[:], scalar=-float(NEXP), in1=io8, op0=ALU.mult, op1=ALU.add))
                step(v.tensor_reduce(ex[:], OH[:], X_, ALU.min))
                step(v.tensor_tensor(OH[:], OH[:], dup(ex[:], NEXP), ALU.is_equal))
                v.sem_inc(s_oh, 1)
                step(v.tensor_scalar(ex[:], ex[:], float(NEXP), None, ALU.add))
                step(v.tensor_tensor(L[:], L[:], dup(top[:], NEXP), ALU.subtract))
                v.sem_inc(s_l, 1)
                v.wait_ge(s_e, 1)
                step(v.tensor_reduce(a[:], tmp[:], X_, ALU.add))
                step(v.reciprocal(m.gscale[:], a[:]))
                v.wait_ge(s_mm, 2)
                p0 = m.ps[:, 0, 0:T * NEXP].rearrange("p (t e) -> p t e", e=NEXP)
                p1 = m.ps[:, 1, 0:T * NEXP].rearrange("p (t e) -> p t e", e=NEXP)
                step(v.tensor_copy(tot[:], p1))
                for e in range(NEXP):
                    ins = v.tensor_tensor_scan(tmp[:, :, e], m.ones[:, 0:T], tot[:, :, e], 0.0, ALU.mult, ALU.add)
                step(ins)
                step(v.tensor_tensor(tmp[:], tmp[:], tot[:], ALU.subtract))
                step(v.tensor_tensor(tmp[:], tmp[:], p0, ALU.add))
                step(v.tensor_tensor(tmp[:], tmp[:], OH[:], ALU.mult))
                step(v.tensor_reduce(pos[:], tmp[:], X_, ALU.add))
                step(v.tensor_scalar(kept[:], pos[:], float(CAP), None, ALU.is_le))
                step(v.tensor_tensor(m.gscale[:], m.gscale[:], kept[:], ALU.mult))
                step(v.tensor_scalar(ex[:], ex[:], float(CAP), -1.0, ALU.mult, ALU.add))
                step(v.scalar_tensor_tensor(out=a[:], in0=pos[:], scalar=float(CAP), in1=ex[:], op0=ALU.min, op1=ALU.add))
                step(v.tensor_copy(m.gidx[:], a[:]))
                v.wait_ge(s_io, 1)
                step(v.tensor_tensor(a[:], a[:], node[:], ALU.subtract))
                step(v.tensor_tensor(a[:], a[:], kept[:], ALU.mult))
                step(v.tensor_tensor(a[:], a[:], node[:], ALU.add))
                v.tensor_copy(idx[:], a[:]).then_inc(s_idx, 1)


def experts(nc, m, A):
    FT = HID // P
    with Phase(nc, "ex") as f:
        w1 = f.sb("w1", [P, 2, 2, HID])
        w2 = f.sb("w2", [P, 2, FT, D])
        xin = f.sb("xin", [P, 2, 4, D])
        xt = f.sb("xt", [P, 2, 512])
        b2 = f.sb("b2", [P, NEXP * D])
        b1r = f.sb("b1r", [NEXP * FT, P])
        b1 = f.sb("b1", [P, NEXP * FT])
        Y = f.sb("Y", [P, 2, 4, D])
        hid = m.ACC[:].rearrange("p t c -> p (t c)")[:, 0:FT * 512].rearrange("p (f n) -> p f n", f=FT)
        s_b = f.sem("b")
        s_bt = f.sem("bt")
        s_bc = f.sem("bc")
        s_in = [f.sem(f"in{q}") for q in range(2)]
        s_done = f.sem("done")
        s_tr = f.sem("tr")
        s_xt = f.sem("xt")
        s_up = f.sem("up")
        s_h = f.sem("h")
        s_dn = f.sem("dn")
        s_y = f.sem("y")
        s_turn = f.sem("turn")
        s_st = [f.sem(f"st{q}") for q in range(2)]
        last = CAP - 3 * P
        with nc.Block() as block:

            @block.sync
            def _(sp):
                sp.dma_start(b2[:], A["L0_ffn_b2"].rearrange("e d -> (e d)").partition_broadcast(P)).then_inc(s_b, 16)
                sp.dma_start(b1r[:], A["L0_ffn_b1"].rearrange("e (f p) -> (e f) p", p=P)).then_inc(s_b, 16)
                with sp.Fori(0, NEXP // 2) as i:
                    for q in range(2):
                        e = 2 * i + q
                        sp.wait_ge(s_done, e + 1)
                        sp.sem_inc(s_turn, 1)
                        sp.dma_start(xin[:, q, :, :], m.slots[ds(CAP * e, 4 * P), :].rearrange("(s p) d -> p s d", p=P)).then_inc(s_in[q], 16)
                        sp.dma_start(w1[:, q, :, :], A["L0_ffn_w1"].rearrange("e (k p) f -> p e k f", p=P)[:, ds(e, 1), :, :].rearrange("p o k f -> p (o k) f")).then_inc(s_in[q], 16)
                        sp.dma_start(w2[:, q, :, :], A["L0_ffn_w2"].rearrange("e (k p) f -> p e k f", p=P)[:, ds(e, 1), :, :].rearrange("p o k f -> p (o k) f")).then_inc(s_in[q], 16)

            @block.gpsimd
            def _(pool):
                with pool.Fori(0, NEXP // 2) as i:
                    for q in range(2):
                        e = 2 * i + q
                        pool.wait_ge(s_y, 4 * e + 4)
                        pool.sem_inc(s_turn, 1)
                        pool.dma_start(m.yslots[ds(CAP * e, 3 * P), :].rearrange("(s p) d -> p s d", p=P), Y[:, q, 0:3, :]).then_inc(s_st[q], 16)
                        pool.dma_start(m.yslots[ds(CAP * e + 3 * P, last), :], Y[0:last, q, 3, :]).then_inc(s_st[q], 16)
                for q in range(2):
                    pool.wait_ge(s_st[q], 32 * (NEXP // 2))

            @block.tensor
            def _(pe):
                pe.wait_ge(s_b, 32)
                pe.transpose(m.ps[:, 7, 0:NEXP * FT], b1r[:], m.ident[0:NEXP * FT, 0:NEXP * FT]).then_inc(s_bt, 1)
                pe.sem_inc(s_done, 2)
                pe.sem_inc(s_up, 2)
                with pe.Fori(0, NEXP // 2) as i:
                    for q in range(2):
                        e = 2 * i + q
                        pe.wait_ge(s_in[q], 48 * (i + 1))
                        pe.wait_ge(s_xt, 2 * e)
                        for k in range(2):
                            for s in range(4):
                                ins = pe.transpose(m.ps[:, k, s * P:(s + 1) * P], xin[:, q, s, k * P:(k + 1) * P], m.ident[:])
                            ins.then_inc(s_tr, 1)
                        pe.wait_ge(s_xt, 2 * e + 2)
                        for g in range(FT):
                            pe.wait_ge(s_h, FT * e + g + 1)
                            for k in range(2):
                                ins = pe.matmul(m.ps[:, 2 + g % 2, :], w1[:, q, k, g * P:(g + 1) * P], xt[:, k, :],
                                                start=(k == 0), stop=(k == 1))
                            ins.then_inc(s_up, 1)
                        pe.wait_ge(s_h, FT * e + FT + 2)
                        for s in range(4):
                            pe.wait_ge(s_y, 4 * e + s)
                            for g in range(FT):
                                ins = pe.matmul(m.ps[:, 4 + s, 0:D], hid[:, g, s * P:(s + 1) * P], w2[:, q, g, :],
                                                start=(g == 0), stop=(g == FT - 1))
                            ins.then_inc(s_dn, 1)
                        pe.drain().then_inc(s_done, 1)

            @block.scalar
            def _(act):
                act.wait_ge(s_bt, 1)
                act.copy(b1[:], m.ps[:, 7, 0:NEXP * FT]).then_inc(s_bc, 1)
                act.wait_ge(s_bc, 1)
                act.sem_inc(s_h, 2)
                with act.Fori(0, NEXP // 2) as i:
                    for q in range(2):
                        e = 2 * i + q
                        for k in range(2):
                            act.wait_ge(s_tr, 2 * e + k + 1)
                            act.copy(xt[:, k, :], m.ps[:, k, :]).then_inc(s_xt, 1)
                        for g in range(FT):
                            act.wait_ge(s_up, FT * e + g + 3)
                            act.activation(hid[:, g, :], m.ps[:, 2 + g % 2, :], ACT.Relu,
                                           bias=b1[:, ds(FT * e + g, 1)]).then_inc(s_h, 1)

            @block.vector
            def _(v):
                v.wait_ge(s_b, 32)
                with v.Fori(0, NEXP // 2) as i:
                    for q in range(2):
                        e = 2 * i + q
                        v.wait_ge(s_st[q], 32 * i)
                        for s in range(4):
                            v.wait_ge(s_dn, 4 * e + s + 1)
                            v.tensor_tensor(Y[:, q, s, :], m.ps[:, 4 + s, 0:D], b2[:, ds(D * e, D)], ALU.add).then_inc(s_y, 1)


def combine(nc, m):
    with Phase(nc, "cb") as f:
        r = f.sb("r", [P, U, D])
        r2 = f.sb("r2", [P, U, D])
        fin = f.sb("fin", [P, U, D], I32)
        s_g = [f.sem(f"g{k}") for k in range(TURNS)]
        s_v = f.sem("v")
        with nc.Block() as block:

            @block.gpsimd
            def _(pool):
                for t in range(T):
                    pool.indirect_dma_start(
                        out=m.ACC[:, t, 0:D], out_offset=None, in_=m.yslots[:, :],
                        in_offset=bass.IndirectOffsetOnAxis(ap=m.gidx[:, t:t + 1], axis=0)).then_inc(s_g[t // U], 16)

            @block.vector
            def _(v):
                step = Steps(v, s_v)
                for k in range(TURNS):
                    v.wait_ge(s_g[k], 16 * U)
                    y = m.ACC[:, U * k:U * k + U, 0:D]
                    v.tensor_scalar(r[:], y, FMAX, 1.0e4, ALU.is_gt, ALU.mult)
                    v.tensor_scalar(r2[:], y, -FMAX, -1.0e4, ALU.is_lt, ALU.mult)
                    step(v.tensor_scalar(fin[:], y, 0.0, 0.0, ALU.mult, ALU.is_equal))
                    step(v.tensor_tensor(r[:], r[:], r2[:], ALU.add))
                    step(v.copy_predicated(r[:], fin[:], y))
                    for j in range(U):
                        t = U * k + j
                        ins = v.scalar_tensor_tensor(out=m.X[:, t, :], in0=r[:, j, :], scalar=m.gscale[:, t:t + 1],
                                                     in1=m.X[:, t, :], op0=ALU.mult, op1=ALU.add)
                    step(ins)


def gate_attend(nc, m):
    H, HC = GH, 16
    W = HC + H
    with Phase(nc, "ga") as f:
        G = f.sb("G", [P, 2, FB, W])
        DD = f.sb("DD", [P, 2, FB, 2 * H])
        z = f.sb("z", [P, FB, H])
        ixs = f.sb("ixs", [P, 2, FB], U32)
        ixd = f.sb("ixd", [P, 2, FB], U32)
        lo = f.sb("lo", [P, 2, FB])
        hi = f.sb("hi", [P, 2, FB])
        S = f.sb("S", [P, FB, P])
        hot = f.sb("hot", [P, FB, T])
        R = f.sb("R", [P, FB, T, W])
        zz = f.sb("zz", [P, T * W])
        s_stage = f.sem("stage")
        s_rows = [f.sem(f"rows{q}") for q in range(2)]
        s_z = f.sem("z")
        s_w = f.sem("w")
        s_m = f.sem("m")
        s_S = f.sem("S")
        s_R = f.sem("R")
        s_mm = f.sem("mm")
        s_turn = f.sem("turn")
        s_v = f.sem("v")
        s_zero = f.sem("zero")
        s_end = f.sem("end")
        with nc.Block() as block:

            @block.scalar
            def _(act):
                def stage(b, q):
                    act.wait_ge(s_mm, FB * b + FB)
                    act.copy(ixs[:, q, :], m.fsrc[:, :, ds(b, 1)]).then_inc(s_stage, 1)
                    act.copy(ixd[:, q, :], m.fdst[:, :, ds(b, 1)]).then_inc(s_stage, 1)
                    act.copy(lo[:, q, :], m.flo[:, :, ds(b, 1)]).then_inc(s_stage, 1)
                    act.copy(hi[:, q, :], m.fhi[:, :, ds(b, 1)]).then_inc(s_stage, 1)

                def weights(b, q):
                    act.wait_ge(s_z, b + 1)
                    act.activation(G[:, q, :, HC:W], z[:], ACT.Exp).then_inc(s_w, 1)

                stage(0, 0)
                stage(1, 1)
                with act.Fori(0, FNBLK // 2 - 1) as i:
                    for q in range(2):
                        weights(2 * i + q, q)
                        stage(2 * i + q + 2, q)
                for q in range(2):
                    weights(FNBLK - 2 + q, q)

            @block.gpsimd
            def _(pool):
                with pool.Fori(0, FNBLK // 2) as i:
                    for q in range(2):
                        pool.wait_ge(s_stage, 4 * (2 * i + q) + 4)
                        pool.sem_inc(s_turn, 1)
                        for j in range(FB):
                            pool.indirect_dma_start(
                                out=G[:, q, j, :], out_offset=None, in_=m.gtable[:, :],
                                in_offset=bass.IndirectOffsetOnAxis(ap=ixs[:, q, j:j + 1], axis=0),
                            ).then_inc(s_rows[q], 16)
                            pool.indirect_dma_start(
                                out=DD[:, q, j, :], out_offset=None, in_=m.gedu[:, :],
                                in_offset=bass.IndirectOffsetOnAxis(ap=ixd[:, q, j:j + 1], axis=0),
                            ).then_inc(s_rows[q], 16)

            @block.vector
            def _(v):
                v.memset(zz[:], 0.0).then_inc(s_zero, 1)
                with v.Fori(0, FNBLK // 2) as i:
                    for q in range(2):
                        b = 2 * i + q
                        v.wait_ge(s_stage, 4 * b + 4)
                        v.wait_ge(s_mm, FB * b + 2 * FB)
                        io = m.iota[:, 0:P].rearrange("p (o c) -> p o c", o=1).broadcast_to([P, FB, P])
                        v.tensor_tensor(S[:], io, dup(lo[:, q, :], P), ALU.is_equal).then_inc(s_S, 1)
                        io = m.iota[:, 0:T].rearrange("p (o c) -> p o c", o=1).broadcast_to([P, FB, T])
                        v.tensor_tensor(hot[:], io, dup(hi[:, q, :], T), ALU.is_equal).then_inc(s_S, 1)
                        v.wait_ge(s_rows[q], 32 * FB * (i + 1))
                        edge_weights(v, s_z, s_w, Steps(v, s_v, 2 * b), z[:], G[:, q, :, HC:W],
                                     DD[:, q, :, 0:H], DD[:, q, :, H:2 * H])
                        v.wait_ge(s_w, b + 1)
                        g4 = G[:, q, :, 0:HC].rearrange("p j (h c) -> p j h c", h=H)
                        w4 = G[:, q, :, HC:W].rearrange("p j (h o) -> p j h o", o=1).broadcast_to([P, FB, H, HC // H])
                        v.tensor_tensor(g4, g4, w4, ALU.mult).then_inc(s_m, 1)
                        v.wait_ge(s_m, b + 1)
                        v.wait_ge(s_S, 2 * b + 2)
                        for j in range(FB):
                            val = G[:, q, j:j + 1, :].broadcast_to([P, T, W])
                            v.tensor_tensor(R[:, j, :, :], dup(hot[:, j, :], W), val, ALU.mult).then_inc(s_R, 1)

            @block.tensor
            def _(pe):
                pe.sem_inc(s_mm, 2 * FB)
                pe.wait_ge(s_zero, 1)
                pe.matmul(m.ps[:, 0, 0:T * W], zz[:, 0:P], zz[:], start=True, stop=False)
                with pe.Fori(0, FNBLK // 2) as i:
                    for q in range(2):
                        b = 2 * i + q
                        for j in range(FB):
                            pe.wait_ge(s_R, FB * b + j + 1)
                            pe.matmul(m.ps[:, 0, 0:T * W], S[:, j, :], R[:, j, :, :].rearrange("p t w -> p (t w)"),
                                      start=False, stop=False).then_inc(s_mm, 1)
                pe.matmul(m.ps[:, 0, 0:T * W], zz[:, 0:P], zz[:], start=False, stop=True).then_inc(s_end, 1)
        with nc.Block() as block:

            @block.vector
            def _(v):
                a = m.ACC[:, :, 0:W]
                v.tensor_tensor(a, a, m.ps[:, 0, 0:T * W].rearrange("p (t w) -> p t w", w=W), ALU.add).then_inc(s_v, 1)


def gates(nc, m, A):
    C = 16
    with Phase(nc, "gt") as f:
        vec = f.sb("vec", [P, 3, C])
        a = f.sb("a", [P, T, C])
        b = f.sb("b", [P, T, C])
        mu = f.sb("mu", [P, T])
        sd = f.sb("sd", [P, T])
        den = f.sb("den", [P, T, GH])
        sc = f.sb("sc", [P, T, KEXP])
        o1 = f.sb("o1", [P, T, KEXP])
        o2 = f.sb("o2", [P, T, KEXP])
        m1 = f.sb("m1", [P, T])
        m2 = f.sb("m2", [P, T])
        k1 = f.sb("k1", [P, T])
        s_dma = f.sem("dma")
        s_v = f.sem("v")
        s_var = f.sem("var")
        s_sd = f.sem("sd")
        s_d = f.sem("d")
        s_e = f.sem("e")
        with nc.Block() as block:

            @block.sync
            def _(sp):
                for k, name in enumerate(("L1_ffn_b_gat", "L1_ffn_ln_gamma", "L1_ffn_ln_beta")):
                    sp.dma_start(vec[:, k, :], A[name].partition_broadcast(P)).then_inc(s_dma, 16)

            @block.scalar
            def _(act):
                act.wait_ge(s_var, 1)
                act.activation(sd[:], sd[:], ACT.Sqrt).then_inc(s_sd, 1)
                act.wait_ge(s_d, 1)
                act.activation(m2[:], m2[:], ACT.Exp).then_inc(s_e, 1)

            @block.vector
            def _(v):
                step = Steps(v, s_v)

                def row(k):
                    return vec[:, k:k + 1, :].broadcast_to([P, T, C])

                step(v.tensor_scalar(den[:], m.ACC[:, :, C:C + GH], 1e-16, None, ALU.add))
                step(v.reciprocal(den[:], den[:]))
                step(v.tensor_tensor(a[:].rearrange("p t (h c) -> p t h c", h=GH),
                                     m.ACC[:, :, 0:C].rearrange("p t (h c) -> p t h c", h=GH),
                                     den[:].rearrange("p t (h o) -> p t h o", o=1).broadcast_to([P, T, GH, C // GH]), ALU.mult))
                v.wait_ge(s_dma, 48)
                step(v.tensor_tensor(a[:], a[:], row(0), ALU.add))
                step(v.tensor_reduce(mu[:], a[:], X_, ALU.add))
                step(v.tensor_scalar(mu[:], mu[:], 1.0 / C, None, ALU.mult))
                step(v.tensor_tensor(a[:], a[:], dup(mu[:], C), ALU.subtract))
                step(v.tensor_tensor(b[:], a[:], a[:], ALU.mult))
                step(v.tensor_reduce(sd[:], b[:], X_, ALU.add))
                step(v.tensor_scalar(sd[:], sd[:], 1.0 / C, EPS, ALU.mult, ALU.add))
                v.sem_inc(s_var, 1)
                v.wait_ge(s_sd, 1)
                step(v.reciprocal(sd[:], sd[:]))
                step(v.tensor_tensor(a[:], a[:], dup(sd[:], C), ALU.mult))
                step(v.tensor_tensor(a[:], a[:], row(1), ALU.mult))
                step(v.tensor_tensor(a[:], a[:], row(2), ALU.add))
                step(v.tensor_reduce(sc[:], a[:].rearrange("p t (h e) -> p t e h", h=GH), X_, ALU.add))
                step(v.tensor_scalar(sc[:], sc[:], 1.0 / GH, None, ALU.mult))
                io4 = m.iota[:, 0:KEXP].rearrange("p (o e) -> p o e", o=1).broadcast_to([P, T, KEXP])

                def first_best(o, best):
                    step(v.tensor_reduce(best[:], sc[:], X_, ALU.max))
                    step(v.tensor_tensor(o[:], sc[:], dup(best[:], KEXP), ALU.is_equal))
                    step(v.scalar_tensor_tensor(out=o[:], in0=o[:], scalar=-float(KEXP), in1=io4, op0=ALU.mult, op1=ALU.add))
                    step(v.tensor_reduce(k1[:], o[:], X_, ALU.min))
                    step(v.tensor_tensor(o[:], o[:], dup(k1[:], KEXP), ALU.is_equal))

                first_best(o1, m1)
                step(v.scalar_tensor_tensor(out=sc[:], in0=o1[:], scalar=NEG, in1=sc[:], op0=ALU.mult, op1=ALU.add))
                first_best(o2, m2)
                step(v.tensor_tensor(m2[:], m2[:], m1[:], ALU.subtract))
                v.sem_inc(s_d, 1)
                v.wait_ge(s_e, 1)
                step(v.tensor_scalar(m1[:], m2[:], 1.0, None, ALU.add))
                step(v.reciprocal(m1[:], m1[:]))
                step(v.tensor_tensor(m2[:], m2[:], m1[:], ALU.mult))
                step(v.tensor_tensor(o1[:], o1[:], dup(m1[:], KEXP), ALU.mult))
                step(v.tensor_tensor(o2[:], o2[:], dup(m2[:], KEXP), ALU.mult))
                step(v.tensor_tensor(m.gate[:], o1[:], o2[:], ALU.add))


def second_experts(nc, m, A, out):
    FT = HID2 // P
    CW = U * P
    HW = CW // 2
    with Phase(nc, "e2") as f:
        w1 = f.sb("w1", [P, KEXP, 2, HID2])
        w2 = f.sb("w2", [P, KEXP, FT, D])
        b2 = f.sb("b2", [P, KEXP, D])
        b1r = f.sb("b1r", [KEXP * FT, P])
        b1 = f.sb("b1", [P, KEXP * FT])
        hid = f.sb("hid", [P, 2, FT, CW])
        g = f.sb("g", [P, U, KEXP])
        y = f.sb("y", [P, U, D])
        s_in = f.sem("in")
        s_bt = f.sem("bt")
        s_bc = f.sem("bc")
        s_up = f.sem("up")
        s_h = f.sem("h")
        s_dn = f.sem("dn")
        s_y = f.sem("y")
        s_x = f.sem("x")
        s_g = f.sem("g")
        s_turn = f.sem("turn")
        s_out = f.sem("out")
        NU = 2 * FT
        with nc.Block() as block:

            @block.sync
            def _(sp):
                sp.dma_start(b1r[:], A["L1_ffn_b1"].rearrange("e (f p) -> (e f) p", p=P)).then_inc(s_in, 16)
                for e in range(KEXP):
                    sp.dma_start(w1[:, e, :, :], A["L1_ffn_W1"][e].rearrange("(k p) n -> p k n", p=P)).then_inc(s_in, 16)
                    sp.dma_start(w2[:, e, :, :], A["L1_ffn_W2"][e].rearrange("(k p) n -> p k n", p=P)).then_inc(s_in, 16)
                    sp.dma_start(b2[:, e, :], A["L1_ffn_b2"][e].partition_broadcast(P)).then_inc(s_in, 16)
                with sp.Fori(0, TURNS - 1) as i:
                    sp.wait_ge(s_x, KEXP * U * (i + 1))
                    sp.sem_inc(s_turn, 1)
                    sp.dma_start(out[ds(CW * i, CW), :].rearrange("(t p) d -> p t d", p=P), m.X[:, ds(U * i, U), :]).then_inc(s_out, 16)
                sp.wait_ge(s_x, KEXP * T)
                sp.dma_start(out[(TURNS - 1) * CW:(T - 1) * P, :].rearrange("(t p) d -> p t d", p=P), m.X[:, (TURNS - 1) * U:T - 1, :]).then_inc(s_out, 16)
                sp.dma_start(out[(T - 1) * P:N, :], m.X[0:TAIL, T - 1, :]).then_inc(s_out, 16)
                sp.wait_ge(s_out, 16 * (TURNS + 1))

            @block.tensor
            def _(pe):
                pe.wait_ge(s_in, 16 * (1 + 3 * KEXP))
                pe.transpose(m.ps[:, 7, 0:KEXP * FT], b1r[:], m.ident[0:KEXP * FT, 0:KEXP * FT]).then_inc(s_bt, 1)
                pe.sem_inc(s_up, 4)
                pe.sem_inc(s_dn, 4)
                with pe.Fori(0, TURNS) as i:
                    for e in range(KEXP):
                        at = NU * (KEXP * i + e)
                        for g_ in range(FT):
                            for hf in range(2):
                                n = 2 * g_ + hf
                                pe.wait_ge(s_h, at + n + 1)
                                for k in range(2):
                                    ins = pe.matmul(m.ps[:, n % 4, 0:HW], w1[:, e, k, g_ * P:(g_ + 1) * P],
                                                    m.XT[:, k, ds(CW * i + HW * hf, HW)], start=(k == 0), stop=(k == 1))
                                ins.then_inc(s_up, 1)
                        pe.wait_ge(s_h, at + NU + 4)
                        dn = U * (KEXP * i + e)
                        for j in range(U):
                            pe.wait_ge(s_y, dn + j + 1)
                            for g_ in range(FT):
                                ins = pe.matmul(m.ps[:, 4 + (U * e + j) % 4, 0:D], hid[:, e % 2, g_, j * P:(j + 1) * P], w2[:, e, g_, :],
                                                start=(g_ == 0), stop=(g_ == FT - 1))
                            ins.then_inc(s_dn, 1)

            @block.scalar
            def _(act):
                act.wait_ge(s_bt, 1)
                act.copy(b1[:], m.ps[:, 7, 0:KEXP * FT]).then_inc(s_bc, 1)
                act.wait_ge(s_bc, 1)
                act.sem_inc(s_h, 4)
                with act.Fori(0, TURNS) as i:
                    for e in range(KEXP):
                        at = NU * (KEXP * i + e)
                        for n in range(NU):
                            act.wait_ge(s_up, at + n + 5)
                            g_, hf = n // 2, n % 2
                            act.activation(hid[:, e % 2, g_, hf * HW:(hf + 1) * HW], m.ps[:, n % 4, 0:HW], ACT.Gelu,
                                           bias=b1[:, FT * e + g_:FT * e + g_ + 1]).then_inc(s_h, 1)

            @block.vector
            def _(v):
                v.sem_inc(s_y, 4)
                v.wait_ge(s_in, 16 * (1 + 3 * KEXP))
                v.wait_ge(s_bc, 1)
                with v.Fori(0, TURNS) as i:
                    v.wait_ge(s_x, KEXP * U * i)
                    v.tensor_copy(g[:], m.gate[:, ds(U * i, U), :]).then_inc(s_g, 1)
                    v.wait_ge(s_g, i + 1)
                    for e in range(KEXP):
                        dn = U * (KEXP * i + e)
                        for j in range(U):
                            v.wait_ge(s_dn, dn + j + 5)
                            if e:
                                v.wait_ge(s_x, dn - U + j + 1)
                            v.tensor_tensor(y[:, j, :], m.ps[:, 4 + (U * e + j) % 4, 0:D], b2[:, e, :], ALU.add).then_inc(s_y, 1)
                        for j in range(U):
                            v.wait_ge(s_y, dn + j + 5)
                            x = m.X[:, ds(U * i + j, 1), :]
                            v.scalar_tensor_tensor(out=x, in0=y[:, j:j + 1, :], scalar=g[:, j, e:e + 1], in1=x,
                                                   op0=ALU.mult, op1=ALU.add).then_inc(s_x, 1)


def add_to_x(nc, m, name):
    with Phase(nc, name) as f:
        s = f.sem("s")
        with nc.Block() as block:

            @block.vector
            def _(v):
                v.tensor_tensor(m.X[:], m.X[:], m.ACC[:, :, 0:D], ALU.add).then_inc(s, 1)


def load_rows(nc, m, name, aps):
    with Phase(nc, name) as f:
        s = f.sem("s")
        with nc.Block() as block:

            @block.sync
            def _(sp):
                for k, ap in enumerate(aps):
                    sp.dma_start(m.vec[:, k, :], ap.partition_broadcast(P)).then_inc(s, 16)
                sp.wait_ge(s, 16 * len(aps))


def store_x(nc, m, out):
    with Phase(nc, "end") as f:
        s = f.sem("s")
        with nc.Block() as block:

            @block.sync
            def _(sp):
                sp.dma_start(out[0:(T - 1) * P, :].rearrange("(t p) d -> p t d", p=P), m.X[:, 0:T - 1, :]).then_inc(s, 16)
                sp.dma_start(out[(T - 1) * P:N, :], m.X[0:TAIL, T - 1, :]).then_inc(s, 16)
                sp.wait_ge(s, 32)


def program(nc, A, out, upto=99):
    ctx = ExitStack()
    m = Memory()
    m.support = [nc.dram_tensor(f"support{k}", (NP_, D), F32).ap() for k in range(2)]
    m.slots = nc.dram_tensor("slots", (NEXP * CAP + NP_, D), F32).ap()
    m.yslots = nc.dram_tensor("yslots", (NEXP * CAP, D), F32).ap()
    m.atable = [nc.dram_tensor(f"atable{k}", (NP_, D + h), F32).ap() for k, h in ((0, 4), (1, 1))]
    m.aedu = [nc.dram_tensor(f"aedu{k}", (NP_, 2 * h), F32).ap() for k, h in ((0, 4), (1, 1))]
    m.gtable = nc.dram_tensor("gtable", (NP_, 20), F32).ap()
    m.gedu = nc.dram_tensor("gedu", (NP_, 8), F32).ap()
    with ctx:
        alloc(nc, ctx, m)
        prepare(nc, m, A)
        row_moments(nc, m, "m0", m.X)
        project(nc, m, "p0", "ln", m.W["c1"], D, table=m.support[0])
        convolve(nc, m, "c0", m.support[0])
        project(nc, m, "p1", "acc", m.W["c2"], D, table=m.support[1])
        convolve(nc, m, "c1", m.support[1])
        add_to_x(nc, m, "a1")
        if upto == 1:
            return store_x(nc, m, out)
        row_moments(nc, m, "m1", m.X)
        project(nc, m, "route", "ln", m.W["gate"], NEXP)
        route(nc, m, A)
        experts(nc, m, A)
        combine(nc, m)
        if upto == 2:
            return store_x(nc, m, out)
        row_moments(nc, m, "m2", m.X)
        load_rows(nc, m, "lv", (A["L1_gnn_ln_g"], A["L1_gnn_ln_b"]))
        project(nc, m, "p2", "ln", m.W["g1"], D + 4, heads=4, table=m.atable[0])
        self_loops(nc, m, "s2", D, 4, m.aedu[0], LOOPS)
        attend(nc, m, "t2", 4, m.atable[0], m.aedu[0])
        finish_attention(nc, m, "f2", 4, A["L1_gnn_b1"], False)
        if upto == 25:
            m.X = m.ACC[:, :, 0:D]
            return store_x(nc, m, out)
        row_moments(nc, m, "m3", m.ACC[:, :, 0:D])
        project(nc, m, "p3", "relu", m.W["g2"], D + 1, heads=1, table=m.atable[1],
                vecs=(m.vec[:, 0, :], m.vec[:, 1, :]))
        self_loops(nc, m, "s3", D, 1, m.aedu[1], LOOPS)
        attend(nc, m, "t3", 1, m.atable[1], m.aedu[1])
        finish_attention(nc, m, "f3", 1, A["L1_gnn_b2"], True)
        if upto == 3:
            return store_x(nc, m, out)
        row_moments(nc, m, "m4", m.X)
        project(nc, m, "gatep", "ln", m.W["gat"], 20, heads=4, table=m.gtable)
        self_loops(nc, m, "s4", 16, 4, m.gedu, N)
        gate_attend(nc, m)
        gates(nc, m, A)
        second_experts(nc, m, A, out)


_INS = ['x', 'src', 'dst', 'edge_weight', 'L0_gnn_W1', 'L0_gnn_W2', 'L0_ffn_gate_w', 'L0_ffn_gate_b', 'L0_ffn_w1',
        'L0_ffn_b1', 'L0_ffn_w2', 'L0_ffn_b2', 'L1_gnn_W1', 'L1_gnn_a1_src', 'L1_gnn_a1_dst', 'L1_gnn_b1',
        'L1_gnn_ln_g', 'L1_gnn_ln_b', 'L1_gnn_W2', 'L1_gnn_a2_src', 'L1_gnn_a2_dst', 'L1_gnn_b2', 'L1_ffn_W_gat',
        'L1_ffn_att_src', 'L1_ffn_att_dst', 'L1_ffn_b_gat', 'L1_ffn_ln_gamma', 'L1_ffn_ln_beta', 'L1_ffn_W1',
        'L1_ffn_b1', 'L1_ffn_W2', 'L1_ffn_b2', 'L1_ffn_edge_index']


def kernel(**inputs):
    import numpy as _np
    import concourse.bacc as _bacc
    from concourse import mybir as _mybir
    from concourse.bass_utils import run_bass_kernel_spmd as _run

    nc = _bacc.Bacc("TRN2", target_bir_lowering=False, num_devices=1)
    arrays, args = {}, {}
    for name in _INS:
        a = _np.ascontiguousarray(inputs[name])
        arrays[f"in_{name}_dram"] = a
        args[name] = nc.dram_tensor(f"in_{name}_dram", a.shape, _mybir.dt.from_np(a.dtype), kind="ExternalInput").ap()
    out = nc.dram_tensor("out_0_dram", (N, D), _mybir.dt.float32, kind="ExternalOutput").ap()
    program(nc, args, out)
    r = _run(nc, [arrays], core_ids=[0])
    return r.results[0]["out_0_dram"]
```

```python
from contextlib import ExitStack

import concourse.bass as bass
from concourse import mybir

P = 128
D = 256
N = 3125
T = 25
NP_ = T * P
TAIL = N - (T - 1) * P
U = 5
TURNS = T // U

E0 = 50000
B = 7
NBLK = 56
EPAD = NBLK * B * P
ROWE = B * P
DEPTH = 7
AHEAD = 3
LEAD = DEPTH - AHEAD
NONE = T
VIS = NBLK * T + 4
TURNS2 = NBLK * T // 2 + 1

E1 = 32768
FB = 13
FROW = FB * P
FNBLK = -(-E1 // FROW)

NEXP = 8
CAP = 489
HID = 1024
KEXP = 4
HID2 = 512
GH = 4
EPS = 1e-5
SLOPE = 0.2
LOOPS = 625
NEG = -1.0e30
FMAX = 3.4028234663852886e38

ALU = mybir.AluOpType
ACT = mybir.ActivationFunctionType
F32 = mybir.dt.float32
BF16 = mybir.dt.bfloat16
U16 = mybir.dt.uint16
I32 = mybir.dt.int32
U32 = mybir.dt.uint32
X_ = mybir.AxisListType.X
ds = bass.ds


class Steps:

    def __init__(self, eng, sem, start=0):
        self.eng, self.sem, self.at = eng, sem, start

    def __call__(self, ins):
        ins.then_inc(self.sem, 1)
        self.at = self.at + 1
        self.eng.wait_ge(self.sem, self.at)


class Phase:

    def __init__(self, nc, name):
        self.nc, self.name, self.ctx, self.sems = nc, name, ExitStack(), []

    def __enter__(self):
        return self

    def __exit__(self, *a):
        self.ctx.close()
        self.nc.clear_and_free_semaphores(self.sems)
        self.nc.all_engine_barrier()

    def sb(self, name, shape, dt=F32):
        return self.ctx.enter_context(self.nc.sbuf_tensor(f"{self.name}_{name}", shape, dt))

    def sem(self, name):
        self.sems.append(self.nc.alloc_semaphore(f"{self.name}_{name}"))
        return self.sems[-1]


class Memory:
    pass


def dup(ap, k):
    p, a = ap.shape
    return ap.rearrange("p (a o) -> p a o", o=1).broadcast_to([p, a, k])


def alloc(nc, ctx, m):
    def sb(name, shape, dt=F32):
        return ctx.enter_context(nc.sbuf_tensor(name, shape, dt))

    m.X = sb("X", [P, T, D])
    m.ACCX = sb("ACC", [P, T + 1, D + GH])
    m.ACC = m.ACCX[:, 0:T, :]
    m.XN = sb("XN", [P, T, D])
    m.iota = sb("iota", [P, NP_ + P])
    m.pcol = sb("pcol", [P, 1])
    m.ident = sb("ident", [P, P])
    m.upper = sb("upper", [P, P])
    m.ones = sb("ones", [P, P])
    m.pen = sb("pen", [P, 1])
    m.own = sb("own", [P, 1])
    m.src = sb("src_t", [P, NBLK, B], U32)
    m.dw = sb("dw_t", [P, NBLK, 2, B])
    m.tiles = sb("tiles", [1, TURNS2], I32)
    m.blocks = sb("blocks", [1, TURNS2], I32)
    m.cum = sb("cum", [1, LEAD + NBLK], I32)
    m.fsrc = sb("fsrc", [P, FB, FNBLK], U32)
    m.fdst = sb("fdst", [P, FB, FNBLK], U32)
    m.flo = sb("flo", [P, FB, FNBLK])
    m.fhi = sb("fhi", [P, FB, FNBLK])
    m.mean = sb("mean", [P, T])
    m.rstd = sb("rstd", [P, T])
    m.XT = m.XN[:].rearrange("p t c -> p (t c)").rearrange("p (k n) -> p k n", k=2)
    m.vec = sb("vec", [P, 2, D])
    m.gscale = sb("gscale", [P, T])
    m.gidx = sb("gidx", [P, T], U32)
    m.gate = sb("gate", [P, T, KEXP])
    m.EDU = sb("EDU", [P, T, 2 * GH])
    m.EDB = sb("EDB", [P, T + 1, 6 * GH], BF16)
    m.W = {k: sb(f"W_{k}", [P, 2, n]) for k, n in
           (("c1", D), ("c2", D), ("g1", D + 8), ("g2", D + 2), ("gate", 8), ("gat", 24))}
    m.ps = ctx.enter_context(nc.psum_tensor("ps", [P, 8, 512], F32))


def prepare(nc, m, A):
    with Phase(nc, "prep") as f:
        raw = f.sb("raw", [NBLK, 2, ROWE], I32)
        rawf = f.sb("rawf", [NBLK, 3, ROWE])
        fraw = f.sb("fraw", [FNBLK, 2, FROW], I32)
        frawf = f.sb("frawf", [FNBLK, 4, FROW])
        bi = f.sb("bi", [NBLK, 2], I32)
        bf = f.sb("bf", [NBLK, 2])
        cnt = f.sb("cnt", [NBLK, 4])
        inb = f.sb("inb", [NBLK, VIS])
        spare = m.ACC.rearrange("p t c -> p (t c)")
        inb2 = spare[0:NBLK, 0:VIS]
        seq = f.sb("seq", [1, 3, VIS + 1])
        fifth = f.sb("fifth", [1, TURNS2], I32)
        half = f.sb("half", [1, 2, TURNS2])
        rows16 = f.sb("rows16", [NBLK, ROWE], U16)
        s_sum = f.sem("sum")
        s_base = f.sem("base")
        s_vis = f.sem("vis")
        s_r16 = f.sem("r16")
        s_rd = f.sem("rd")
        att = spare[:, VIS:VIS + 4 * D + 32]
        prod = spare[:, VIS + 4 * D + 32:VIS + 5 * D + 32]
        s_in = f.sem("in")
        s_fill = f.sem("fill")
        s_edge = f.sem("edge")
        s_iota = f.sem("iota")
        s_v = f.sem("v")
        s_tr = f.sem("tr")
        s_cp = f.sem("cp")
        s_row = f.sem("row")
        s_zero = f.sem("zero")
        full = E0 // ROWE
        rest = E0 - full * ROWE
        fwhole = E1 // FROW
        frest = E1 - fwhole * FROW
        zrow = 15 * P
        with nc.Block() as block:

            @block.sync
            def _(sp):
                sp.dma_start(m.W["c1"][:], A["L0_gnn_W1"].rearrange("(k p) n -> p k n", p=P)).then_inc(s_in, 16)
                sp.dma_start(m.W["c2"][:], A["L0_gnn_W2"].rearrange("(k p) n -> p k n", p=P)).then_inc(s_in, 16)
                sp.dma_start(m.W["g1"][:, :, 0:D], A["L1_gnn_W1"].rearrange("(k p) n -> p k n", p=P)).then_inc(s_in, 16)
                sp.dma_start(m.W["g2"][:, :, 0:D], A["L1_gnn_W2"].rearrange("(k p) n -> p k n", p=P)).then_inc(s_in, 16)
                sp.dma_start(m.W["gate"][:], A["L0_ffn_gate_w"].rearrange("(k p) n -> p k n", p=P)).then_inc(s_in, 16)
                sp.dma_start(m.W["gat"][:, :, 0:16], A["L1_ffn_W_gat"].rearrange("(k p) n -> p k n", p=P)).then_inc(s_in, 16)
                for k, name in enumerate(("L1_gnn_a1_src", "L1_gnn_a1_dst", "L1_gnn_a2_src", "L1_gnn_a2_dst")):
                    sp.dma_start(att[:, k * D:(k + 1) * D],
                                 A[name].rearrange("a b -> (a b)").partition_broadcast(P)).then_inc(s_in, 16)
                for k, name in enumerate(("L1_ffn_att_src", "L1_ffn_att_dst")):
                    sp.dma_start(att[:, 4 * D + 16 * k:4 * D + 16 * k + 16],
                                 A[name].rearrange("a b -> (a b)").partition_broadcast(P)).then_inc(s_in, 16)
                sp.wait_ge(s_fill, 5)
                for k, name in enumerate(("src", "dst")):
                    sp.dma_start(raw[0:full, k, :], A[name][0:full * ROWE].rearrange("(b e) -> b e", e=ROWE)).then_inc(s_edge, 16)
                    sp.dma_start(raw[full:full + 1, k, 0:rest], A[name][full * ROWE:E0].rearrange("(b e) -> b e", b=1)).then_inc(s_edge, 16)
                sp.dma_start(rawf[0:full, 2, :], A["edge_weight"][0:full * ROWE].rearrange("(b e) -> b e", e=ROWE)).then_inc(s_edge, 16)
                sp.dma_start(rawf[full:full + 1, 2, 0:rest], A["edge_weight"][full * ROWE:E0].rearrange("(b e) -> b e", b=1)).then_inc(s_edge, 16)
                for k in range(2):
                    edge = A["L1_ffn_edge_index"][k]
                    sp.dma_start(fraw[0:fwhole, k, :], edge[0:fwhole * FROW].rearrange("(b e) -> b e", e=FROW)).then_inc(s_edge, 16)
                    sp.dma_start(fraw[fwhole:fwhole + 1, k, 0:frest], edge[fwhole * FROW:E1].rearrange("(b e) -> b e", b=1)).then_inc(s_edge, 16)
                sp.wait_ge(s_in, 12 * 16)
                sp.wait_ge(s_edge, 10 * 16)
                sp.wait_ge(s_r16, 1)
                sp.dma_start(m.drows[:, :], rows16[:]).then_inc(s_rd, 16)
                sp.wait_ge(s_rd, 16)

            @block.scalar
            def _(act):
                act.wait_ge(s_fill, 6)
                act.dma_start(m.X[:, 0:T - 1, :], A["x"][0:(T - 1) * P, :].rearrange("(t p) d -> p t d", p=P)).then_inc(s_zero, 16)
                act.dma_start(m.X[0:TAIL, T - 1, :], A["x"][(T - 1) * P:N, :]).then_inc(s_zero, 16)
                act.wait_ge(s_fill, 7)
                zero = m.XN[:, 0:15, :]
                for k in range(2):
                    act.dma_start(m.slots[k * zrow:(k + 1) * zrow, :].rearrange("(p a) d -> p a d", p=P), zero).then_inc(s_zero, 16)
                act.dma_start(m.slots[2 * zrow:2 * zrow + P, :], m.XN[:, 0, :]).then_inc(s_zero, 16)
                act.wait_ge(s_zero, 5 * 16)

            @block.gpsimd
            def _(pool):
                pool.iota(m.iota[:], [[1, NP_ + P]], base=0, channel_multiplier=0,
                          allow_small_or_imprecise_dtypes=True).then_inc(s_iota, 1)
                pool.iota(m.pcol[:], [[0, 1]], base=0, channel_multiplier=1,
                          allow_small_or_imprecise_dtypes=True).then_inc(s_iota, 1)

            @block.vector
            def _(v):
                v.memset(raw[:, 0, :], 0).then_inc(s_fill, 1)
                v.memset(raw[:, 1, :], NP_ - 1).then_inc(s_fill, 1)
                v.memset(rawf[:, 2, :], 0.0).then_inc(s_fill, 1)
                v.memset(fraw[:, 0, :], 0).then_inc(s_fill, 1)
                v.memset(fraw[:, 1, :], NP_ - 1).then_inc(s_fill, 1)
                v.memset(m.X[:, T - 1, :], 0.0).then_inc(s_fill, 1)
                v.memset(m.XN[:], 0.0).then_inc(s_fill, 1)
                step = Steps(v, s_v)
                v.memset(m.ACCX[:, T:T + 1, :], 0.0).then_inc(s_fill, 1)
                v.memset(m.EDB[:, T:T + 1, :], 0.0).then_inc(s_fill, 1)
                v.memset(m.ones[:], 1.0).then_inc(s_fill, 1)
                v.wait_ge(s_iota, 2)
                step(v.tensor_scalar(m.ident[:], m.iota[:, 0:P], m.pcol[:, 0:1], None, ALU.is_equal))
                step(v.tensor_scalar(m.upper[:], m.iota[:, 0:P], m.pcol[:, 0:1], None, ALU.is_ge))
                step(v.tensor_scalar(m.pen[:], m.pcol[:], float(TAIL), NEG, ALU.is_ge, ALU.mult))
                step(v.tensor_scalar(m.own[:], m.pcol[:], float(LOOPS % P), NEG, ALU.is_ge, ALU.mult))
                v.wait_ge(s_in, 12 * 16)
                for k in range(2):
                    for name, heads, base in (("g1", 4, 0), ("g2", 1, 2 * D)):
                        w = m.W[name]
                        for a in range(2):
                            step(v.tensor_tensor(prod[:, 0:D], w[:, k, 0:D], att[:, base + a * D:base + (a + 1) * D], ALU.mult))
                            step(v.tensor_reduce(w[:, k, D + a * heads:D + (a + 1) * heads],
                                                 prod[:, 0:D].rearrange("p (h c) -> p h c", h=heads), X_, ALU.add))
                    for a in range(2):
                        w = m.W["gat"]
                        step(v.tensor_tensor(prod[:, 0:16], w[:, k, 0:16], att[:, 4 * D + 16 * a:4 * D + 16 * a + 16], ALU.mult))
                        step(v.tensor_reduce(w[:, k, 16 + 4 * a:20 + 4 * a],
                                             prod[:, 0:16].rearrange("p (h c) -> p h c", h=4), X_, ALU.add))
                v.wait_ge(s_edge, 10 * 16)
                step(v.tensor_copy(rawf[:, 0:2, :], raw[:]))
                step(v.tensor_reduce(bf[:, 0:1], rawf[:, 1, :], X_, ALU.min))
                step(v.tensor_reduce(bf[:, 1:2], rawf[:, 1, :], X_, ALU.max))
                step(v.tensor_copy(bi[:], bf[:]))
                step(v.tensor_scalar(bi[:], bi[:], 7, None, ALU.logical_shift_right))
                step(v.tensor_copy(bf[:], bi[:]))
                step(v.tensor_copy(frawf[:, 0:2, :], fraw[:]))
                step(v.tensor_scalar(fraw[:, 0, :], fraw[:, 1, :], 7, None, ALU.logical_shift_right))
                step(v.tensor_scalar(fraw[:, 1, :], fraw[:, 1, :], P - 1, None, ALU.bitwise_and))
                step(v.tensor_copy(frawf[:, 2:4, :], fraw[:]))
                v.sem_inc(s_row, 1)
                v.tensor_copy(rows16[:], rawf[:, 1, :]).then_inc(s_r16, 1)
                n = 0
                for k, out in ((0, m.src[:]), (1, m.dw[:, :, 0, :]), (2, m.dw[:, :, 1, :])):
                    n += 1
                    v.wait_ge(s_tr, n)
                    v.tensor_copy(out.rearrange("p b j -> p j b"), m.ps[:, 0, 0:B * NBLK].rearrange("p (j b) -> p j b", j=B)).then_inc(s_cp, 1)
                for k, out in enumerate((m.fsrc, m.fdst, m.fhi, m.flo)):
                    n += 1
                    v.wait_ge(s_tr, n)
                    v.tensor_copy(out[:], m.ps[:, 0, 0:FB * FNBLK].rearrange("p (j b) -> p j b", j=FB)).then_inc(s_cp, 1)
                step(v.tensor_tensor(cnt[:, 0:1], bf[:, 1:2], bf[:, 0:1], ALU.subtract))
                step(v.tensor_scalar(cnt[:, 0:1], cnt[:, 0:1], 1.0, None, ALU.add))
                v.sem_inc(s_base, 1)
                v.wait_ge(s_sum, 1)
                step(v.tensor_copy(cnt[:, 1:2], m.ps[0:NBLK, 1, 0:1]))
                v.sem_inc(s_base, 1)
                step(v.tensor_tensor(cnt[:, 2:3], cnt[:, 1:2], cnt[:, 0:1], ALU.subtract))
                step(v.tensor_tensor(cnt[:, 3:4], bf[:, 0:1], cnt[:, 2:3], ALU.subtract))
                io = m.iota[0:NBLK, 0:VIS]
                step(v.tensor_scalar(inb2, io, cnt[:, 1:2], None, ALU.is_lt))
                step(v.scalar_tensor_tensor(out=inb[:], in0=io, scalar=cnt[:, 2:3], in1=inb2, op0=ALU.is_ge, op1=ALU.mult))
                v.sem_inc(s_base, 1)
                v.wait_ge(s_sum, 2)
                v.memset(m.cum[:], 0).then_inc(s_vis, 1)
                v.wait_ge(s_vis, 1)
                step(v.tensor_copy(m.cum[:, LEAD:LEAD + NBLK], m.ps[0:1, 1, 0:NBLK]))
                for k in range(3):
                    v.wait_ge(s_sum, 3 + k)
                    step(v.tensor_copy(seq[:, k, 1:VIS + 1].rearrange("p (a c) -> p a c", a=3), m.ps[0:1, 2:5, 0:VIS // 3]))
                    v.sem_inc(s_vis, 1)
                tl, bl, on = seq[:, 0, 1:VIS + 1], seq[:, 1, 1:VIS + 1], seq[:, 2, 1:VIS + 1]
                step(v.tensor_tensor(tl, tl, m.iota[0:1, 0:VIS], ALU.add))
                step(v.scalar_tensor_tensor(out=tl, in0=tl, scalar=-float(NONE), in1=on, op0=ALU.add, op1=ALU.mult))
                step(v.tensor_scalar(tl, tl, float(NONE), None, ALU.add))
                step(v.scalar_tensor_tensor(out=bl, in0=bl, scalar=-float(NBLK - 1), in1=on, op0=ALU.add, op1=ALU.mult))
                step(v.tensor_scalar(bl, bl, float(NBLK - 1), None, ALU.add))
                step(v.memset(seq[:, 0, 0:1], float(NONE)))
                def pick(k, at):
                    return seq[:, k, at:at + 2 * TURNS2 - 1:2]

                step(v.scalar_tensor_tensor(out=half[:, 0, :], in0=pick(0, 1), scalar=32.0, in1=pick(0, 0), op0=ALU.mult, op1=ALU.add))
                step(v.scalar_tensor_tensor(out=half[:, 0, :], in0=pick(0, 2), scalar=1024.0, in1=half[:, 0, :], op0=ALU.mult, op1=ALU.add))
                step(v.scalar_tensor_tensor(out=half[:, 0, :], in0=pick(0, 3), scalar=32768.0, in1=half[:, 0, :], op0=ALU.mult, op1=ALU.add))
                step(v.scalar_tensor_tensor(out=half[:, 1, :], in0=pick(1, 2), scalar=64.0, in1=pick(1, 1), op0=ALU.mult, op1=ALU.add))
                step(v.scalar_tensor_tensor(out=half[:, 1, :], in0=pick(1, 3), scalar=4096.0, in1=half[:, 1, :], op0=ALU.mult, op1=ALU.add))
                step(v.scalar_tensor_tensor(out=half[:, 1, :], in0=pick(1, 4), scalar=262144.0, in1=half[:, 1, :], op0=ALU.mult, op1=ALU.add))
                step(v.tensor_copy(m.tiles[:], half[:, 0, :]))
                step(v.tensor_copy(m.blocks[:], half[:, 1, :]))
                step(v.tensor_copy(fifth[:], pick(0, 4)))
                step(v.tensor_scalar(fifth[:], fifth[:], 20, None, ALU.logical_shift_left))
                step(v.tensor_tensor(m.tiles[:], m.tiles[:], fifth[:], ALU.bitwise_or))

            @block.tensor
            def _(pe):
                pe.wait_ge(s_row, 1)
                n = 0
                for k in (0, 1, 2):
                    if n:
                        pe.wait_ge(s_cp, n)
                    for j in range(B):
                        last = pe.transpose(m.ps[:, 0, j * NBLK:(j + 1) * NBLK], rawf[:, k, j * P:(j + 1) * P],
                                            m.ident[0:NBLK, 0:NBLK])
                    last.then_inc(s_tr, 1)
                    n += 1
                for k in range(4):
                    pe.wait_ge(s_cp, n)
                    for j in range(FB):
                        last = pe.transpose(m.ps[:, 0, j * FNBLK:(j + 1) * FNBLK], frawf[:, k, j * P:(j + 1) * P],
                                            m.ident[0:FNBLK, 0:FNBLK])
                    last.then_inc(s_tr, 1)
                    n += 1
                pe.wait_ge(s_base, 1)
                pe.matmul(m.ps[0:NBLK, 1, 0:1], m.upper[0:NBLK, 0:NBLK], cnt[:, 0:1], start=True, stop=True).then_inc(s_sum, 1)
                pe.wait_ge(s_base, 2)
                pe.transpose(m.ps[0:1, 1, 0:NBLK], cnt[:, 1:2], m.ident[0:NBLK, 0:NBLK]).then_inc(s_sum, 1)
                pe.wait_ge(s_base, 3)
                for k, col in enumerate((cnt[:, 3:4], m.pcol[0:NBLK, 0:1], m.ones[0:NBLK, 0:1])):
                    pe.wait_ge(s_vis, k + 1)
                    for a in range(3):
                        last = pe.matmul(m.ps[0:1, 2 + a, 0:VIS // 3], col, inb[:, a * (VIS // 3):(a + 1) * (VIS // 3)],
                                         start=True, stop=True)
                    last.then_inc(s_sum, 1)


def row_moments(nc, m, name, src):
    with Phase(nc, name) as f:
        st = f.sb("st", [P, U, 6])
        mv = f.sb("mv", [P, U, 2])
        s_st = f.sem("st")
        s_mv = f.sem("mv")
        s_cp = f.sem("cp")
        s_v = f.sem("v")
        s_sq = f.sem("sq")
        s_turn = f.sem("turn")
        with nc.Block() as block:

            @block.vector
            def _(v):
                with v.Fori(0, TURNS) as i:
                    for j in range(U):
                        v.bn_stats(st[:, j, :], src[:, ds(U * i + j, 1), :]).then_inc(s_st, 1)
                    v.wait_ge(s_cp, 2 * i)
                    for j in range(U):
                        v.wait_ge(s_st, U * i + j + 1)
                        v.sem_inc(s_turn, 1)
                        v.bn_aggr(mv[:, j, :], st[:, j, :]).then_inc(s_mv, 1)
                    v.wait_ge(s_mv, U * i + U)
                    v.tensor_copy(m.mean[:, ds(U * i, U)], mv[:, :, 0]).then_inc(s_cp, 1)
                    v.tensor_scalar(m.rstd[:, ds(U * i, U)], mv[:, :, 1], EPS, None, ALU.add).then_inc(s_cp, 1)
                v.wait_ge(s_sq, 1)
                v.reciprocal(m.rstd[:], m.rstd[:]).then_inc(s_v, 1)

            @block.scalar
            def _(act):
                act.wait_ge(s_cp, 2 * TURNS)
                act.activation(m.rstd[:], m.rstd[:], ACT.Sqrt).then_inc(s_sq, 1)


def project(nc, m, name, kind, w, cols, heads=0, table=None, vecs=None):
    full = cols + heads
    width = cols + 1 if heads == 1 else cols
    with Phase(nc, name) as f:
        xs = f.sb("xs", [P, U, D])
        xt = f.sb("xt", [P, U, 2, P])
        s_xs = f.sem("xs")
        s_tr = f.sem("tr")
        s_xt = f.sem("xt")
        s_mm = f.sem("mm")
        s_out = f.sem("out")
        s_keep = f.sem("keep")
        s_dma = f.sem("dma")
        s_v = f.sem("v")
        s_one = f.sem("one")
        keep_x = name == "route"
        keep_xt = name == "gatep"

        def p_turn(j):
            return m.ps[:, j, 0:2 * P]

        with nc.Block() as block:

            @block.sync
            def _(sp):
                if heads == 1:
                    sp.wait_ge(s_one, 1)
                if table is not None:
                    with sp.Fori(0, TURNS) as i:
                        sp.wait_ge(s_out, U * i + 2 * U)
                        sp.sem_inc(s_keep, 1)
                        sp.dma_start(table.rearrange("(t p) c -> p t c", p=P)[:, ds(U * i, U), :],
                                     m.ACC[:, ds(U * i, U), 0:width]).then_inc(s_dma, 16)
                    sp.wait_ge(s_dma, 16 * TURNS)

            @block.vector
            def _(v):
                if heads == 1:
                    v.memset(m.ACC[:, :, D:D + 1], 1.0).then_inc(s_one, 1)
                with v.Fori(0, TURNS) as i:
                    for j in range(U):
                        t = U * i + j
                        v.wait_ge(s_tr, t + 1)
                        if keep_x:
                            v.wait_ge(s_keep, t + 1)
                        if kind == "acc":
                            v.tensor_copy(xs[:, j, :], m.ACC[:, ds(t, 1), 0:D]).then_inc(s_xs, 1)
                            continue
                        src = m.X[:, ds(t, 1), :] if kind == "ln" else m.ACC[:, ds(t, 1), 0:D]
                        ins = v.tensor_scalar(xs[:, j, :], src, m.mean[:, ds(t, 1)], m.rstd[:, ds(t, 1)],
                                              ALU.subtract, ALU.mult)
                        if kind == "relu":
                            base = 3 * t
                            ins.then_inc(s_v, 1)
                            v.wait_ge(s_v, base + 1)
                            v.tensor_tensor(xs[:, j, :], xs[:, j, :], vecs[0], ALU.mult).then_inc(s_v, 1)
                            v.wait_ge(s_v, base + 2)
                            v.tensor_tensor(xs[:, j, :], xs[:, j, :], vecs[1], ALU.add).then_inc(s_v, 1)
                            v.wait_ge(s_v, base + 3)
                            ins = v.tensor_scalar(xs[:, j, :], xs[:, j, :], 0.0, None, ALU.max)
                        ins.then_inc(s_xs, 1)

            @block.scalar
            def _(act):
                act.sem_inc(s_xt, U)
                act.sem_inc(s_out, U)
                if keep_x:
                    act.sem_inc(s_keep, U)
                with act.Fori(0, TURNS) as i:
                    for j in range(U):
                        t = U * i + j
                        if keep_x:
                            act.wait_ge(s_xs, t + 1)
                            act.copy(m.XN[:, ds(t, 1), :], xs[:, j, :]).then_inc(s_keep, 1)
                        act.wait_ge(s_tr, U + t + 1)
                        act.wait_ge(s_mm, t + 1)
                        pt = p_turn(j).rearrange("p (k n) -> p k n", k=2)
                        if keep_xt:
                            act.copy(m.XT[:, :, ds(P * t, P)], pt)
                        act.copy(xt[:, j, :, :], pt).then_inc(s_xt, 1)
                    for j in range(U):
                        t = U * i + j
                        act.wait_ge(s_mm, U + t + 1)
                        if heads:
                            act.copy(m.EDU[:, ds(t, 1), 0:heads], m.ps[:, j, cols:full])
                        if heads == 1:
                            act.copy(m.ACC[:, ds(t, 1), D + 1:D + 2], m.ps[:, j, D:D + 1])
                            act.copy(m.ACC[:, ds(t, 1), 0:D], m.ps[:, j, 0:D]).then_inc(s_out, 1)
                        else:
                            act.copy(m.ACC[:, ds(t, 1), 0:cols], m.ps[:, j, 0:cols]).then_inc(s_out, 1)

            @block.tensor
            def _(pe):
                pe.sem_inc(s_tr, U)
                pe.sem_inc(s_mm, U)
                with pe.Fori(0, TURNS) as i:
                    for j in range(U):
                        t = U * i + j
                        pe.wait_ge(s_xs, t + 1)
                        pe.wait_ge(s_out, t + 1)
                        for k in range(2):
                            ins = pe.transpose(p_turn(j)[:, k * P:(k + 1) * P], xs[:, j, k * P:(k + 1) * P], m.ident[:])
                        ins.then_inc(s_tr, 1)
                    for j in range(U):
                        t = U * i + j
                        pe.wait_ge(s_xt, U + t + 1)
                        for k in range(2):
                            ins = pe.matmul(m.ps[:, j, 0:full], xt[:, j, k, :], w[:, k, 0:full],
                                            start=(k == 0), stop=(k == 1))
                        ins.then_inc(s_mm, 1)


def visit_turn(nc, eng, m, i):
    tiles = eng.value_load(m.tiles[0:1, ds(i, 1)], min_val=0, max_val=(1 << 25) - 1)
    blocks = eng.value_load(m.blocks[0:1, ds(i, 1)], min_val=0, max_val=(1 << 24) - 1)

    def part(packed, k, bits, top):
        return nc.s_assert_within(eng.snap(packed // (1 << bits * k) % (1 << bits)), 0, top,
                                  skip_runtime_bounds_check_because="packed from smaller values")

    return [part(tiles, k, 5, NONE) for k in range(5)], [part(blocks, k, 6, NBLK - 1) for k in range(4)]


def visit_turns(eng, m):
    total = eng.value_load(m.cum[0:1, LEAD + NBLK - 1:LEAD + NBLK], min_val=NBLK, max_val=NBLK * T)
    return eng.snap((total + 1) // 2)


def feed(sp, m, ix, s_ix, s_rows, s_ready, s_used, ahead, s_free, rows=None, s_rowsin=None, s_dready=None):
    def load(b, turn, q, waits=True):
        if waits:
            before = sp.value_load(m.cum[0:1, ds(b - DEPTH + LEAD, 1)], min_val=0, max_val=NBLK * T)
            sp.wait_ge(s_used, before + ahead)
            sp.sem_inc(s_free, 1)
        sp.dma_start(ix[:, q, :], m.src[:, ds(b, 1), :]).then_inc(s_ix[q], 16)
        if rows is not None:
            sp.dma_start(rows[:, q, :], m.drows[ds(b, 1), :].rearrange("o n -> (o n)").partition_broadcast(P)).then_inc(s_rowsin[q], 16)
            sp.wait_ge(s_rowsin[q], 16 * (turn + 1))
            sp.sem_inc(s_dready, 1)

    def passed(turn, q):
        sp.wait_ge(s_rows[q], 16 * B * (turn + 1))
        sp.sem_inc(s_ready, 1)

    for b in range(AHEAD):
        load(b, 0, b, waits=False)
    with sp.Fori(0, NBLK // DEPTH - 1) as i:
        for q in range(DEPTH):
            load(DEPTH * i + q + AHEAD, i + (q + AHEAD) // DEPTH, (q + AHEAD) % DEPTH)
            passed(i, q)
    for q in range(DEPTH):
        if q + AHEAD < DEPTH:
            load(NBLK - DEPTH + q + AHEAD, NBLK // DEPTH - 1, q + AHEAD)
        passed(NBLK // DEPTH - 1, q)


def gather_rows(pool, G, ix, table, s_ix, s_rows, s_turn):
    with pool.Fori(0, NBLK // DEPTH) as i:
        for q in range(DEPTH):
            pool.wait_ge(s_ix[q], 16 * (i + 1))
            pool.sem_inc(s_turn, 1)
            for j in range(B):
                pool.indirect_dma_start(
                    out=G[:, q, j, :], out_offset=None, in_=table[:, :],
                    in_offset=bass.IndirectOffsetOnAxis(ap=ix[:, q, j:j + 1], axis=0),
                ).then_inc(s_rows[q], 16)


def convolve(nc, m, name, table):
    with Phase(nc, name) as f:
        G = f.sb("G", [P, DEPTH, B, D])
        ix = f.sb("ix", [P, DEPTH, B], U32)
        dw = f.sb("dw", [P, 2, 2, B])
        S = f.sb("S", [P, 2, B, P])
        s_zero = f.sem("zero")
        s_ix = [f.sem(f"ix{q}") for q in range(DEPTH)]
        s_rows = [f.sem(f"rows{q}") for q in range(DEPTH)]
        s_ready = f.sem("ready")
        s_free = f.sem("free")
        s_turn = f.sem("turn")
        s_dw = f.sem("dw")
        s_S = f.sem("S")
        s_mm = f.sem("mm")
        s_add = f.sem("add")
        with nc.Block() as block:

            @block.sync
            def _(sp):
                feed(sp, m, ix, s_ix, s_rows, s_ready, s_mm, 1, s_free)

            @block.gpsimd
            def _(pool):
                gather_rows(pool, G, ix, table, s_ix, s_rows, s_turn)

            @block.vector
            def _(v):
                v.memset(m.ACC[:], 0.0).then_inc(s_zero, 1)
                v.wait_ge(s_zero, 1)
                v.sem_inc(s_add, 1)

                def place(n, p, t, b):
                    if n is not p:
                        v.wait_ge(s_mm, n)
                        v.wait_ge(s_S, n - 1)
                    v.tensor_copy(dw[:, p, :, :], m.dw[:, ds(b, 1), :, :].rearrange("p o a j -> p (o a) j")).then_inc(s_dw, 1)
                    v.wait_ge(s_dw, n + 1)
                    for j in range(B):
                        ins = v.tensor_scalar(S[:, p, j, :], m.iota[:, ds(P * t, P)], dw[:, p, 0, j:j + 1],
                                              dw[:, p, 1, j:j + 1], ALU.is_equal, ALU.mult)
                    ins.then_inc(s_S, 1)

                def add(n, p, t):
                    v.wait_ge(s_mm, n + 2)
                    v.wait_ge(s_add, n + 1)
                    v.tensor_tensor(m.ACCX[:, ds(t, 1), 0:D], m.ACCX[:, ds(t, 1), 0:D],
                                    m.ps[:, p:p + 1, 0:D], ALU.add).then_inc(s_add, 1)

                t, b = visit_turn(nc, v, m, 0)
                place(0, 0, t[1], b[0])
                place(1, 1, t[2], b[1])
                add(0, 0, t[1])
                turns = visit_turns(v, m)
                with v.Fori(1, turns) as i:
                    t, b = visit_turn(nc, v, m, i)
                    place(2 * i, 0, t[1], b[0])
                    add(2 * i - 1, 1, t[0])
                    place(2 * i + 1, 1, t[2], b[1])
                    add(2 * i, 0, t[1])
                t, b = visit_turn(nc, v, m, turns)
                add(2 * turns - 1, 1, t[0])

            @block.tensor
            def _(pe):
                pe.sem_inc(s_mm, 1)
                turns = visit_turns(pe, m)

                with pe.Fori(0, turns) as i:
                    t, b = visit_turn(nc, pe, m, i)
                    for p in range(2):
                        n = 2 * i + p
                        pe.wait_ge(s_ready, b[p] + 1)
                        pe.wait_ge(s_S, n + 1)
                        for j in range(B):
                            ins = pe.matmul(m.ps[:, p, 0:D], S[:, p, j, :], G[:, ds(b[p] % DEPTH, 1), j, :],
                                            start=(j == 0), stop=(j == B - 1))
                        ins.then_inc(s_mm, 1)


def self_loops(nc, m, name, hc, H, edu_table, loops, at=None):
    at = hc if at is None else at
    with Phase(nc, name) as f:
        es = f.sb("es", [P, T, H])
        top = f.sb("top", [P, H])
        tops = f.sb("tops", [P, H])
        sc = f.sb("sc", [P, T, H])
        left = f.sb("left", [P, T, 2 * H])
        s_v = f.sem("v")
        s_top = f.sem("top")
        s_tops = f.sem("tops")
        s_edu = f.sem("edu")
        s_sc = f.sem("sc")
        s_w = f.sem("w")
        s_dma = f.sem("dma")
        ed = m.EDU[:, :, 0:H]
        bound = m.EDU[:, :, H:2 * H]
        with nc.Block() as block:

            @block.vector
            def _(v):
                step = Steps(v, s_v)
                step(v.tensor_copy(es[:], m.ACC[:, :, at:at + H]))
                step(v.tensor_scalar(es[:, T - 1, :], es[:, T - 1, :], m.pen[:, 0:1], None, ALU.add))
                v.tensor_reduce(top[:], es[:].rearrange("p t h -> p h t"), X_, ALU.max).then_inc(s_top, 1)
                v.wait_ge(s_tops, 1)
                big = tops[:].rearrange("p (o h) -> p o h", o=1).broadcast_to([P, T, H])
                step(v.tensor_tensor(bound, ed, big, ALU.add))
                step(v.scalar_tensor_tensor(out=bound, in0=bound, scalar=SLOPE, in1=bound, op0=ALU.mult, op1=ALU.max))
                v.sem_inc(s_edu, 1)
                if edu_table is None:
                    rest = m.EDU[:, :, 0:2 * H]
                    step(v.tensor_copy(left[:], rest))
                    for k in range(3):
                        part = m.EDB[:, 0:T, 2 * H * k:2 * H * (k + 1)]
                        step(v.tensor_copy(part, left[:]))
                        if k < 2:
                            step(v.tensor_tensor(left[:], left[:], part, ALU.subtract))
                step(v.tensor_tensor(sc[:], m.ACC[:, :, at:at + H], ed, ALU.add))
                step(v.scalar_tensor_tensor(out=sc[:], in0=sc[:], scalar=SLOPE, in1=sc[:], op0=ALU.mult, op1=ALU.max))
                step(v.tensor_tensor(sc[:], sc[:], bound, ALU.subtract))
                step(v.tensor_scalar(sc[:], sc[:], 0.0, None, ALU.min))
                if loops < N:
                    k = loops // P
                    step(v.tensor_scalar(sc[:, k, :], sc[:, k, :], m.own[:, 0:1], None, ALU.add))
                    step(v.memset(sc[:, k + 1:T, :], NEG))
                v.sem_inc(s_sc, 1)
                v.wait_ge(s_w, 1)
                w4 = m.ACC[:, :, hc:hc + H].rearrange("p t (h o) -> p t h o", o=1).broadcast_to([P, T, H, hc // H])
                h4 = m.ACC[:, :, 0:hc].rearrange("p t (h c) -> p t h c", h=H)
                step(v.tensor_tensor(h4, h4, w4, ALU.mult))

            @block.gpsimd
            def _(pool):
                pool.wait_ge(s_top, 1)
                pool.partition_all_reduce(tops[:], top[:], P, bass.bass_isa.ReduceOp.max).then_inc(s_tops, 1)

            @block.scalar
            def _(act):
                act.wait_ge(s_sc, 1)
                act.activation(m.ACC[:, :, hc:hc + H], sc[:], ACT.Exp).then_inc(s_w, 1)

            @block.sync
            def _(sp):
                sp.wait_ge(s_edu, 1)
                if edu_table is None:
                    return
                sp.dma_start(edu_table.rearrange("(t p) c -> p t c", p=P), m.EDU[:, :, 0:2 * H]).then_inc(s_dma, 16)
                sp.wait_ge(s_dma, 16)


def edge_weights(v, act_sem, exp_sem, step, z, g_es, d_ed, d_bound):
    step(v.tensor_tensor(z, g_es, d_ed, ALU.add))
    step(v.scalar_tensor_tensor(out=z, in0=z, scalar=SLOPE, in1=z, op0=ALU.mult, op1=ALU.max))
    v.tensor_tensor(z, z, d_bound, ALU.subtract).then_inc(act_sem, 1)


def attend(nc, m, name, H, table):
    one = H == 1
    W = D + H
    ES = D + 1 if one else D
    C = D // H
    SHARE = 2
    with Phase(nc, name) as f:
        G = f.sb("G", [P, DEPTH, B, ES + H])
        ix = f.sb("ix", [P, DEPTH, B], U32)
        rows = f.sb("rows", [P, DEPTH, ROWE], U16)
        M = None if one else f.sb("M", [P, 2, B, W])
        dw = f.sb("dw", [P, 2, B])
        wt = f.sb("wt", [P, 2, B, H])
        S = f.sb("S", [P, 2, B, P])
        ST = f.sb("ST", [P, 2, B, P], BF16)
        tcol = f.sb("tcol", [P, T + 1])
        eb = f.sb("eb", [P, 2, B, 2 * H])
        z = f.sb("z", [P, 2, B, H])
        s_ix = [f.sem(f"ix{q}") for q in range(DEPTH)]
        s_rows = [f.sem(f"rows{q}") for q in range(DEPTH)]
        s_rowsin = [f.sem(f"rowsin{q}") for q in range(DEPTH)]
        s_dready = f.sem("dready")
        s_ready = f.sem("ready")
        s_free = f.sem("free")
        s_turn = f.sem("turn")
        s_col = f.sem("col")
        s_ST = f.sem("ST")
        s_ed = f.sem("ed")
        s_v = f.sem("v")
        s_z = f.sem("z")
        s_e = f.sem("e")
        s_w = f.sem("w")
        s_dw = f.sem("dw")
        s_S = f.sem("S")
        s_msg = f.sem("msg")
        s_mm = f.sem("mm")
        s_add = f.sem("add")
        with nc.Block() as block:

            @block.sync
            def _(sp):
                used, ahead = (s_mm, 2) if one else (s_msg, 1)
                feed(sp, m, ix, s_ix, s_rows, s_ready, used, ahead, s_free, rows, s_rowsin, s_dready)

            @block.gpsimd
            def _(pool):
                gather_rows(pool, G, ix, table, s_ix, s_rows, s_turn)

            @block.scalar
            def _(act):
                turns = visit_turns(act, m)
                with act.Fori(0, turns) as i:
                    if not one:
                        _, blk = visit_turn(nc, act, m, i)
                    for p in range(2):
                        n = 2 * i + p
                        act.wait_ge(s_z, n + 1)
                        act.wait_ge(s_mm, n + 1)
                        if one:
                            act.activation(wt[:, p, :, :], z[:, p, :, :], ACT.Exp).then_inc(s_w, 1)
                            continue
                        act.activation(wt[:, p, :, :], z[:, p, :, :], ACT.Exp).then_inc(s_e, 1)
                        act.wait_ge(s_e, n + 1)
                        act.copy(M[:, p, :, D:W], wt[:, p, :, :])
                        q = blk[p] % DEPTH
                        for j in range(SHARE):
                            for h in range(H):
                                ins = act.activation(M[:, p, j:j + 1, C * h:C * h + C], G[:, ds(q, 1), j, C * h:C * h + C],
                                                     ACT.Copy, scale=wt[:, p, j, h:h + 1])
                        ins.then_inc(s_w, 1)

            @block.vector
            def _(v):
                v.tensor_scalar(tcol[:], m.iota[:, 0:(T + 1) * P:P], m.pcol[:, 0:1], None, ALU.add).then_inc(s_col, 1)
                v.wait_ge(s_col, 1)
                if not one:
                    v.sem_inc(s_msg, 1)
                v.sem_inc(s_add, 1)

                def turned(n, p, t, b):
                    v.wait_ge(s_dready, b + 1)
                    v.tensor_scalar(ST[:, p, :, :].rearrange("p j e -> p (j e)"),
                                    rows[:, ds(b % DEPTH, 1), :].rearrange("p o e -> p (o e)"),
                                    tcol[:, ds(t, 1)], None, ALU.is_equal).then_inc(s_ST, 1)

                def score1(n, p):
                    v.wait_ge(s_ed, n + 1)
                    v.tensor_reduce(eb[:, p, :, :], m.ps[:, 2 + p, 0:B * 6 * H].rearrange("p (j k c) -> p j c k", j=B, k=3),
                                    X_, ALU.add).then_inc(s_v, 1)

                def score2(n, p, b):
                    v.wait_ge(s_v, 4 * n + 1)
                    v.wait_ge(s_ready, b + 1)
                    es = G[:, ds(b % DEPTH, 1), :, ES:ES + H].rearrange("p o j h -> p (o j) h")
                    v.tensor_tensor(z[:, p, :, :], es, eb[:, p, :, 0:H], ALU.add).then_inc(s_v, 1)

                def score3(n, p):
                    v.wait_ge(s_v, 4 * n + 2)
                    zp = z[:, p, :, :]
                    v.scalar_tensor_tensor(out=zp, in0=zp, scalar=SLOPE, in1=zp, op0=ALU.mult, op1=ALU.max).then_inc(s_v, 1)

                def score4(n, p):
                    v.wait_ge(s_v, 4 * n + 3)
                    zp = z[:, p, :, :]
                    v.tensor_tensor(zp, zp, eb[:, p, :, H:2 * H], ALU.subtract).then_inc(s_v, 1)

                def score5(n, p):
                    v.wait_ge(s_v, 4 * n + 4)
                    zp = z[:, p, :, :]
                    v.tensor_scalar(zp, zp, 0.0, None, ALU.min).then_inc(s_z, 1)

                def visit(n, p, t, b, b_next, t_after, b_after, t_last):
                    dst = m.dw[:, ds(b, 1), 0:1, :].rearrange("p o a j -> p (o a j)")
                    if one:
                        score1(n, p)
                        v.wait_ge(s_mm, n + 1)
                        v.tensor_copy(dw[:, p, :], dst).then_inc(s_dw, 1)
                        score2(n, p, b)
                        score3(n, p)
                        score4(n, p)
                        score5(n, p)
                        turned(n + 2, p, t_after, b_after)
                        v.wait_ge(s_dw, n + 1)
                        v.wait_ge(s_w, n + 1)
                        for j in range(B):
                            ins = v.tensor_scalar(S[:, p, j, :], m.iota[:, ds(P * t, P)], dw[:, p, j:j + 1],
                                                  wt[:, p, j, 0:1], ALU.is_equal, ALU.mult)
                        ins.then_inc(s_S, 1)
                        if t_last is not None:
                            add(n - 1, 1 - p, t_last)
                        return
                    score1(n + 1, 1 - p)
                    v.wait_ge(s_mm, n + 1)
                    io = m.iota[:, ds(P * t, P)].rearrange("p (o c) -> p o c", o=1).broadcast_to([P, B, P])
                    v.tensor_tensor(S[:, p, :, :], io, dup(dst, P), ALU.is_equal).then_inc(s_S, 1)
                    score2(n + 1, 1 - p, b_next)
                    turned(n + 2, p, t_after, b_after)
                    score3(n + 1, 1 - p)
                    v.wait_ge(s_w, n + 1)
                    R = B - SHARE
                    g4 = G[:, ds(b % DEPTH, 1), SHARE:B, 0:D].rearrange("p o j (h c) -> p (o j) h c", h=H)
                    m4 = M[:, p, SHARE:B, 0:D].rearrange("p j (h c) -> p j h c", h=H)
                    w4 = wt[:, p, SHARE:B, :].rearrange("p j (h o) -> p j h o", o=1).broadcast_to([P, R, H, C])
                    v.tensor_tensor(m4, g4, w4, ALU.mult).then_inc(s_msg, 1)
                    score4(n + 1, 1 - p)
                    if t_last is not None:
                        add(n - 1, 1 - p, t_last)
                    score5(n + 1, 1 - p)

                def add(n, p, t):
                    v.wait_ge(s_mm, n + 3)
                    v.wait_ge(s_add, n + 1)
                    v.tensor_tensor(m.ACCX[:, ds(t, 1), 0:W], m.ACCX[:, ds(t, 1), 0:W],
                                    m.ps[:, p:p + 1, 0:W], ALU.add).then_inc(s_add, 1)

                t, b = visit_turn(nc, v, m, 0)
                turned(0, 0, t[1], b[0])
                turned(1, 1, t[2], b[1])
                if not one:
                    score1(0, 0)
                    score2(0, 0, b[0])
                    score3(0, 0)
                    score4(0, 0)
                    score5(0, 0)
                visit(0, 0, t[1], b[0], b[1], t[3], b[2], None)
                visit(1, 1, t[2], b[1], b[2], t[4], b[3], t[1])
                turns = visit_turns(v, m)
                with v.Fori(1, turns) as i:
                    t, b = visit_turn(nc, v, m, i)
                    visit(2 * i, 0, t[1], b[0], b[1], t[3], b[2], t[0])
                    visit(2 * i + 1, 1, t[2], b[1], b[2], t[4], b[3], t[1])
                t, b = visit_turn(nc, v, m, turns)
                add(2 * turns - 1, 1, t[0])

            @block.tensor
            def _(pe):
                pe.sem_inc(s_mm, 2)

                def find(n, p, t):
                    pe.wait_ge(s_ST, n + 1)
                    if n is not p:
                        pe.wait_ge(s_v, 4 * n - 7)
                    for j in range(B):
                        ins = pe.matmul(m.ps[:, 2 + p, j * 6 * H:(j + 1) * 6 * H], ST[:, p, j, :],
                                        m.EDB[:, ds(t, 1), 0:6 * H], start=True, stop=True)
                    ins.then_inc(s_ed, 1)

                def sums(n, p, b):
                    pe.wait_ge(s_S, n + 1)
                    if not one:
                        pe.wait_ge(s_msg, n + 2)
                    if n is not p:
                        pe.wait_ge(s_add, n)
                    for j in range(B):
                        row = G[:, ds(b % DEPTH, 1), j, 0:W] if one else M[:, p, j, :]
                        ins = pe.matmul(m.ps[:, p, 0:W], S[:, p, j, :], row,
                                        start=(j == 0), stop=(j == B - 1))
                    ins.then_inc(s_mm, 1)

                t, b = visit_turn(nc, pe, m, 0)
                find(0, 0, t[1])
                find(1, 1, t[2])
                find(2, 0, t[3])
                sums(0, 0, b[0])
                find(3, 1, t[4])
                sums(1, 1, b[1])
                turns = visit_turns(pe, m)
                with pe.Fori(1, turns) as i:
                    t, b = visit_turn(nc, pe, m, i)
                    find(2 * i + 2, 0, t[3])
                    sums(2 * i, 0, b[0])
                    find(2 * i + 3, 1, t[4])
                    sums(2 * i + 1, 1, b[1])


def finish_attention(nc, m, name, H, bias_ap, to_x):
    with Phase(nc, name) as f:
        bias = f.sb("bias", [P, D])
        none = f.sb("none", [P, T, H])
        s_dma = f.sem("dma")
        s_v = f.sem("v")
        with nc.Block() as block:

            @block.sync
            def _(sp):
                sp.dma_start(bias[:], bias_ap.partition_broadcast(P)).then_inc(s_dma, 16)
                sp.wait_ge(s_dma, 16)

            @block.vector
            def _(v):
                step = Steps(v, s_v)
                den = m.ACC[:, :, D:D + H]
                a = m.ACC[:, :, 0:D]
                step(v.tensor_scalar(none[:], den, 0.0, None, ALU.is_equal))
                step(v.tensor_tensor(den, den, none[:], ALU.add))
                step(v.reciprocal(den, den))
                a4 = a.rearrange("p t (h c) -> p t h c", h=H)
                r4 = den.rearrange("p t (h o) -> p t h o", o=1).broadcast_to([P, T, H, D // H])
                step(v.tensor_tensor(a4, a4, r4, ALU.mult))
                v.wait_ge(s_dma, 16)
                step(v.tensor_tensor(a, a, bias[:].rearrange("p (o d) -> p o d", o=1).broadcast_to([P, T, D]), ALU.add))
                if to_x:
                    step(v.tensor_tensor(m.X[:], m.X[:], a, ALU.add))


def route(nc, m, A):
    with Phase(nc, "rt") as f:
        bias = f.sb("bias", [P, NEXP])
        L = f.sb("L", [P, T, NEXP])
        OH = f.sb("OH", [P, T, NEXP])
        tmp = f.sb("tmp", [P, T, NEXP])
        tot = f.sb("tot", [P, T, NEXP])
        top = f.sb("top", [P, T])
        node = f.sb("node", [P, T])
        pos = f.sb("pos", [P, T])
        ex = f.sb("ex", [P, T])
        kept = f.sb("kept", [P, T])
        a = f.sb("a", [P, T])
        idx = f.sb("idx", [P, T], U32)
        s_dma = f.sem("dma")
        s_v = f.sem("v")
        s_io = f.sem("io")
        s_l = f.sem("l")
        s_e = f.sem("e")
        s_oh = f.sem("oh")
        s_mm = f.sem("mm")
        s_idx = f.sem("idx")
        s_put = f.sem("put")
        with nc.Block() as block:

            @block.sync
            def _(sp):
                sp.dma_start(bias[:], A["L0_ffn_gate_b"].partition_broadcast(P)).then_inc(s_dma, 16)

            @block.gpsimd
            def _(pool):
                pool.iota(node[:], [[P, T]], base=NEXP * CAP, channel_multiplier=1,
                          allow_small_or_imprecise_dtypes=True).then_inc(s_io, 1)
                pool.wait_ge(s_idx, 1)
                for t in range(T):
                    pool.indirect_dma_start(
                        out=m.slots[:, :], out_offset=bass.IndirectOffsetOnAxis(ap=idx[:, t:t + 1], axis=0),
                        in_=m.XN[:, t, :], in_offset=None).then_inc(s_put, 16)
                pool.wait_ge(s_put, 16 * T)

            @block.scalar
            def _(act):
                act.wait_ge(s_l, 1)
                act.activation(tmp[:], L[:], ACT.Exp).then_inc(s_e, 1)

            @block.tensor
            def _(pe):
                pe.wait_ge(s_oh, 1)
                oh = OH[:].rearrange("p t e -> p (t e)")
                pe.matmul(m.ps[:, 0, 0:T * NEXP], m.upper[:], oh, start=True, stop=True).then_inc(s_mm, 1)
                pe.matmul(m.ps[:, 1, 0:T * NEXP], m.ones[:], oh, start=True, stop=True).then_inc(s_mm, 1)

            @block.vector
            def _(v):
                step = Steps(v, s_v)
                v.wait_ge(s_dma, 16)
                eb = [P, T, NEXP]
                step(v.tensor_tensor(L[:], m.ACC[:, :, 0:NEXP],
                                     bias[:].rearrange("p (o e) -> p o e", o=1).broadcast_to(eb), ALU.add))
                step(v.tensor_reduce(top[:], L[:], X_, ALU.max))
                step(v.tensor_tensor(OH[:], L[:], dup(top[:], NEXP), ALU.is_equal))
                io8 = m.iota[:, 0:NEXP].rearrange("p (o e) -> p o e", o=1).broadcast_to(eb)
                step(v.scalar_tensor_tensor(out=OH[:], in0=OH[:], scalar=-float(NEXP), in1=io8, op0=ALU.mult, op1=ALU.add))
                step(v.tensor_reduce(ex[:], OH[:], X_, ALU.min))
                step(v.tensor_tensor(OH[:], OH[:], dup(ex[:], NEXP), ALU.is_equal))
                v.sem_inc(s_oh, 1)
                step(v.tensor_scalar(ex[:], ex[:], float(NEXP), None, ALU.add))
                step(v.tensor_tensor(L[:], L[:], dup(top[:], NEXP), ALU.subtract))
                v.sem_inc(s_l, 1)
                v.wait_ge(s_e, 1)
                step(v.tensor_reduce(a[:], tmp[:], X_, ALU.add))
                step(v.reciprocal(m.gscale[:], a[:]))
                v.wait_ge(s_mm, 2)
                p0 = m.ps[:, 0, 0:T * NEXP].rearrange("p (t e) -> p t e", e=NEXP)
                p1 = m.ps[:, 1, 0:T * NEXP].rearrange("p (t e) -> p t e", e=NEXP)
                step(v.tensor_copy(tot[:], p1))
                for e in range(NEXP):
                    ins = v.tensor_tensor_scan(tmp[:, :, e], m.ones[:, 0:T], tot[:, :, e], 0.0, ALU.mult, ALU.add)
                step(ins)
                step(v.tensor_tensor(tmp[:], tmp[:], tot[:], ALU.subtract))
                step(v.tensor_tensor(tmp[:], tmp[:], p0, ALU.add))
                step(v.tensor_tensor(tmp[:], tmp[:], OH[:], ALU.mult))
                step(v.tensor_reduce(pos[:], tmp[:], X_, ALU.add))
                step(v.tensor_scalar(kept[:], pos[:], float(CAP), None, ALU.is_le))
                step(v.tensor_tensor(m.gscale[:], m.gscale[:], kept[:], ALU.mult))
                step(v.tensor_scalar(ex[:], ex[:], float(CAP), -1.0, ALU.mult, ALU.add))
                step(v.scalar_tensor_tensor(out=a[:], in0=pos[:], scalar=float(CAP), in1=ex[:], op0=ALU.min, op1=ALU.add))
                step(v.tensor_copy(m.gidx[:], a[:]))
                v.wait_ge(s_io, 1)
                step(v.tensor_tensor(a[:], a[:], node[:], ALU.subtract))
                step(v.tensor_tensor(a[:], a[:], kept[:], ALU.mult))
                step(v.tensor_tensor(a[:], a[:], node[:], ALU.add))
                v.tensor_copy(idx[:], a[:]).then_inc(s_idx, 1)


def experts(nc, m, A):
    FT = HID // P
    with Phase(nc, "ex") as f:
        w1 = f.sb("w1", [P, 2, 2, HID])
        w2 = f.sb("w2", [P, 2, FT, D])
        xin = f.sb("xin", [P, 2, 4, D])
        xt = f.sb("xt", [P, 2, 512])
        b2 = f.sb("b2", [P, NEXP * D])
        b1r = f.sb("b1r", [NEXP * FT, P])
        b1 = f.sb("b1", [P, NEXP * FT])
        Y = f.sb("Y", [P, 2, 4, D])
        hid = m.ACCX[:].rearrange("p t c -> p (t c)")[:, 0:FT * 512].rearrange("p (f n) -> p f n", f=FT)
        s_b = f.sem("b")
        s_bt = f.sem("bt")
        s_bc = f.sem("bc")
        s_in = [f.sem(f"in{q}") for q in range(2)]
        s_done = f.sem("done")
        s_tr = f.sem("tr")
        s_xt = f.sem("xt")
        s_up = f.sem("up")
        s_h = f.sem("h")
        s_dn = f.sem("dn")
        s_y = f.sem("y")
        s_turn = f.sem("turn")
        s_st = [f.sem(f"st{q}") for q in range(2)]
        last = CAP - 3 * P
        with nc.Block() as block:

            @block.sync
            def _(sp):
                sp.dma_start(b2[:], A["L0_ffn_b2"].rearrange("e d -> (e d)").partition_broadcast(P)).then_inc(s_b, 16)
                sp.dma_start(b1r[:], A["L0_ffn_b1"].rearrange("e (f p) -> (e f) p", p=P)).then_inc(s_b, 16)
                with sp.Fori(0, NEXP // 2) as i:
                    for q in range(2):
                        e = 2 * i + q
                        sp.wait_ge(s_done, e + 1)
                        sp.sem_inc(s_turn, 1)
                        sp.dma_start(xin[:, q, :, :], m.slots[ds(CAP * e, 4 * P), :].rearrange("(s p) d -> p s d", p=P)).then_inc(s_in[q], 16)
                        sp.dma_start(w1[:, q, :, :], A["L0_ffn_w1"].rearrange("e (k p) f -> p e k f", p=P)[:, ds(e, 1), :, :].rearrange("p o k f -> p (o k) f")).then_inc(s_in[q], 16)
                        sp.dma_start(w2[:, q, :, :], A["L0_ffn_w2"].rearrange("e (k p) f -> p e k f", p=P)[:, ds(e, 1), :, :].rearrange("p o k f -> p (o k) f")).then_inc(s_in[q], 16)

            @block.gpsimd
            def _(pool):
                with pool.Fori(0, NEXP // 2) as i:
                    for q in range(2):
                        e = 2 * i + q
                        pool.wait_ge(s_y, 4 * e + 4)
                        pool.sem_inc(s_turn, 1)
                        pool.dma_start(m.yslots[ds(CAP * e, 3 * P), :].rearrange("(s p) d -> p s d", p=P), Y[:, q, 0:3, :]).then_inc(s_st[q], 16)
                        pool.dma_start(m.yslots[ds(CAP * e + 3 * P, last), :], Y[0:last, q, 3, :]).then_inc(s_st[q], 16)
                for q in range(2):
                    pool.wait_ge(s_st[q], 32 * (NEXP // 2))

            @block.tensor
            def _(pe):
                pe.wait_ge(s_b, 32)
                pe.transpose(m.ps[:, 7, 0:NEXP * FT], b1r[:], m.ident[0:NEXP * FT, 0:NEXP * FT]).then_inc(s_bt, 1)
                pe.sem_inc(s_done, 2)
                pe.sem_inc(s_up, 2)
                with pe.Fori(0, NEXP // 2) as i:
                    for q in range(2):
                        e = 2 * i + q
                        pe.wait_ge(s_in[q], 48 * (i + 1))
                        pe.wait_ge(s_xt, 2 * e)
                        for k in range(2):
                            for s in range(4):
                                ins = pe.transpose(m.ps[:, k, s * P:(s + 1) * P], xin[:, q, s, k * P:(k + 1) * P], m.ident[:])
                            ins.then_inc(s_tr, 1)
                        pe.wait_ge(s_xt, 2 * e + 2)
                        for g in range(FT):
                            pe.wait_ge(s_h, FT * e + g + 1)
                            for k in range(2):
                                ins = pe.matmul(m.ps[:, 2 + g % 2, :], w1[:, q, k, g * P:(g + 1) * P], xt[:, k, :],
                                                start=(k == 0), stop=(k == 1))
                            ins.then_inc(s_up, 1)
                        pe.wait_ge(s_h, FT * e + FT + 2)
                        for s in range(4):
                            pe.wait_ge(s_y, 4 * e + s)
                            for g in range(FT):
                                ins = pe.matmul(m.ps[:, 4 + s, 0:D], hid[:, g, s * P:(s + 1) * P], w2[:, q, g, :],
                                                start=(g == 0), stop=(g == FT - 1))
                            ins.then_inc(s_dn, 1)
                        pe.drain().then_inc(s_done, 1)

            @block.scalar
            def _(act):
                act.wait_ge(s_bt, 1)
                act.copy(b1[:], m.ps[:, 7, 0:NEXP * FT]).then_inc(s_bc, 1)
                act.wait_ge(s_bc, 1)
                act.sem_inc(s_h, 2)
                with act.Fori(0, NEXP // 2) as i:
                    for q in range(2):
                        e = 2 * i + q
                        for k in range(2):
                            act.wait_ge(s_tr, 2 * e + k + 1)
                            act.copy(xt[:, k, :], m.ps[:, k, :]).then_inc(s_xt, 1)
                        for g in range(FT):
                            act.wait_ge(s_up, FT * e + g + 3)
                            act.activation(hid[:, g, :], m.ps[:, 2 + g % 2, :], ACT.Relu,
                                           bias=b1[:, ds(FT * e + g, 1)]).then_inc(s_h, 1)

            @block.vector
            def _(v):
                v.wait_ge(s_b, 32)
                with v.Fori(0, NEXP // 2) as i:
                    for q in range(2):
                        e = 2 * i + q
                        v.wait_ge(s_st[q], 32 * i)
                        for s in range(4):
                            v.wait_ge(s_dn, 4 * e + s + 1)
                            v.tensor_tensor(Y[:, q, s, :], m.ps[:, 4 + s, 0:D], b2[:, ds(D * e, D)], ALU.add).then_inc(s_y, 1)


def combine(nc, m):
    with Phase(nc, "cb") as f:
        r = f.sb("r", [P, U, D])
        r2 = f.sb("r2", [P, U, D])
        fin = f.sb("fin", [P, U, D], I32)
        s_g = [f.sem(f"g{k}") for k in range(TURNS)]
        s_v = f.sem("v")
        with nc.Block() as block:

            @block.gpsimd
            def _(pool):
                for t in range(T):
                    pool.indirect_dma_start(
                        out=m.ACC[:, t, 0:D], out_offset=None, in_=m.yslots[:, :],
                        in_offset=bass.IndirectOffsetOnAxis(ap=m.gidx[:, t:t + 1], axis=0)).then_inc(s_g[t // U], 16)

            @block.vector
            def _(v):
                step = Steps(v, s_v)
                for k in range(TURNS):
                    v.wait_ge(s_g[k], 16 * U)
                    y = m.ACC[:, U * k:U * k + U, 0:D]
                    v.tensor_scalar(r[:], y, FMAX, 1.0e4, ALU.is_gt, ALU.mult)
                    v.tensor_scalar(r2[:], y, -FMAX, -1.0e4, ALU.is_lt, ALU.mult)
                    step(v.tensor_scalar(fin[:], y, 0.0, 0.0, ALU.mult, ALU.is_equal))
                    step(v.tensor_tensor(r[:], r[:], r2[:], ALU.add))
                    step(v.copy_predicated(r[:], fin[:], y))
                    for j in range(U):
                        t = U * k + j
                        ins = v.scalar_tensor_tensor(out=m.X[:, t, :], in0=r[:, j, :], scalar=m.gscale[:, t:t + 1],
                                                     in1=m.X[:, t, :], op0=ALU.mult, op1=ALU.add)
                    step(ins)


def gate_attend_and_experts(nc, m, A):
    H, HC = GH, 16
    W = HC + H
    RING = 4
    FT = HID2 // P
    CW = U * P
    HW = CW // 2
    NU = 2 * FT
    assert FNBLK == TURNS * KEXP and KEXP % 2 == 0
    with Phase(nc, "ga") as f:
        G = f.sb("G", [P, 2, FB, W])
        DD = f.sb("DD", [P, 2, FB, 2 * H])
        z = f.sb("z", [P, FB, H])
        ixs = f.sb("ixs", [P, 2, FB], U32)
        ixd = f.sb("ixd", [P, 2, FB], U32)
        lo = f.sb("lo", [P, 2, FB])
        hi = f.sb("hi", [P, 2, FB])
        S = f.sb("S", [P, FB, P])
        hot = f.sb("hot", [P, FB, T])
        R = f.sb("R", [P, RING, T, W])
        zz = f.sb("zz", [P, T * W])
        w1 = f.sb("w1", [P, KEXP, 2, HID2])
        w2 = f.sb("w2", [P, KEXP, FT, D])
        b2 = f.sb("b2", [P, KEXP, D])
        b1r = f.sb("b1r", [KEXP * FT, P])
        b1 = f.sb("b1", [P, KEXP * FT])
        hid = f.sb("hid", [P, 2, FT, CW])
        y = f.sb("y", [P, 2, U, D])
        s_stage = f.sem("stage")
        s_rows = [f.sem(f"rows{q}") for q in range(2)]
        s_z = f.sem("z")
        s_w = f.sem("w")
        s_m = f.sem("m")
        s_S = f.sem("S")
        s_R = f.sem("R")
        s_mm = f.sem("mm")
        s_turn = f.sem("turn")
        s_v = f.sem("v")
        s_zero = f.sem("zero")
        s_end = f.sem("end")
        s_in = f.sem("in")
        s_bt = f.sem("bt")
        s_bc = f.sem("bc")
        s_up = f.sem("up")
        s_h = f.sem("h")
        s_dn = f.sem("dn")
        s_y = f.sem("y")
        s_st = [f.sem(f"st{q}") for q in range(2)]
        with nc.Block() as block:

            @block.sync
            def _(sp):
                sp.dma_start(b1r[:], A["L1_ffn_b1"].rearrange("e (f p) -> (e f) p", p=P)).then_inc(s_in, 16)
                for e in range(KEXP):
                    sp.dma_start(w1[:, e, :, :], A["L1_ffn_W1"][e].rearrange("(k p) n -> p k n", p=P)).then_inc(s_in, 16)
                    sp.dma_start(w2[:, e, :, :], A["L1_ffn_W2"][e].rearrange("(k p) n -> p k n", p=P)).then_inc(s_in, 16)
                    sp.dma_start(b2[:, e, :], A["L1_ffn_b2"][e].partition_broadcast(P)).then_inc(s_in, 16)
                with sp.Fori(0, TURNS) as i:
                    for e in range(KEXP):
                        n = KEXP * i + e
                        sp.wait_ge(s_y, U * n + 2 * U)
                        sp.sem_inc(s_turn, 1)
                        sp.dma_start(m.ymix[e][ds(CW * i, CW), :].rearrange("(t p) d -> p t d", p=P),
                                     y[:, e % 2, :, :]).then_inc(s_st[e % 2], 16)
                for q in range(2):
                    sp.wait_ge(s_st[q], 16 * (FNBLK // 2))

            @block.scalar
            def _(act):
                def stage(b, q):
                    act.wait_ge(s_mm, FB * b + FB)
                    act.copy(ixs[:, q, :], m.fsrc[:, :, ds(b, 1)]).then_inc(s_stage, 1)
                    act.copy(ixd[:, q, :], m.fdst[:, :, ds(b, 1)]).then_inc(s_stage, 1)
                    act.copy(lo[:, q, :], m.flo[:, :, ds(b, 1)]).then_inc(s_stage, 1)
                    act.copy(hi[:, q, :], m.fhi[:, :, ds(b, 1)]).then_inc(s_stage, 1)

                def first_layer(n, e):
                    for k in range(NU):
                        act.wait_ge(s_up, NU * n + k + 3)
                        g_, hf = k // 2, k % 2
                        act.activation(hid[:, e % 2, g_, hf * HW:(hf + 1) * HW], m.ps[:, 1 + k % 2, 0:HW], ACT.Gelu,
                                       bias=b1[:, FT * e + g_:FT * e + g_ + 1]).then_inc(s_h, 1)

                def weights(b, q):
                    act.wait_ge(s_z, b + 1)
                    act.activation(G[:, q, :, HC:W], z[:], ACT.Exp).then_inc(s_w, 1)

                stage(0, 0)
                stage(1, 1)
                act.wait_ge(s_bt, 1)
                act.copy(b1[:], m.ps[:, 7, 0:KEXP * FT]).then_inc(s_bc, 1)
                act.wait_ge(s_bc, 1)
                act.sem_inc(s_h, 2)
                with act.Fori(0, TURNS - 1) as i:
                    for e in range(KEXP):
                        n = KEXP * i + e
                        first_layer(n, e)
                        weights(n, e % 2)
                        stage(n + 2, e % 2)
                for e in range(KEXP):
                    n = KEXP * (TURNS - 1) + e
                    first_layer(n, e)
                    weights(n, e % 2)
                    if n + 2 < FNBLK:
                        stage(n + 2, e % 2)

            @block.gpsimd
            def _(pool):
                with pool.Fori(0, FNBLK // 2) as i:
                    for q in range(2):
                        pool.wait_ge(s_stage, 4 * (2 * i + q) + 4)
                        pool.sem_inc(s_turn, 1)
                        for j in range(FB):
                            pool.indirect_dma_start(
                                out=G[:, q, j, :], out_offset=None, in_=m.gtable[:, :],
                                in_offset=bass.IndirectOffsetOnAxis(ap=ixs[:, q, j:j + 1], axis=0),
                            ).then_inc(s_rows[q], 16)
                            pool.indirect_dma_start(
                                out=DD[:, q, j, :], out_offset=None, in_=m.gedu[:, :],
                                in_offset=bass.IndirectOffsetOnAxis(ap=ixd[:, q, j:j + 1], axis=0),
                            ).then_inc(s_rows[q], 16)

            @block.vector
            def _(v):
                v.memset(zz[:], 0.0).then_inc(s_zero, 1)
                v.sem_inc(s_y, U)

                def edges(b, q, turn):
                    v.wait_ge(s_stage, 4 * b + 4)
                    v.wait_ge(s_mm, FB * b + 2 * FB)
                    io = m.iota[:, 0:P].rearrange("p (o c) -> p o c", o=1).broadcast_to([P, FB, P])
                    v.tensor_tensor(S[:], io, dup(lo[:, q, :], P), ALU.is_equal).then_inc(s_S, 1)
                    io = m.iota[:, 0:T].rearrange("p (o c) -> p o c", o=1).broadcast_to([P, FB, T])
                    v.tensor_tensor(hot[:], io, dup(hi[:, q, :], T), ALU.is_equal).then_inc(s_S, 1)
                    v.wait_ge(s_rows[q], 32 * FB * (turn + 1))
                    edge_weights(v, s_z, s_w, Steps(v, s_v, 2 * b), z[:], G[:, q, :, HC:W],
                                 DD[:, q, :, 0:H], DD[:, q, :, H:2 * H])
                    v.wait_ge(s_w, b + 1)
                    g4 = G[:, q, :, 0:HC].rearrange("p j (h c) -> p j h c", h=H)
                    w4 = G[:, q, :, HC:W].rearrange("p j (h o) -> p j h o", o=1).broadcast_to([P, FB, H, HC // H])
                    v.tensor_tensor(g4, g4, w4, ALU.mult).then_inc(s_m, 1)
                    v.wait_ge(s_m, b + 1)
                    v.wait_ge(s_S, 2 * b + 2)
                    for j in range(FB):
                        if j >= RING:
                            v.wait_ge(s_mm, FB * b + 2 * FB + j - RING + 1)
                        val = G[:, q, j:j + 1, :].broadcast_to([P, T, W])
                        v.tensor_tensor(R[:, j % RING, :, :], dup(hot[:, j, :], W), val, ALU.mult).then_inc(s_R, 1)

                def second_layer(n, e, turn):
                    if e >= 2:
                        v.wait_ge(s_st[e % 2], 16 * (2 * turn + 1))
                    else:
                        v.wait_ge(s_st[e % 2], 32 * turn)
                    for j in range(U):
                        v.wait_ge(s_dn, U * n + j + 1)
                        v.tensor_tensor(y[:, e % 2, j, :], m.ps[:, 3 + j, 0:D], b2[:, e, :], ALU.add).then_inc(s_y, 1)

                v.wait_ge(s_in, 16 * (1 + 3 * KEXP))
                v.wait_ge(s_bc, 1)
                with v.Fori(0, TURNS) as i:
                    for e in range(KEXP):
                        n = KEXP * i + e
                        edges(n, e % 2, 2 * i + e // 2)
                        second_layer(n, e, i)

            @block.tensor
            def _(pe):
                pe.sem_inc(s_mm, 2 * FB)
                pe.sem_inc(s_up, 2)
                pe.wait_ge(s_zero, 1)
                pe.matmul(m.ps[:, 0, 0:T * W], zz[:, 0:P], zz[:], start=True, stop=False)
                pe.wait_ge(s_in, 16 * (1 + 3 * KEXP))
                pe.transpose(m.ps[:, 7, 0:KEXP * FT], b1r[:], m.ident[0:KEXP * FT, 0:KEXP * FT]).then_inc(s_bt, 1)
                with pe.Fori(0, TURNS) as i:
                    for e in range(KEXP):
                        n = KEXP * i + e
                        for k_ in range(NU):
                            g_, hf = k_ // 2, k_ % 2
                            pe.wait_ge(s_h, NU * n + k_ + 1)
                            for k in range(2):
                                ins = pe.matmul(m.ps[:, 1 + k_ % 2, 0:HW], w1[:, e, k, g_ * P:(g_ + 1) * P],
                                                m.XT[:, k, ds(CW * i + HW * hf, HW)], start=(k == 0), stop=(k == 1))
                            ins.then_inc(s_up, 1)
                        for j in range(FB):
                            pe.wait_ge(s_R, FB * n + j + 1)
                            pe.matmul(m.ps[:, 0, 0:T * W], S[:, j, :], R[:, j % RING, :, :].rearrange("p t w -> p (t w)"),
                                      start=False, stop=False).then_inc(s_mm, 1)
                        pe.wait_ge(s_h, NU * n + NU + 2)
                        for j in range(U):
                            pe.wait_ge(s_y, U * n + j + 1)
                            for g_ in range(FT):
                                ins = pe.matmul(m.ps[:, 3 + j, 0:D], hid[:, e % 2, g_, j * P:(j + 1) * P], w2[:, e, g_, :],
                                                start=(g_ == 0), stop=(g_ == FT - 1))
                            ins.then_inc(s_dn, 1)
                pe.matmul(m.ps[:, 0, 0:T * W], zz[:, 0:P], zz[:], start=False, stop=True).then_inc(s_end, 1)
        with nc.Block() as block:

            @block.vector
            def _(v):
                a = m.ACC[:, :, 0:W]
                v.tensor_tensor(a, a, m.ps[:, 0, 0:T * W].rearrange("p (t w) -> p t w", w=W), ALU.add).then_inc(s_v, 1)


def gates(nc, m, A):
    C = 16
    with Phase(nc, "gt") as f:
        vec = f.sb("vec", [P, 3, C])
        a = f.sb("a", [P, T, C])
        b = f.sb("b", [P, T, C])
        mu = f.sb("mu", [P, T])
        sd = f.sb("sd", [P, T])
        den = f.sb("den", [P, T, GH])
        sc = f.sb("sc", [P, T, KEXP])
        o1 = f.sb("o1", [P, T, KEXP])
        o2 = f.sb("o2", [P, T, KEXP])
        m1 = f.sb("m1", [P, T])
        m2 = f.sb("m2", [P, T])
        k1 = f.sb("k1", [P, T])
        s_dma = f.sem("dma")
        s_v = f.sem("v")
        s_var = f.sem("var")
        s_sd = f.sem("sd")
        s_d = f.sem("d")
        s_e = f.sem("e")
        with nc.Block() as block:

            @block.sync
            def _(sp):
                for k, name in enumerate(("L1_ffn_b_gat", "L1_ffn_ln_gamma", "L1_ffn_ln_beta")):
                    sp.dma_start(vec[:, k, :], A[name].partition_broadcast(P)).then_inc(s_dma, 16)

            @block.scalar
            def _(act):
                act.wait_ge(s_var, 1)
                act.activation(sd[:], sd[:], ACT.Sqrt).then_inc(s_sd, 1)
                act.wait_ge(s_d, 1)
                act.activation(m2[:], m2[:], ACT.Exp).then_inc(s_e, 1)

            @block.vector
            def _(v):
                step = Steps(v, s_v)

                def row(k):
                    return vec[:, k:k + 1, :].broadcast_to([P, T, C])

                step(v.tensor_scalar(den[:], m.ACC[:, :, C:C + GH], 1e-16, None, ALU.add))
                step(v.reciprocal(den[:], den[:]))
                step(v.tensor_tensor(a[:].rearrange("p t (h c) -> p t h c", h=GH),
                                     m.ACC[:, :, 0:C].rearrange("p t (h c) -> p t h c", h=GH),
                                     den[:].rearrange("p t (h o) -> p t h o", o=1).broadcast_to([P, T, GH, C // GH]), ALU.mult))
                v.wait_ge(s_dma, 48)
                step(v.tensor_tensor(a[:], a[:], row(0), ALU.add))
                step(v.tensor_reduce(mu[:], a[:], X_, ALU.add))
                step(v.tensor_scalar(mu[:], mu[:], 1.0 / C, None, ALU.mult))
                step(v.tensor_tensor(a[:], a[:], dup(mu[:], C), ALU.subtract))
                step(v.tensor_tensor(b[:], a[:], a[:], ALU.mult))
                step(v.tensor_reduce(sd[:], b[:], X_, ALU.add))
                step(v.tensor_scalar(sd[:], sd[:], 1.0 / C, EPS, ALU.mult, ALU.add))
                v.sem_inc(s_var, 1)
                v.wait_ge(s_sd, 1)
                step(v.reciprocal(sd[:], sd[:]))
                step(v.tensor_tensor(a[:], a[:], dup(sd[:], C), ALU.mult))
                step(v.tensor_tensor(a[:], a[:], row(1), ALU.mult))
                step(v.tensor_tensor(a[:], a[:], row(2), ALU.add))
                step(v.tensor_reduce(sc[:], a[:].rearrange("p t (h e) -> p t e h", h=GH), X_, ALU.add))
                step(v.tensor_scalar(sc[:], sc[:], 1.0 / GH, None, ALU.mult))
                io4 = m.iota[:, 0:KEXP].rearrange("p (o e) -> p o e", o=1).broadcast_to([P, T, KEXP])

                def first_best(o, best):
                    step(v.tensor_reduce(best[:], sc[:], X_, ALU.max))
                    step(v.tensor_tensor(o[:], sc[:], dup(best[:], KEXP), ALU.is_equal))
                    step(v.scalar_tensor_tensor(out=o[:], in0=o[:], scalar=-float(KEXP), in1=io4, op0=ALU.mult, op1=ALU.add))
                    step(v.tensor_reduce(k1[:], o[:], X_, ALU.min))
                    step(v.tensor_tensor(o[:], o[:], dup(k1[:], KEXP), ALU.is_equal))

                first_best(o1, m1)
                step(v.scalar_tensor_tensor(out=sc[:], in0=o1[:], scalar=NEG, in1=sc[:], op0=ALU.mult, op1=ALU.add))
                first_best(o2, m2)
                step(v.tensor_tensor(m2[:], m2[:], m1[:], ALU.subtract))
                v.sem_inc(s_d, 1)
                v.wait_ge(s_e, 1)
                step(v.tensor_scalar(m1[:], m2[:], 1.0, None, ALU.add))
                step(v.reciprocal(m1[:], m1[:]))
                step(v.tensor_tensor(m2[:], m2[:], m1[:], ALU.mult))
                step(v.tensor_tensor(o1[:], o1[:], dup(m1[:], KEXP), ALU.mult))
                step(v.tensor_tensor(o2[:], o2[:], dup(m2[:], KEXP), ALU.mult))
                step(v.tensor_tensor(m.gate[:], o1[:], o2[:], ALU.add))


def mix_experts(nc, m, out):
    CW = U * P
    with Phase(nc, "mx") as f:
        y = f.sb("y", [P, 2, KEXP, U, D])
        s_in = [f.sem(f"in{q}") for q in range(2)]
        s_x = f.sem("x")
        s_out = f.sem("out")
        with nc.Block() as block:

            @block.scalar
            def _(act):
                for i in range(TURNS):
                    if i >= 2:
                        act.wait_ge(s_x, KEXP * U * (i - 1))
                    for e in range(KEXP):
                        act.dma_start(y[:, i % 2, e, :, :], m.ymix[e][CW * i:CW * (i + 1), :].rearrange("(t p) d -> p t d", p=P)).then_inc(s_in[i % 2], 16)

            @block.vector
            def _(v):
                for i in range(TURNS):
                    v.wait_ge(s_in[i % 2], 16 * KEXP * (i // 2 + 1))
                    for e in range(KEXP):
                        for j in range(U):
                            t = U * i + j
                            if e:
                                v.wait_ge(s_x, KEXP * U * i + U * (e - 1) + j + 1)
                            v.scalar_tensor_tensor(out=m.X[:, t, :], in0=y[:, i % 2, e, j, :], scalar=m.gate[:, t, e:e + 1],
                                                   in1=m.X[:, t, :], op0=ALU.mult, op1=ALU.add).then_inc(s_x, 1)

            @block.sync
            def _(sp):
                for i in range(TURNS - 1):
                    sp.wait_ge(s_x, KEXP * U * (i + 1))
                    sp.dma_start(out[CW * i:CW * (i + 1), :].rearrange("(t p) d -> p t d", p=P), m.X[:, U * i:U * (i + 1), :]).then_inc(s_out, 16)
                sp.wait_ge(s_x, KEXP * T)
                sp.dma_start(out[(TURNS - 1) * CW:(T - 1) * P, :].rearrange("(t p) d -> p t d", p=P), m.X[:, (TURNS - 1) * U:T - 1, :]).then_inc(s_out, 16)
                sp.dma_start(out[(T - 1) * P:N, :], m.X[0:TAIL, T - 1, :]).then_inc(s_out, 16)
                sp.wait_ge(s_out, 16 * (TURNS + 1))


def add_to_x(nc, m, name):
    with Phase(nc, name) as f:
        s = f.sem("s")
        with nc.Block() as block:

            @block.vector
            def _(v):
                v.tensor_tensor(m.X[:], m.X[:], m.ACC[:, :, 0:D], ALU.add).then_inc(s, 1)


def load_rows(nc, m, name, aps):
    with Phase(nc, name) as f:
        s = f.sem("s")
        with nc.Block() as block:

            @block.sync
            def _(sp):
                for k, ap in enumerate(aps):
                    sp.dma_start(m.vec[:, k, :], ap.partition_broadcast(P)).then_inc(s, 16)
                sp.wait_ge(s, 16 * len(aps))


def store_x(nc, m, out):
    with Phase(nc, "end") as f:
        s = f.sem("s")
        with nc.Block() as block:

            @block.sync
            def _(sp):
                sp.dma_start(out[0:(T - 1) * P, :].rearrange("(t p) d -> p t d", p=P), m.X[:, 0:T - 1, :]).then_inc(s, 16)
                sp.dma_start(out[(T - 1) * P:N, :], m.X[0:TAIL, T - 1, :]).then_inc(s, 16)
                sp.wait_ge(s, 32)


def program(nc, A, out, upto=99):
    ctx = ExitStack()
    m = Memory()
    m.support = [nc.dram_tensor(f"support{k}", (NP_, D), F32).ap() for k in range(2)]
    m.drows = nc.dram_tensor("drows", (NBLK, ROWE), U16).ap()
    m.slots = nc.dram_tensor("slots", (NEXP * CAP + NP_, D), F32).ap()
    m.yslots = nc.dram_tensor("yslots", (NEXP * CAP, D), F32).ap()
    m.atable = [nc.dram_tensor(f"atable{k}", (NP_, D + h), F32).ap() for k, h in ((0, 4), (1, 2))]
    m.ymix = nc.dram_tensor("ymix", (KEXP, NP_, D), F32).ap()
    m.gtable = nc.dram_tensor("gtable", (NP_, 20), F32).ap()
    m.gedu = nc.dram_tensor("gedu", (NP_, 8), F32).ap()
    with ctx:
        alloc(nc, ctx, m)
        prepare(nc, m, A)
        row_moments(nc, m, "m0", m.X)
        project(nc, m, "p0", "ln", m.W["c1"], D, table=m.support[0])
        convolve(nc, m, "c0", m.support[0])
        project(nc, m, "p1", "acc", m.W["c2"], D, table=m.support[1])
        convolve(nc, m, "c1", m.support[1])
        add_to_x(nc, m, "a1")
        if upto == 1:
            return store_x(nc, m, out)
        row_moments(nc, m, "m1", m.X)
        project(nc, m, "route", "ln", m.W["gate"], NEXP)
        route(nc, m, A)
        experts(nc, m, A)
        combine(nc, m)
        if upto == 2:
            return store_x(nc, m, out)
        row_moments(nc, m, "m2", m.X)
        load_rows(nc, m, "lv", (A["L1_gnn_ln_g"], A["L1_gnn_ln_b"]))
        project(nc, m, "p2", "ln", m.W["g1"], D + 4, heads=4, table=m.atable[0])
        self_loops(nc, m, "s2", D, 4, None, LOOPS)
        attend(nc, m, "t2", 4, m.atable[0])
        finish_attention(nc, m, "f2", 4, A["L1_gnn_b1"], False)
        if upto == 25:
            m.X = m.ACC[:, :, 0:D]
            return store_x(nc, m, out)
        row_moments(nc, m, "m3", m.ACC[:, :, 0:D])
        project(nc, m, "p3", "relu", m.W["g2"], D + 1, heads=1, table=m.atable[1],
                vecs=(m.vec[:, 0, :], m.vec[:, 1, :]))
        self_loops(nc, m, "s3", D, 1, None, LOOPS, at=D + 1)
        attend(nc, m, "t3", 1, m.atable[1])
        finish_attention(nc, m, "f3", 1, A["L1_gnn_b2"], True)
        if upto == 3:
            return store_x(nc, m, out)
        row_moments(nc, m, "m4", m.X)
        project(nc, m, "gatep", "ln", m.W["gat"], 20, heads=4, table=m.gtable)
        self_loops(nc, m, "s4", 16, 4, m.gedu, N)
        gate_attend_and_experts(nc, m, A)
        gates(nc, m, A)
        mix_experts(nc, m, out)


_INS = ['x', 'src', 'dst', 'edge_weight', 'L0_gnn_W1', 'L0_gnn_W2', 'L0_ffn_gate_w', 'L0_ffn_gate_b', 'L0_ffn_w1',
        'L0_ffn_b1', 'L0_ffn_w2', 'L0_ffn_b2', 'L1_gnn_W1', 'L1_gnn_a1_src', 'L1_gnn_a1_dst', 'L1_gnn_b1',
        'L1_gnn_ln_g', 'L1_gnn_ln_b', 'L1_gnn_W2', 'L1_gnn_a2_src', 'L1_gnn_a2_dst', 'L1_gnn_b2', 'L1_ffn_W_gat',
        'L1_ffn_att_src', 'L1_ffn_att_dst', 'L1_ffn_b_gat', 'L1_ffn_ln_gamma', 'L1_ffn_ln_beta', 'L1_ffn_W1',
        'L1_ffn_b1', 'L1_ffn_W2', 'L1_ffn_b2', 'L1_ffn_edge_index']


def kernel(**inputs):
    import numpy as _np
    import concourse.bacc as _bacc
    from concourse import mybir as _mybir
    from concourse.bass_utils import run_bass_kernel_spmd as _run

    nc = _bacc.Bacc("TRN2", target_bir_lowering=False, num_devices=1)
    arrays, args = {}, {}
    for name in _INS:
        a = _np.ascontiguousarray(inputs[name])
        arrays[f"in_{name}_dram"] = a
        args[name] = nc.dram_tensor(f"in_{name}_dram", a.shape, _mybir.dt.from_np(a.dtype), kind="ExternalInput").ap()
    out = nc.dram_tensor("out_0_dram", (N, D), _mybir.dt.float32, kind="ExternalOutput").ap()
    program(nc, args, out)
    r = _run(nc, [arrays], core_ids=[0])
    return r.results[0]["out_0_dram"]
```

```python
from contextlib import ExitStack

import concourse.bass as bass
from concourse import mybir

P = 128
D = 256
N = 3125
T = 25
NP_ = T * P
TAIL = N - (T - 1) * P
U = 5
TURNS = T // U

E0 = 50000
B = 7
NBLK = 56
EPAD = NBLK * B * P
ROWE = B * P
DEPTH = 7
AHEAD = 3
LEAD = DEPTH - AHEAD
NONE = T
VIS = NBLK * T + 4
TURNS2 = NBLK * T // 2 + 1

E1 = 32768
FB = 13
FROW = FB * P
FNBLK = -(-E1 // FROW)

NEXP = 8
CAP = 489
HID = 1024
KEXP = 4
HID2 = 512
GH = 4
EPS = 1e-5
SLOPE = 0.2
LOOPS = 625
NEG = -1.0e30
FMAX = 3.4028234663852886e38

ALU = mybir.AluOpType
ACT = mybir.ActivationFunctionType
F32 = mybir.dt.float32
BF16 = mybir.dt.bfloat16
U16 = mybir.dt.uint16
I32 = mybir.dt.int32
U32 = mybir.dt.uint32
X_ = mybir.AxisListType.X
ds = bass.ds


class Steps:

    def __init__(self, eng, sem, start=0):
        self.eng, self.sem, self.at = eng, sem, start

    def __call__(self, ins):
        ins.then_inc(self.sem, 1)
        self.at = self.at + 1
        self.eng.wait_ge(self.sem, self.at)


class Phase:

    def __init__(self, nc, name):
        self.nc, self.name, self.ctx, self.sems = nc, name, ExitStack(), []

    def __enter__(self):
        return self

    def __exit__(self, *a):
        self.ctx.close()
        self.nc.clear_and_free_semaphores(self.sems)
        self.nc.all_engine_barrier()

    def sb(self, name, shape, dt=F32):
        return self.ctx.enter_context(self.nc.sbuf_tensor(f"{self.name}_{name}", shape, dt))

    def sem(self, name):
        self.sems.append(self.nc.alloc_semaphore(f"{self.name}_{name}"))
        return self.sems[-1]


class Memory:
    pass


def dup(ap, k):
    p, a = ap.shape
    return ap.rearrange("p (a o) -> p a o", o=1).broadcast_to([p, a, k])


def alloc(nc, ctx, m):
    def sb(name, shape, dt=F32):
        return ctx.enter_context(nc.sbuf_tensor(name, shape, dt))

    m.X = sb("X", [P, T, D])
    m.ACCX = sb("ACC", [P, T + 1, D + GH])
    m.ACC = m.ACCX[:, 0:T, :]
    m.XN = sb("XN", [P, T, D])
    m.iota = sb("iota", [P, NP_ + P])
    m.pcol = sb("pcol", [P, 1])
    m.ident = sb("ident", [P, P])
    m.upper = sb("upper", [P, P])
    m.ones = sb("ones", [P, P])
    m.pen = sb("pen", [P, 1])
    m.own = sb("own", [P, 1])
    m.src = sb("src_t", [P, NBLK, B], U32)
    m.dw = sb("dw_t", [P, NBLK, 2, B])
    m.tiles = sb("tiles", [1, TURNS2], I32)
    m.blocks = sb("blocks", [1, TURNS2], I32)
    m.cum = sb("cum", [1, LEAD + NBLK], I32)
    m.fsrc = sb("fsrc", [P, FB, FNBLK], U32)
    m.fdst = sb("fdst", [P, FB, FNBLK], U32)
    m.flo = sb("flo", [P, FB, FNBLK])
    m.fhi = sb("fhi", [P, FB, FNBLK])
    m.mean = sb("mean", [P, T])
    m.rstd = sb("rstd", [P, T])
    m.XT = m.XN[:].rearrange("p t c -> p (t c)").rearrange("p (k n) -> p k n", k=2)
    m.gscale = sb("gscale", [P, T])
    m.gidx = sb("gidx", [P, T], U32)
    m.gate = sb("gate", [P, T, KEXP])
    m.EDU = sb("EDU", [P, T, 2 * GH])
    m.EDB = sb("EDB", [P, T + 1, 6 * GH], BF16)
    m.W = {k: sb(f"W_{k}", [P, 2, n]) for k, n in
           (("c1", D), ("c2", D), ("g1", D + 8), ("g2", D + 2), ("gate", 8), ("gat", 24))}
    m.ps = ctx.enter_context(nc.psum_tensor("ps", [P, 8, 512], F32))


def prepare(nc, m, A):
    with Phase(nc, "prep") as f:
        raw = f.sb("raw", [NBLK, 2, ROWE], I32)
        rawf = f.sb("rawf", [NBLK, 3, ROWE])
        bi = f.sb("bi", [NBLK, 2], I32)
        bf = f.sb("bf", [NBLK, 2])
        cnt = f.sb("cnt", [NBLK, 4])
        inb = f.sb("inb", [NBLK, VIS])
        spare = m.ACC.rearrange("p t c -> p (t c)")
        inb2 = spare[0:NBLK, 0:VIS]
        seq = f.sb("seq", [1, 3, VIS + 1])
        fifth = f.sb("fifth", [1, TURNS2], I32)
        half = f.sb("half", [1, 2, TURNS2])
        rows16 = f.sb("rows16", [NBLK, ROWE], U16)
        s_sum = f.sem("sum")
        s_base = f.sem("base")
        s_vis = f.sem("vis")
        s_r16 = f.sem("r16")
        s_rd = f.sem("rd")
        s_in = f.sem("in")
        s_fill = f.sem("fill")
        s_edge = f.sem("edge")
        s_iota = f.sem("iota")
        s_v = f.sem("v")
        s_tr = f.sem("tr")
        s_cp = f.sem("cp")
        s_row = f.sem("row")
        s_zero = f.sem("zero")
        full = E0 // ROWE
        rest = E0 - full * ROWE
        with nc.Block() as block:

            @block.sync
            def _(sp):
                sp.wait_ge(s_fill, 3)
                for k, name in enumerate(("src", "dst")):
                    sp.dma_start(raw[0:full, k, :], A[name][0:full * ROWE].rearrange("(b e) -> b e", e=ROWE)).then_inc(s_edge, 16)
                    sp.dma_start(raw[full:full + 1, k, 0:rest], A[name][full * ROWE:E0].rearrange("(b e) -> b e", b=1)).then_inc(s_edge, 16)
                sp.dma_start(rawf[0:full, 2, :], A["edge_weight"][0:full * ROWE].rearrange("(b e) -> b e", e=ROWE)).then_inc(s_edge, 16)
                sp.dma_start(rawf[full:full + 1, 2, 0:rest], A["edge_weight"][full * ROWE:E0].rearrange("(b e) -> b e", b=1)).then_inc(s_edge, 16)
                sp.dma_start(m.W["c1"][:], A["L0_gnn_W1"].rearrange("(k p) n -> p k n", p=P)).then_inc(s_in, 16)
                sp.dma_start(m.W["c2"][:], A["L0_gnn_W2"].rearrange("(k p) n -> p k n", p=P)).then_inc(s_in, 16)
                sp.dma_start(m.W["g1"][:, :, 0:D], A["L1_gnn_W1"].rearrange("(k p) n -> p k n", p=P)).then_inc(s_in, 16)
                sp.dma_start(m.W["g2"][:, :, 0:D], A["L1_gnn_W2"].rearrange("(k p) n -> p k n", p=P)).then_inc(s_in, 16)
                sp.dma_start(m.W["gate"][:], A["L0_ffn_gate_w"].rearrange("(k p) n -> p k n", p=P)).then_inc(s_in, 16)
                sp.dma_start(m.W["gat"][:, :, 0:16], A["L1_ffn_W_gat"].rearrange("(k p) n -> p k n", p=P)).then_inc(s_in, 16)
                sp.wait_ge(s_in, 6 * 16)
                sp.wait_ge(s_edge, 6 * 16)
                sp.wait_ge(s_r16, 1)
                sp.dma_start(m.drows[:, :], rows16[:]).then_inc(s_rd, 16)
                sp.wait_ge(s_rd, 16)

            @block.scalar
            def _(act):
                act.wait_ge(s_fill, 4)
                act.dma_start(m.X[:, 0:T - 1, :], A["x"][0:(T - 1) * P, :].rearrange("(t p) d -> p t d", p=P)).then_inc(s_zero, 16)
                act.dma_start(m.X[0:TAIL, T - 1, :], A["x"][(T - 1) * P:N, :]).then_inc(s_zero, 16)
                act.wait_ge(s_zero, 2 * 16)

            @block.gpsimd
            def _(pool):
                pool.iota(m.iota[:], [[1, NP_ + P]], base=0, channel_multiplier=0,
                          allow_small_or_imprecise_dtypes=True).then_inc(s_iota, 1)
                pool.iota(m.pcol[:], [[0, 1]], base=0, channel_multiplier=1,
                          allow_small_or_imprecise_dtypes=True).then_inc(s_iota, 1)
                pool.memset(m.XN[:], 0.0)

            @block.vector
            def _(v):
                v.memset(raw[:, 0, :], 0).then_inc(s_fill, 1)
                v.memset(raw[:, 1, :], NP_ - 1).then_inc(s_fill, 1)
                v.memset(rawf[:, 2, :], 0.0).then_inc(s_fill, 1)
                v.memset(m.X[:, T - 1, :], 0.0).then_inc(s_fill, 1)
                step = Steps(v, s_v)
                v.memset(m.ACCX[:, T:T + 1, :], 0.0).then_inc(s_fill, 1)
                v.memset(m.EDB[:, T:T + 1, :], 0.0).then_inc(s_fill, 1)
                v.memset(m.ones[:], 1.0).then_inc(s_fill, 1)
                v.wait_ge(s_iota, 2)
                step(v.tensor_scalar(m.ident[:], m.iota[:, 0:P], m.pcol[:, 0:1], None, ALU.is_equal))
                step(v.tensor_scalar(m.upper[:], m.iota[:, 0:P], m.pcol[:, 0:1], None, ALU.is_ge))
                step(v.tensor_scalar(m.pen[:], m.pcol[:], float(TAIL), NEG, ALU.is_ge, ALU.mult))
                step(v.tensor_scalar(m.own[:], m.pcol[:], float(LOOPS % P), NEG, ALU.is_ge, ALU.mult))
                v.wait_ge(s_edge, 6 * 16)
                step(v.tensor_copy(rawf[:, 0:2, :], raw[:]))
                step(v.tensor_reduce(bf[:, 0:1], rawf[:, 1, :], X_, ALU.min))
                step(v.tensor_reduce(bf[:, 1:2], rawf[:, 1, :], X_, ALU.max))
                step(v.tensor_copy(bi[:], bf[:]))
                step(v.tensor_scalar(bi[:], bi[:], 7, None, ALU.logical_shift_right))
                step(v.tensor_copy(bf[:], bi[:]))
                v.sem_inc(s_row, 1)
                v.tensor_copy(rows16[:], rawf[:, 1, :]).then_inc(s_r16, 1)
                n = 0
                for k, out in ((0, m.src[:]), (1, m.dw[:, :, 0, :]), (2, m.dw[:, :, 1, :])):
                    n += 1
                    v.wait_ge(s_tr, n)
                    v.tensor_copy(out.rearrange("p b j -> p j b"), m.ps[:, 0, 0:B * NBLK].rearrange("p (j b) -> p j b", j=B)).then_inc(s_cp, 1)
                step(v.tensor_tensor(cnt[:, 0:1], bf[:, 1:2], bf[:, 0:1], ALU.subtract))
                step(v.tensor_scalar(cnt[:, 0:1], cnt[:, 0:1], 1.0, None, ALU.add))
                v.sem_inc(s_base, 1)
                v.wait_ge(s_sum, 1)
                step(v.tensor_copy(cnt[:, 1:2], m.ps[0:NBLK, 1, 0:1]))
                v.sem_inc(s_base, 1)
                step(v.tensor_tensor(cnt[:, 2:3], cnt[:, 1:2], cnt[:, 0:1], ALU.subtract))
                step(v.tensor_tensor(cnt[:, 3:4], bf[:, 0:1], cnt[:, 2:3], ALU.subtract))
                io = m.iota[0:NBLK, 0:VIS]
                step(v.tensor_scalar(inb2, io, cnt[:, 1:2], None, ALU.is_lt))
                step(v.scalar_tensor_tensor(out=inb[:], in0=io, scalar=cnt[:, 2:3], in1=inb2, op0=ALU.is_ge, op1=ALU.mult))
                v.sem_inc(s_base, 1)
                v.wait_ge(s_sum, 2)
                v.memset(m.cum[:], 0).then_inc(s_vis, 1)
                v.wait_ge(s_vis, 1)
                step(v.tensor_copy(m.cum[:, LEAD:LEAD + NBLK], m.ps[0:1, 1, 0:NBLK]))
                for k in range(3):
                    v.wait_ge(s_sum, 3 + k)
                    step(v.tensor_copy(seq[:, k, 1:VIS + 1].rearrange("p (a c) -> p a c", a=3), m.ps[0:1, 2 + 3 * (k % 2):5 + 3 * (k % 2), 0:VIS // 3]))
                    v.sem_inc(s_vis, 1)
                tl, bl, on = seq[:, 0, 1:VIS + 1], seq[:, 1, 1:VIS + 1], seq[:, 2, 1:VIS + 1]
                step(v.tensor_tensor(tl, tl, m.iota[0:1, 0:VIS], ALU.add))
                step(v.scalar_tensor_tensor(out=tl, in0=tl, scalar=-float(NONE), in1=on, op0=ALU.add, op1=ALU.mult))
                step(v.tensor_scalar(tl, tl, float(NONE), None, ALU.add))
                step(v.scalar_tensor_tensor(out=bl, in0=bl, scalar=-float(NBLK - 1), in1=on, op0=ALU.add, op1=ALU.mult))
                step(v.tensor_scalar(bl, bl, float(NBLK - 1), None, ALU.add))
                step(v.memset(seq[:, 0, 0:1], float(NONE)))
                def pick(k, at):
                    return seq[:, k, at:at + 2 * TURNS2 - 1:2]

                step(v.scalar_tensor_tensor(out=half[:, 0, :], in0=pick(0, 1), scalar=32.0, in1=pick(0, 0), op0=ALU.mult, op1=ALU.add))
                step(v.scalar_tensor_tensor(out=half[:, 0, :], in0=pick(0, 2), scalar=1024.0, in1=half[:, 0, :], op0=ALU.mult, op1=ALU.add))
                step(v.scalar_tensor_tensor(out=half[:, 0, :], in0=pick(0, 3), scalar=32768.0, in1=half[:, 0, :], op0=ALU.mult, op1=ALU.add))
                step(v.scalar_tensor_tensor(out=half[:, 1, :], in0=pick(1, 2), scalar=64.0, in1=pick(1, 1), op0=ALU.mult, op1=ALU.add))
                step(v.scalar_tensor_tensor(out=half[:, 1, :], in0=pick(1, 3), scalar=4096.0, in1=half[:, 1, :], op0=ALU.mult, op1=ALU.add))
                step(v.scalar_tensor_tensor(out=half[:, 1, :], in0=pick(1, 4), scalar=262144.0, in1=half[:, 1, :], op0=ALU.mult, op1=ALU.add))
                step(v.tensor_copy(m.tiles[:], half[:, 0, :]))
                step(v.tensor_copy(m.blocks[:], half[:, 1, :]))
                step(v.tensor_copy(fifth[:], pick(0, 4)))
                step(v.tensor_scalar(fifth[:], fifth[:], 20, None, ALU.logical_shift_left))
                step(v.tensor_tensor(m.tiles[:], m.tiles[:], fifth[:], ALU.bitwise_or))

            @block.tensor
            def _(pe):
                pe.wait_ge(s_row, 1)
                n = 0
                for k in (0, 1, 2):
                    if n:
                        pe.wait_ge(s_cp, n)
                    for j in range(B):
                        last = pe.transpose(m.ps[:, 0, j * NBLK:(j + 1) * NBLK], rawf[:, k, j * P:(j + 1) * P],
                                            m.ident[0:NBLK, 0:NBLK])
                    last.then_inc(s_tr, 1)
                    n += 1
                pe.wait_ge(s_base, 1)
                pe.matmul(m.ps[0:NBLK, 1, 0:1], m.upper[0:NBLK, 0:NBLK], cnt[:, 0:1], start=True, stop=True).then_inc(s_sum, 1)
                pe.wait_ge(s_base, 2)
                pe.transpose(m.ps[0:1, 1, 0:NBLK], cnt[:, 1:2], m.ident[0:NBLK, 0:NBLK]).then_inc(s_sum, 1)
                pe.wait_ge(s_base, 3)
                for k, col in enumerate((cnt[:, 3:4], m.pcol[0:NBLK, 0:1], m.ones[0:NBLK, 0:1])):
                    pe.wait_ge(s_vis, max(k, 1))
                    for a in range(3):
                        last = pe.matmul(m.ps[0:1, 2 + 3 * (k % 2) + a, 0:VIS // 3], col, inb[:, a * (VIS // 3):(a + 1) * (VIS // 3)],
                                         start=True, stop=True)
                    last.then_inc(s_sum, 1)


def project(nc, m, name, kind, w, cols, heads=0, table=None, first=None, gat=0, params=()):
    full = cols + heads
    width = cols + 1 if heads == 1 else cols
    FIRST = {None: 0, "add": 1, "attention": 5, "both": 6, "combine": 4}[first]
    combine = first == "combine"
    with Phase(nc, name) as f:
        xs = f.sb("xs", [P, U, D])
        xt = f.sb("xt", [P, U, 2, P])
        st = f.sb("st", [P, U, 6])
        mv = f.sb("mv", [P, U, 2])
        none = f.sb("none", [P, U, GH])
        par = f.sb("par", [P, 3, D])
        r = f.sb("r", [P, U, D]) if combine else None
        r2 = f.sb("r2", [P, U, D]) if combine else None
        fin = f.sb("fin", [P, U, D], I32) if combine else None
        s_g = [f.sem(f"g{k}") for k in range(TURNS)] if combine else None
        s_par = f.sem("par")
        s_f = f.sem("f")
        s_st = f.sem("st")
        s_mv = f.sem("mv")
        s_cp = f.sem("cp")
        s_sq = f.sem("sq")
        s_rc = f.sem("rc")
        s_turn = f.sem("turn")
        s_xs = f.sem("xs")
        s_tr = f.sem("tr")
        s_xt = f.sem("xt")
        s_mm = f.sem("mm")
        s_out = f.sem("out")
        s_keep = f.sem("keep")
        s_dma = f.sem("dma")
        s_v = f.sem("v")
        keep_x = name == "route"
        keep_xt = name == "gatep"
        norm = kind != "acc"

        def p_turn(j):
            return m.ps[:, j, 0:2 * P]

        with nc.Block() as block:

            @block.sync
            def _(sp):
                for k, ap in enumerate(params):
                    sp.dma_start(par[:, k, :], ap.partition_broadcast(P)).then_inc(s_par, 16)
                if table is not None:
                    with sp.Fori(0, TURNS) as i:
                        sp.wait_ge(s_out, U * i + 2 * U)
                        sp.sem_inc(s_keep, 1)
                        sp.dma_start(table.rearrange("(t p) c -> p t c", p=P)[:, ds(U * i, U), :],
                                     m.ACC[:, ds(U * i, U), 0:width]).then_inc(s_dma, 16)
                    sp.wait_ge(s_dma, 16 * TURNS)

            @block.vector
            def _(v):
                if params:
                    v.wait_ge(s_par, 16 * len(params))

                def moments(i):
                    step = Steps(v, s_f, FIRST * i)
                    a = m.ACC[:, ds(U * i, U), 0:D]
                    if first in ("attention", "both"):
                        den = m.ACC[:, ds(U * i, U), D:D + gat]
                        no = none[:, :, 0:gat]
                        step(v.tensor_scalar(no, den, 0.0, None, ALU.is_equal))
                        step(v.tensor_tensor(den, den, no, ALU.add))
                        v.sem_inc(s_turn, 1)
                        step(v.reciprocal(den, den))
                        a4 = a.rearrange("p t (h c) -> p t h c", h=gat)
                        r4 = den.rearrange("p t (h o) -> p t h o", o=1).broadcast_to([P, U, gat, D // gat])
                        step(v.tensor_tensor(a4, a4, r4, ALU.mult))
                        step(v.tensor_tensor(a, a, par[:, 0:1, :].broadcast_to([P, U, D]), ALU.add))
                    if first in ("add", "both"):
                        x = m.X[:, ds(U * i, U), :]
                        step(v.tensor_tensor(x, x, a, ALU.add))
                    if combine:
                        v.wait_ge(s_g[i], 16 * U)
                        v.tensor_scalar(r[:], a, FMAX, 1.0e4, ALU.is_gt, ALU.mult)
                        v.tensor_scalar(r2[:], a, -FMAX, -1.0e4, ALU.is_lt, ALU.mult)
                        step(v.tensor_scalar(fin[:], a, 0.0, 0.0, ALU.mult, ALU.is_equal))
                        step(v.tensor_tensor(r[:], r[:], r2[:], ALU.add))
                        step(v.copy_predicated(r[:], fin[:], a))
                        for j in range(U):
                            t = U * i + j
                            ins = v.scalar_tensor_tensor(out=m.X[:, t, :], in0=r[:, j, :], scalar=m.gscale[:, t:t + 1],
                                                         in1=m.X[:, t, :], op0=ALU.mult, op1=ALU.add)
                        step(ins)
                    src = m.X if kind == "ln" else m.ACC
                    v.sem_inc(s_turn, 1)
                    for j in range(U):
                        v.bn_stats(st[:, j, :], src[:, ds(U * i + j, 1), 0:D]).then_inc(s_st, 1)
                    for j in range(U):
                        v.wait_ge(s_st, U * i + j + 1)
                        v.sem_inc(s_turn, 1)
                        v.bn_aggr(mv[:, j, :], st[:, j, :]).then_inc(s_mv, 1)
                    v.wait_ge(s_mv, U * i + U)
                    v.tensor_copy(m.mean[:, ds(U * i, U)], mv[:, :, 0]).then_inc(s_cp, 1)
                    v.tensor_scalar(m.rstd[:, ds(U * i, U)], mv[:, :, 1], EPS, None, ALU.add).then_inc(s_cp, 1)
                    v.wait_ge(s_cp, 2 * i + 2)

                def tiles(i):
                    if norm:
                        r = m.rstd[:, ds(U * i, U)]
                        v.wait_ge(s_sq, i + 1)
                        v.sem_inc(s_turn, 1)
                        v.reciprocal(r, r).then_inc(s_rc, 1)
                        v.wait_ge(s_rc, i + 1)
                    for j in range(U):
                        t = U * i + j
                        v.wait_ge(s_tr, t + 1)
                        if keep_x:
                            v.wait_ge(s_keep, t + 1)
                        if kind == "acc":
                            v.tensor_copy(xs[:, j, :], m.ACC[:, ds(t, 1), 0:D]).then_inc(s_xs, 1)
                            continue
                        src = m.X[:, ds(t, 1), :] if kind == "ln" else m.ACC[:, ds(t, 1), 0:D]
                        ins = v.tensor_scalar(xs[:, j, :], src, m.mean[:, ds(t, 1)], m.rstd[:, ds(t, 1)],
                                              ALU.subtract, ALU.mult)
                        if kind == "relu":
                            base = 2 * t
                            ins.then_inc(s_v, 1)
                            v.wait_ge(s_v, base + 1)
                            v.tensor_tensor(xs[:, j, :], xs[:, j, :], par[:, 1, :], ALU.mult).then_inc(s_v, 1)
                            v.wait_ge(s_v, base + 2)
                            ins = v.tensor_tensor(xs[:, j, :], xs[:, j, :], par[:, 2, :], ALU.add)
                        ins.then_inc(s_xs, 1)

                if combine:
                    moments(0)
                    for i in range(TURNS - 1):
                        tiles(i)
                        moments(i + 1)
                    tiles(TURNS - 1)
                elif norm:
                    moments(0)
                    with v.Fori(0, TURNS - 1) as i:
                        tiles(i)
                        moments(i + 1)
                    tiles(TURNS - 1)
                else:
                    with v.Fori(0, TURNS) as i:
                        tiles(i)

            @block.gpsimd
            def _(pool):
                for t in range(T if combine else 0):
                    pool.indirect_dma_start(
                        out=m.ACC[:, t, 0:D], out_offset=None, in_=m.yslots[:, :],
                        in_offset=bass.IndirectOffsetOnAxis(ap=m.gidx[:, t:t + 1], axis=0)).then_inc(s_g[t // U], 16)

            @block.scalar
            def _(act):
                def root(i):
                    r = m.rstd[:, ds(U * i, U)]
                    act.wait_ge(s_cp, 2 * i + 2)
                    act.activation(r, r, ACT.Sqrt).then_inc(s_sq, 1)

                def turned(i):
                    for j in range(U):
                        t = U * i + j
                        if keep_x:
                            act.wait_ge(s_xs, t + 1)
                            act.copy(m.XN[:, ds(t, 1), :], xs[:, j, :]).then_inc(s_keep, 1)
                        act.wait_ge(s_tr, U + t + 1)
                        act.wait_ge(s_mm, t + 1)
                        pt = p_turn(j).rearrange("p (k n) -> p k n", k=2)
                        if keep_xt:
                            act.copy(m.XT[:, :, ds(P * t, P)], pt)
                        if kind == "relu":
                            act.activation(xt[:, j, :, :], pt, ACT.Relu).then_inc(s_xt, 1)
                        else:
                            act.copy(xt[:, j, :, :], pt).then_inc(s_xt, 1)

                def results(i):
                    for j in range(U):
                        t = U * i + j
                        act.wait_ge(s_mm, U + t + 1)
                        if heads:
                            act.copy(m.EDU[:, ds(t, 1), 0:heads], m.ps[:, j, cols:full])
                        if heads == 1:
                            act.copy(m.ACC[:, ds(t, 1), D:D + 1], m.ones[:, 0:1])
                            act.copy(m.ACC[:, ds(t, 1), D + 1:D + 2], m.ps[:, j, D:D + 1])
                            act.copy(m.ACC[:, ds(t, 1), 0:D], m.ps[:, j, 0:D]).then_inc(s_out, 1)
                        else:
                            act.copy(m.ACC[:, ds(t, 1), 0:cols], m.ps[:, j, 0:cols]).then_inc(s_out, 1)

                act.sem_inc(s_xt, U)
                act.sem_inc(s_out, U)
                if keep_x:
                    act.sem_inc(s_keep, U)
                if norm:
                    root(0)
                    with act.Fori(0, TURNS - 1) as i:
                        turned(i)
                        root(i + 1)
                        results(i)
                    turned(TURNS - 1)
                    results(TURNS - 1)
                else:
                    with act.Fori(0, TURNS) as i:
                        turned(i)
                        results(i)

            @block.tensor
            def _(pe):
                pe.sem_inc(s_tr, U)
                pe.sem_inc(s_mm, U)
                with pe.Fori(0, TURNS) as i:
                    for j in range(U):
                        t = U * i + j
                        pe.wait_ge(s_xs, t + 1)
                        pe.wait_ge(s_out, t + 1)
                        for k in range(2):
                            ins = pe.transpose(p_turn(j)[:, k * P:(k + 1) * P], xs[:, j, k * P:(k + 1) * P], m.ident[:])
                        ins.then_inc(s_tr, 1)
                    for j in range(U):
                        t = U * i + j
                        pe.wait_ge(s_xt, U + t + 1)
                        for k in range(2):
                            ins = pe.matmul(m.ps[:, j, 0:full], xt[:, j, k, :], w[:, k, 0:full],
                                            start=(k == 0), stop=(k == 1))
                        ins.then_inc(s_mm, 1)


def visit_turn(nc, eng, m, i):
    tiles = eng.value_load(m.tiles[0:1, ds(i, 1)], min_val=0, max_val=(1 << 25) - 1)
    blocks = eng.value_load(m.blocks[0:1, ds(i, 1)], min_val=0, max_val=(1 << 24) - 1)

    def part(packed, k, bits, top):
        return nc.s_assert_within(eng.snap(packed // (1 << bits * k) % (1 << bits)), 0, top,
                                  skip_runtime_bounds_check_because="packed from smaller values")

    return [part(tiles, k, 5, NONE) for k in range(5)], [part(blocks, k, 6, NBLK - 1) for k in range(4)]


def visit_turns(eng, m):
    total = eng.value_load(m.cum[0:1, LEAD + NBLK - 1:LEAD + NBLK], min_val=NBLK, max_val=NBLK * T)
    return eng.snap((total + 1) // 2)


def feed(sp, m, ix, s_ix, s_rows, s_ready, s_used, ahead, s_free, rows=None, s_rowsin=None, s_dready=None):
    def load(b, turn, q, waits=True):
        if waits:
            before = sp.value_load(m.cum[0:1, ds(b - DEPTH + LEAD, 1)], min_val=0, max_val=NBLK * T)
            sp.wait_ge(s_used, before + ahead)
            sp.sem_inc(s_free, 1)
        sp.dma_start(ix[:, q, :], m.src[:, ds(b, 1), :]).then_inc(s_ix[q], 16)
        if rows is not None:
            sp.dma_start(rows[:, q, :], m.drows[ds(b, 1), :].rearrange("o n -> (o n)").partition_broadcast(P)).then_inc(s_rowsin[q], 16)
            sp.wait_ge(s_rowsin[q], 16 * (turn + 1))
            sp.sem_inc(s_dready, 1)

    def passed(turn, q):
        sp.wait_ge(s_rows[q], 16 * B * (turn + 1))
        sp.sem_inc(s_ready, 1)

    for b in range(AHEAD):
        load(b, 0, b, waits=False)
    with sp.Fori(0, NBLK // DEPTH - 1) as i:
        for q in range(DEPTH):
            load(DEPTH * i + q + AHEAD, i + (q + AHEAD) // DEPTH, (q + AHEAD) % DEPTH)
            passed(i, q)
    for q in range(DEPTH):
        if q + AHEAD < DEPTH:
            load(NBLK - DEPTH + q + AHEAD, NBLK // DEPTH - 1, q + AHEAD)
        passed(NBLK // DEPTH - 1, q)


def gather_rows(pool, G, ix, table, s_ix, s_rows, s_turn):
    with pool.Fori(0, NBLK // DEPTH) as i:
        for q in range(DEPTH):
            pool.wait_ge(s_ix[q], 16 * (i + 1))
            pool.sem_inc(s_turn, 1)
            for j in range(B):
                pool.indirect_dma_start(
                    out=G[:, q, j, :], out_offset=None, in_=table[:, :],
                    in_offset=bass.IndirectOffsetOnAxis(ap=ix[:, q, j:j + 1], axis=0),
                ).then_inc(s_rows[q], 16)


class LaterNeeds:

    def __init__(self, f, A):
        self.A = A
        self.raw = f.sb("fraw", [FNBLK, 2, FROW], I32)
        self.rawf = f.sb("frawf", [FNBLK, 2, FROW])
        self.att = f.sb("att", [P, 4 * D + 32])
        self.prod = f.sb("prod", [P, D])
        self.s_fill = f.sem("ffill")
        self.s_in = f.sem("fin")
        self.s_edge = f.sem("fedge")
        self.s_row = f.sem("frow")
        self.s_zero = f.sem("fzero")
        self.s_tr = f.sem("ftr")
        self.s_cp = f.sem("fcp")
        self.s_v = f.sem("fv")

    def load(self, eng, m):
        A = self.A
        names = ("L1_gnn_a1_src", "L1_gnn_a1_dst", "L1_gnn_a2_src", "L1_gnn_a2_dst")
        for k, name in enumerate(names):
            eng.dma_start(self.att[:, k * D:(k + 1) * D],
                          A[name].rearrange("a b -> (a b)").partition_broadcast(P)).then_inc(self.s_in, 16)
        for k, name in enumerate(("L1_ffn_att_src", "L1_ffn_att_dst")):
            eng.dma_start(self.att[:, 4 * D + 16 * k:4 * D + 16 * k + 16],
                          A[name].rearrange("a b -> (a b)").partition_broadcast(P)).then_inc(self.s_in, 16)
        eng.wait_ge(self.s_fill, 2)
        whole = E1 // FROW
        rest = E1 - whole * FROW
        for k in range(2):
            edge = A["L1_ffn_edge_index"][k]
            eng.dma_start(self.raw[0:whole, k, :], edge[0:whole * FROW].rearrange("(b e) -> b e", e=FROW)).then_inc(self.s_edge, 16)
            eng.dma_start(self.raw[whole:whole + 1, k, 0:rest], edge[whole * FROW:E1].rearrange("(b e) -> b e", b=1)).then_inc(self.s_edge, 16)
        zrow = 15 * P
        for k in range(2):
            eng.dma_start(m.slots[k * zrow:(k + 1) * zrow, :].rearrange("(p a) d -> p a d", p=P), m.XN[:, 0:15, :]).then_inc(self.s_zero, 16)
        eng.dma_start(m.slots[2 * zrow:2 * zrow + P, :], m.XN[:, 0, :]).then_inc(self.s_zero, 16)
        eng.wait_ge(self.s_zero, 3 * 16)

    def vector(self, v, m):
        raw, rawf, att, prod = self.raw, self.rawf, self.att, self.prod
        v.memset(raw[:, 0, :], 0).then_inc(self.s_fill, 1)
        v.memset(raw[:, 1, :], NP_ - 1).then_inc(self.s_fill, 1)
        step = Steps(v, self.s_v)
        v.wait_ge(self.s_in, 6 * 16)
        for k in range(2):
            for w, wide, heads, base in ((m.W["g1"], D, 4, 0), (m.W["g2"], D, 1, 2 * D), (m.W["gat"], 16, 4, 4 * D)):
                for a in range(2):
                    step(v.tensor_tensor(prod[:, 0:wide], w[:, k, 0:wide], att[:, base + a * wide:base + (a + 1) * wide], ALU.mult))
                    step(v.tensor_reduce(w[:, k, wide + a * heads:wide + (a + 1) * heads],
                                         prod[:, 0:wide].rearrange("p (h c) -> p h c", h=heads), X_, ALU.add))
        v.wait_ge(self.s_edge, 4 * 16)
        step(v.tensor_copy(rawf[:], raw[:]))
        v.sem_inc(self.s_row, 1)
        step(v.tensor_scalar(raw[:, 0, :], raw[:, 1, :], 7, None, ALU.logical_shift_right))
        step(v.tensor_scalar(raw[:, 1, :], raw[:, 1, :], P - 1, None, ALU.bitwise_and))
        for n, out in enumerate((m.fsrc, m.fdst, m.fhi, m.flo)):
            if n == 2:
                step(v.tensor_copy(rawf[:], raw[:]))
                v.sem_inc(self.s_row, 1)
            v.wait_ge(self.s_tr, n + 1)
            v.tensor_copy(out[:], m.ps[:, 7, 0:FB * FNBLK].rearrange("p (j b) -> p j b", j=FB)).then_inc(self.s_cp, 1)

    def tensor(self, pe, m):
        for n in range(4):
            pe.wait_ge(self.s_row, 1 + n // 2)
            if n:
                pe.wait_ge(self.s_cp, n)
            for j in range(FB):
                last = pe.transpose(m.ps[:, 7, j * FNBLK:(j + 1) * FNBLK], self.rawf[:, n % 2, j * P:(j + 1) * P],
                                    m.ident[0:FNBLK, 0:FNBLK])
            last.then_inc(self.s_tr, 1)


def convolve(nc, m, name, table, A=None):
    with Phase(nc, name) as f:
        G = f.sb("G", [P, DEPTH, B, D])
        ix = f.sb("ix", [P, DEPTH, B], U32)
        dw = f.sb("dw", [P, 2, 2, B])
        S = f.sb("S", [P, 2, B, P])
        s_zero = f.sem("zero")
        s_ix = [f.sem(f"ix{q}") for q in range(DEPTH)]
        s_rows = [f.sem(f"rows{q}") for q in range(DEPTH)]
        s_ready = f.sem("ready")
        s_free = f.sem("free")
        s_turn = f.sem("turn")
        s_dw = f.sem("dw")
        s_S = f.sem("S")
        s_mm = f.sem("mm")
        s_add = f.sem("add")
        later = LaterNeeds(f, A) if A is not None else None
        with nc.Block() as block:

            @block.sync
            def _(sp):
                feed(sp, m, ix, s_ix, s_rows, s_ready, s_mm, 1, s_free)

            @block.scalar
            def _(act):
                if later is not None:
                    later.load(act, m)

            @block.gpsimd
            def _(pool):
                gather_rows(pool, G, ix, table, s_ix, s_rows, s_turn)

            @block.vector
            def _(v):
                if later is not None:
                    later.vector(v, m)
                v.memset(m.ACC[:], 0.0).then_inc(s_zero, 1)
                v.wait_ge(s_zero, 1)
                v.sem_inc(s_add, 1)

                def place(n, p, t, b):
                    if n is not p:
                        v.wait_ge(s_mm, n)
                        v.wait_ge(s_S, n - 1)
                    v.tensor_copy(dw[:, p, :, :], m.dw[:, ds(b, 1), :, :].rearrange("p o a j -> p (o a) j")).then_inc(s_dw, 1)
                    v.wait_ge(s_dw, n + 1)
                    for j in range(B):
                        ins = v.tensor_scalar(S[:, p, j, :], m.iota[:, ds(P * t, P)], dw[:, p, 0, j:j + 1],
                                              dw[:, p, 1, j:j + 1], ALU.is_equal, ALU.mult)
                    ins.then_inc(s_S, 1)

                def add(n, p, t):
                    v.wait_ge(s_mm, n + 2)
                    v.wait_ge(s_add, n + 1)
                    v.tensor_tensor(m.ACCX[:, ds(t, 1), 0:D], m.ACCX[:, ds(t, 1), 0:D],
                                    m.ps[:, p:p + 1, 0:D], ALU.add).then_inc(s_add, 1)

                t, b = visit_turn(nc, v, m, 0)
                place(0, 0, t[1], b[0])
                place(1, 1, t[2], b[1])
                add(0, 0, t[1])
                turns = visit_turns(v, m)
                with v.Fori(1, turns) as i:
                    t, b = visit_turn(nc, v, m, i)
                    place(2 * i, 0, t[1], b[0])
                    add(2 * i - 1, 1, t[0])
                    place(2 * i + 1, 1, t[2], b[1])
                    add(2 * i, 0, t[1])
                t, b = visit_turn(nc, v, m, turns)
                add(2 * turns - 1, 1, t[0])

            @block.tensor
            def _(pe):
                if later is not None:
                    later.tensor(pe, m)
                pe.sem_inc(s_mm, 1)
                turns = visit_turns(pe, m)

                with pe.Fori(0, turns) as i:
                    t, b = visit_turn(nc, pe, m, i)
                    for p in range(2):
                        n = 2 * i + p
                        pe.wait_ge(s_ready, b[p] + 1)
                        pe.wait_ge(s_S, n + 1)
                        for j in range(B):
                            ins = pe.matmul(m.ps[:, p, 0:D], S[:, p, j, :], G[:, ds(b[p] % DEPTH, 1), j, :],
                                            start=(j == 0), stop=(j == B - 1))
                        ins.then_inc(s_mm, 1)


def self_loops(nc, m, name, hc, H, edu_table, loops, at=None):
    at = hc if at is None else at
    with Phase(nc, name) as f:
        es = f.sb("es", [P, T, H])
        top = f.sb("top", [P, H])
        tops = f.sb("tops", [P, H])
        sc = f.sb("sc", [P, T, H])
        left = f.sb("left", [P, T, 2 * H])
        s_v = f.sem("v")
        s_top = f.sem("top")
        s_tops = f.sem("tops")
        s_edu = f.sem("edu")
        s_sc = f.sem("sc")
        s_w = f.sem("w")
        s_dma = f.sem("dma")
        ed = m.EDU[:, :, 0:H]
        bound = m.EDU[:, :, H:2 * H]
        with nc.Block() as block:

            @block.vector
            def _(v):
                step = Steps(v, s_v)
                step(v.tensor_copy(es[:], m.ACC[:, :, at:at + H]))
                step(v.tensor_scalar(es[:, T - 1, :], es[:, T - 1, :], m.pen[:, 0:1], None, ALU.add))
                v.tensor_reduce(top[:], es[:].rearrange("p t h -> p h t"), X_, ALU.max).then_inc(s_top, 1)
                v.wait_ge(s_tops, 1)
                big = tops[:].rearrange("p (o h) -> p o h", o=1).broadcast_to([P, T, H])
                step(v.tensor_tensor(bound, ed, big, ALU.add))
                step(v.scalar_tensor_tensor(out=bound, in0=bound, scalar=SLOPE, in1=bound, op0=ALU.mult, op1=ALU.max))
                v.sem_inc(s_edu, 1)
                if edu_table is None:
                    rest = m.EDU[:, :, 0:2 * H]
                    step(v.tensor_copy(left[:], rest))
                    for k in range(3):
                        part = m.EDB[:, 0:T, 2 * H * k:2 * H * (k + 1)]
                        step(v.tensor_copy(part, left[:]))
                        if k < 2:
                            step(v.tensor_tensor(left[:], left[:], part, ALU.subtract))
                step(v.tensor_tensor(sc[:], m.ACC[:, :, at:at + H], ed, ALU.add))
                step(v.scalar_tensor_tensor(out=sc[:], in0=sc[:], scalar=SLOPE, in1=sc[:], op0=ALU.mult, op1=ALU.max))
                step(v.tensor_tensor(sc[:], sc[:], bound, ALU.subtract))
                step(v.tensor_scalar(sc[:], sc[:], 0.0, None, ALU.min))
                if loops < N:
                    k = loops // P
                    step(v.tensor_scalar(sc[:, k, :], sc[:, k, :], m.own[:, 0:1], None, ALU.add))
                    step(v.memset(sc[:, k + 1:T, :], NEG))
                v.sem_inc(s_sc, 1)
                v.wait_ge(s_w, 1)
                w4 = m.ACC[:, :, hc:hc + H].rearrange("p t (h o) -> p t h o", o=1).broadcast_to([P, T, H, hc // H])
                h4 = m.ACC[:, :, 0:hc].rearrange("p t (h c) -> p t h c", h=H)
                step(v.tensor_tensor(h4, h4, w4, ALU.mult))

            @block.gpsimd
            def _(pool):
                pool.wait_ge(s_top, 1)
                pool.partition_all_reduce(tops[:], top[:], P, bass.bass_isa.ReduceOp.max).then_inc(s_tops, 1)

            @block.scalar
            def _(act):
                act.wait_ge(s_sc, 1)
                act.activation(m.ACC[:, :, hc:hc + H], sc[:], ACT.Exp).then_inc(s_w, 1)

            @block.sync
            def _(sp):
                sp.wait_ge(s_edu, 1)
                if edu_table is None:
                    return
                sp.dma_start(edu_table.rearrange("(t p) c -> p t c", p=P), m.EDU[:, :, 0:2 * H]).then_inc(s_dma, 16)
                sp.wait_ge(s_dma, 16)


def edge_weights(v, act_sem, exp_sem, step, z, g_es, d_ed, d_bound):
    step(v.tensor_tensor(z, g_es, d_ed, ALU.add))
    step(v.scalar_tensor_tensor(out=z, in0=z, scalar=SLOPE, in1=z, op0=ALU.mult, op1=ALU.max))
    v.tensor_tensor(z, z, d_bound, ALU.subtract).then_inc(act_sem, 1)


def attend(nc, m, name, H, table):
    one = H == 1
    W = D + H
    ES = D + 1 if one else D
    C = D // H
    SHARE = 3
    with Phase(nc, name) as f:
        G = f.sb("G", [P, DEPTH, B, ES + H])
        ix = f.sb("ix", [P, DEPTH, B], U32)
        rows = f.sb("rows", [P, DEPTH, ROWE], U16)
        M = None if one else f.sb("M", [P, 2, B, W])
        dw = f.sb("dw", [P, 2, B])
        wt = f.sb("wt", [P, 2, B, H])
        S = f.sb("S", [P, 2, B, P])
        ST = f.sb("ST", [P, 2, B, P], BF16)
        tcol = f.sb("tcol", [P, T + 1])
        eb = f.sb("eb", [P, 2, B, 2 * H])
        z = f.sb("z", [P, 2, B, H])
        s_ix = [f.sem(f"ix{q}") for q in range(DEPTH)]
        s_rows = [f.sem(f"rows{q}") for q in range(DEPTH)]
        s_rowsin = [f.sem(f"rowsin{q}") for q in range(DEPTH)]
        s_dready = f.sem("dready")
        s_ready = f.sem("ready")
        s_free = f.sem("free")
        s_turn = f.sem("turn")
        s_col = f.sem("col")
        s_ST = f.sem("ST")
        s_ed = f.sem("ed")
        s_v = f.sem("v")
        s_z = f.sem("z")
        s_e = f.sem("e")
        s_w = f.sem("w")
        s_dw = f.sem("dw")
        s_S = f.sem("S")
        s_msg = f.sem("msg")
        s_mm = f.sem("mm")
        s_add = f.sem("add")
        with nc.Block() as block:

            @block.sync
            def _(sp):
                feed(sp, m, ix, s_ix, s_rows, s_ready, s_mm, 2, s_free, rows, s_rowsin, s_dready)

            @block.gpsimd
            def _(pool):
                gather_rows(pool, G, ix, table, s_ix, s_rows, s_turn)

            @block.scalar
            def _(act):
                turns = visit_turns(act, m)
                with act.Fori(0, turns) as i:
                    if not one:
                        _, blk = visit_turn(nc, act, m, i)
                    for p in range(2):
                        n = 2 * i + p
                        act.wait_ge(s_z, n + 1)
                        act.wait_ge(s_mm, n + 1)
                        if one:
                            act.activation(wt[:, p, :, :], z[:, p, :, :], ACT.Exp).then_inc(s_w, 1)
                            continue
                        act.activation(wt[:, p, :, :], z[:, p, :, :], ACT.Exp).then_inc(s_e, 1)
                        act.wait_ge(s_e, n + 1)
                        act.copy(M[:, p, :, D:W], wt[:, p, :, :])
                        q = blk[p] % DEPTH
                        for j in range(SHARE):
                            for h in range(H):
                                ins = act.activation(M[:, p, j:j + 1, C * h:C * h + C], G[:, ds(q, 1), j, C * h:C * h + C],
                                                     ACT.Copy, scale=wt[:, p, j, h:h + 1])
                        ins.then_inc(s_w, 1)

            @block.vector
            def _(v):
                v.tensor_scalar(tcol[:], m.iota[:, 0:(T + 1) * P:P], m.pcol[:, 0:1], None, ALU.add).then_inc(s_col, 1)
                v.wait_ge(s_col, 1)
                v.sem_inc(s_add, 1)

                def turned(n, p, t, b):
                    v.wait_ge(s_dready, b + 1)
                    v.tensor_scalar(ST[:, p, :, :].rearrange("p j e -> p (j e)"),
                                    rows[:, ds(b % DEPTH, 1), :].rearrange("p o e -> p (o e)"),
                                    tcol[:, ds(t, 1)], None, ALU.is_equal).then_inc(s_ST, 1)

                def score1(n, p):
                    v.wait_ge(s_ed, n + 1)
                    v.tensor_reduce(eb[:, p, :, :], m.ps[:, 2 + p, 0:B * 6 * H].rearrange("p (j k c) -> p j c k", j=B, k=3),
                                    X_, ALU.add).then_inc(s_v, 1)

                def score2(n, p, b):
                    v.wait_ge(s_v, 4 * n + 1)
                    v.wait_ge(s_ready, b + 1)
                    es = G[:, ds(b % DEPTH, 1), :, ES:ES + H].rearrange("p o j h -> p (o j) h")
                    v.tensor_tensor(z[:, p, :, :], es, eb[:, p, :, 0:H], ALU.add).then_inc(s_v, 1)

                def score3(n, p):
                    v.wait_ge(s_v, 4 * n + 2)
                    zp = z[:, p, :, :]
                    v.scalar_tensor_tensor(out=zp, in0=zp, scalar=SLOPE, in1=zp, op0=ALU.mult, op1=ALU.max).then_inc(s_v, 1)

                def score4(n, p):
                    v.wait_ge(s_v, 4 * n + 3)
                    zp = z[:, p, :, :]
                    v.tensor_tensor(zp, zp, eb[:, p, :, H:2 * H], ALU.subtract).then_inc(s_v, 1)

                def score5(n, p):
                    v.wait_ge(s_v, 4 * n + 4)
                    zp = z[:, p, :, :]
                    v.tensor_scalar(zp, zp, 0.0, None, ALU.min).then_inc(s_z, 1)

                def visit(n, p, t, b, b_next, t_after, b_after, t_last):
                    dst = m.dw[:, ds(b, 1), 0:1, :].rearrange("p o a j -> p (o a j)")
                    if one:
                        score1(n, p)
                        v.wait_ge(s_mm, n + 1)
                        v.tensor_copy(dw[:, p, :], dst).then_inc(s_dw, 1)
                        score2(n, p, b)
                        score3(n, p)
                        score4(n, p)
                        score5(n, p)
                        turned(n + 2, p, t_after, b_after)
                        v.wait_ge(s_dw, n + 1)
                        v.wait_ge(s_w, n + 1)
                        for j in range(B):
                            ins = v.tensor_scalar(S[:, p, j, :], m.iota[:, ds(P * t, P)], dw[:, p, j:j + 1],
                                                  wt[:, p, j, 0:1], ALU.is_equal, ALU.mult)
                        ins.then_inc(s_S, 1)
                        if t_last is not None:
                            add(n - 1, 1 - p, t_last)
                        return
                    score1(n + 1, 1 - p)
                    v.wait_ge(s_mm, n + 1)
                    io = m.iota[:, ds(P * t, P)].rearrange("p (o c) -> p o c", o=1).broadcast_to([P, B, P])
                    v.tensor_tensor(S[:, p, :, :], io, dup(dst, P), ALU.is_equal).then_inc(s_S, 1)
                    score2(n + 1, 1 - p, b_next)
                    turned(n + 2, p, t_after, b_after)
                    score3(n + 1, 1 - p)
                    v.wait_ge(s_e, n + 1)
                    R = B - SHARE
                    g4 = G[:, ds(b % DEPTH, 1), SHARE:B, 0:D].rearrange("p o j (h c) -> p (o j) h c", h=H)
                    m4 = M[:, p, SHARE:B, 0:D].rearrange("p j (h c) -> p j h c", h=H)
                    w4 = wt[:, p, SHARE:B, :].rearrange("p j (h o) -> p j h o", o=1).broadcast_to([P, R, H, C])
                    v.tensor_tensor(m4, g4, w4, ALU.mult).then_inc(s_msg, 1)
                    score4(n + 1, 1 - p)
                    if t_last is not None:
                        add(n - 1, 1 - p, t_last)
                    score5(n + 1, 1 - p)

                def add(n, p, t):
                    v.wait_ge(s_mm, n + 3)
                    v.wait_ge(s_add, n + 1)
                    v.tensor_tensor(m.ACCX[:, ds(t, 1), 0:W], m.ACCX[:, ds(t, 1), 0:W],
                                    m.ps[:, p:p + 1, 0:W], ALU.add).then_inc(s_add, 1)

                t, b = visit_turn(nc, v, m, 0)
                turned(0, 0, t[1], b[0])
                turned(1, 1, t[2], b[1])
                if not one:
                    score1(0, 0)
                    score2(0, 0, b[0])
                    score3(0, 0)
                    score4(0, 0)
                    score5(0, 0)
                visit(0, 0, t[1], b[0], b[1], t[3], b[2], None)
                visit(1, 1, t[2], b[1], b[2], t[4], b[3], t[1])
                turns = visit_turns(v, m)
                with v.Fori(1, turns) as i:
                    t, b = visit_turn(nc, v, m, i)
                    visit(2 * i, 0, t[1], b[0], b[1], t[3], b[2], t[0])
                    visit(2 * i + 1, 1, t[2], b[1], b[2], t[4], b[3], t[1])
                t, b = visit_turn(nc, v, m, turns)
                add(2 * turns - 1, 1, t[0])

            @block.tensor
            def _(pe):
                pe.sem_inc(s_mm, 2)

                def find(n, p, t):
                    pe.wait_ge(s_ST, n + 1)
                    if n is not p:
                        pe.wait_ge(s_v, 4 * n - 7)
                    for j in range(B):
                        ins = pe.matmul(m.ps[:, 2 + p, j * 6 * H:(j + 1) * 6 * H], ST[:, p, j, :],
                                        m.EDB[:, ds(t, 1), 0:6 * H], start=True, stop=True)
                    ins.then_inc(s_ed, 1)

                def sums(n, p, b):
                    pe.wait_ge(s_S, n + 1)
                    if not one:
                        pe.wait_ge(s_msg, n + 1)
                        pe.wait_ge(s_w, n + 1)
                    if n is not p:
                        pe.wait_ge(s_add, n)
                    for j in range(B):
                        row = G[:, ds(b % DEPTH, 1), j, 0:W] if one else M[:, p, j, :]
                        ins = pe.matmul(m.ps[:, p, 0:W], S[:, p, j, :], row,
                                        start=(j == 0), stop=(j == B - 1))
                    ins.then_inc(s_mm, 1)

                t, b = visit_turn(nc, pe, m, 0)
                find(0, 0, t[1])
                find(1, 1, t[2])
                find(2, 0, t[3])
                sums(0, 0, b[0])
                find(3, 1, t[4])
                sums(1, 1, b[1])
                turns = visit_turns(pe, m)
                with pe.Fori(1, turns) as i:
                    t, b = visit_turn(nc, pe, m, i)
                    find(2 * i + 2, 0, t[3])
                    sums(2 * i, 0, b[0])
                    find(2 * i + 3, 1, t[4])
                    sums(2 * i + 1, 1, b[1])


def load_expert(eng, A, w, q, e, sem):
    w1 = A["L0_ffn_w1"].rearrange("e (k p) f -> p e k f", p=P)
    w2 = A["L0_ffn_w2"].rearrange("e (k p) f -> p e k f", p=P)
    eng.dma_start(w[0][:, q, :, :], w1[:, ds(e, 1), :, :].rearrange("p o k f -> p (o k) f")).then_inc(sem, 16)
    eng.dma_start(w[1][:, q, :, :], w2[:, ds(e, 1), :, :].rearrange("p o k f -> p (o k) f")).then_inc(sem, 16)


def route(nc, m, A, w):
    with Phase(nc, "rt") as f:
        bias = f.sb("bias", [P, NEXP])
        L = f.sb("L", [P, T, NEXP])
        OH = f.sb("OH", [P, T, NEXP])
        tmp = f.sb("tmp", [P, T, NEXP])
        tot = f.sb("tot", [P, T, NEXP])
        top = f.sb("top", [P, T])
        node = f.sb("node", [P, T])
        pos = f.sb("pos", [P, T])
        ex = f.sb("ex", [P, T])
        kept = f.sb("kept", [P, T])
        a = f.sb("a", [P, T])
        idx = f.sb("idx", [P, T], U32)
        s_dma = f.sem("dma")
        s_v = f.sem("v")
        s_io = f.sem("io")
        s_l = f.sem("l")
        s_e = f.sem("e")
        s_oh = f.sem("oh")
        s_mm = f.sem("mm")
        s_idx = f.sem("idx")
        s_put = f.sem("put")
        s_ew = f.sem("ew")
        with nc.Block() as block:

            @block.sync
            def _(sp):
                sp.dma_start(bias[:], A["L0_ffn_gate_b"].partition_broadcast(P)).then_inc(s_dma, 16)
                for q in range(2):
                    load_expert(sp, A, w, q, q, s_ew)
                sp.wait_ge(s_ew, 64)

            @block.gpsimd
            def _(pool):
                pool.iota(node[:], [[P, T]], base=NEXP * CAP, channel_multiplier=1,
                          allow_small_or_imprecise_dtypes=True).then_inc(s_io, 1)
                pool.wait_ge(s_idx, 1)
                for t in range(T):
                    pool.indirect_dma_start(
                        out=m.slots[:, :], out_offset=bass.IndirectOffsetOnAxis(ap=idx[:, t:t + 1], axis=0),
                        in_=m.XN[:, t, :], in_offset=None).then_inc(s_put, 16)
                pool.wait_ge(s_put, 16 * T)

            @block.scalar
            def _(act):
                act.wait_ge(s_l, 1)
                act.activation(tmp[:], L[:], ACT.Exp).then_inc(s_e, 1)

            @block.tensor
            def _(pe):
                pe.wait_ge(s_oh, 1)
                oh = OH[:].rearrange("p t e -> p (t e)")
                pe.matmul(m.ps[:, 0, 0:T * NEXP], m.upper[:], oh, start=True, stop=True).then_inc(s_mm, 1)
                pe.matmul(m.ps[:, 1, 0:T * NEXP], m.ones[:], oh, start=True, stop=True).then_inc(s_mm, 1)

            @block.vector
            def _(v):
                step = Steps(v, s_v)
                v.wait_ge(s_dma, 16)
                eb = [P, T, NEXP]
                step(v.tensor_tensor(L[:], m.ACC[:, :, 0:NEXP],
                                     bias[:].rearrange("p (o e) -> p o e", o=1).broadcast_to(eb), ALU.add))
                step(v.tensor_reduce(top[:], L[:], X_, ALU.max))
                step(v.tensor_tensor(OH[:], L[:], dup(top[:], NEXP), ALU.is_equal))
                io8 = m.iota[:, 0:NEXP].rearrange("p (o e) -> p o e", o=1).broadcast_to(eb)
                step(v.scalar_tensor_tensor(out=OH[:], in0=OH[:], scalar=-float(NEXP), in1=io8, op0=ALU.mult, op1=ALU.add))
                step(v.tensor_reduce(ex[:], OH[:], X_, ALU.min))
                step(v.tensor_tensor(OH[:], OH[:], dup(ex[:], NEXP), ALU.is_equal))
                v.sem_inc(s_oh, 1)
                step(v.tensor_scalar(ex[:], ex[:], float(NEXP), None, ALU.add))
                step(v.tensor_tensor(L[:], L[:], dup(top[:], NEXP), ALU.subtract))
                v.sem_inc(s_l, 1)
                v.wait_ge(s_e, 1)
                step(v.tensor_reduce(a[:], tmp[:], X_, ALU.add))
                step(v.reciprocal(m.gscale[:], a[:]))
                v.wait_ge(s_mm, 2)
                p0 = m.ps[:, 0, 0:T * NEXP].rearrange("p (t e) -> p t e", e=NEXP)
                p1 = m.ps[:, 1, 0:T * NEXP].rearrange("p (t e) -> p t e", e=NEXP)
                step(v.tensor_copy(tot[:], p1))
                for e in range(NEXP):
                    ins = v.tensor_tensor_scan(tmp[:, :, e], m.ones[:, 0:T], tot[:, :, e], 0.0, ALU.mult, ALU.add)
                step(ins)
                step(v.tensor_tensor(tmp[:], tmp[:], tot[:], ALU.subtract))
                step(v.tensor_tensor(tmp[:], tmp[:], p0, ALU.add))
                step(v.tensor_tensor(tmp[:], tmp[:], OH[:], ALU.mult))
                step(v.tensor_reduce(pos[:], tmp[:], X_, ALU.add))
                step(v.tensor_scalar(kept[:], pos[:], float(CAP), None, ALU.is_le))
                step(v.tensor_tensor(m.gscale[:], m.gscale[:], kept[:], ALU.mult))
                step(v.tensor_scalar(ex[:], ex[:], float(CAP), -1.0, ALU.mult, ALU.add))
                step(v.scalar_tensor_tensor(out=a[:], in0=pos[:], scalar=float(CAP), in1=ex[:], op0=ALU.min, op1=ALU.add))
                step(v.tensor_copy(m.gidx[:], a[:]))
                v.wait_ge(s_io, 1)
                step(v.tensor_tensor(a[:], a[:], node[:], ALU.subtract))
                step(v.tensor_tensor(a[:], a[:], kept[:], ALU.mult))
                step(v.tensor_tensor(a[:], a[:], node[:], ALU.add))
                v.tensor_copy(idx[:], a[:]).then_inc(s_idx, 1)


def experts(nc, m, A, w):
    FT = HID // P
    with Phase(nc, "ex") as f:
        w1, w2 = w
        xin = f.sb("xin", [P, 2, 4, D])
        xt = f.sb("xt", [P, 2, 2, 512])
        b2 = f.sb("b2", [P, NEXP * D])
        b1r = f.sb("b1r", [NEXP * FT, P])
        b1 = f.sb("b1", [P, NEXP * FT])
        Y = f.sb("Y", [P, 2, 4, D])
        hid = m.ACCX[:].rearrange("p t c -> p (t c)")[:, 0:FT * 512].rearrange("p (f n) -> p f n", f=FT)
        s_b = f.sem("b")
        s_bt = f.sem("bt")
        s_bc = f.sem("bc")
        s_in = [f.sem(f"in{q}") for q in range(2)]
        s_w = [f.sem(f"w{q}") for q in range(2)]
        s_tr = f.sem("tr")
        s_xt = f.sem("xt")
        s_up = f.sem("up")
        s_h = f.sem("h")
        s_dn = f.sem("dn")
        s_y = f.sem("y")
        s_turn = f.sem("turn")
        s_st = [f.sem(f"st{q}") for q in range(2)]
        last = CAP - 3 * P
        with nc.Block() as block:

            @block.sync
            def _(sp):
                sp.dma_start(b2[:], A["L0_ffn_b2"].rearrange("e d -> (e d)").partition_broadcast(P)).then_inc(s_b, 16)
                sp.dma_start(b1r[:], A["L0_ffn_b1"].rearrange("e (f p) -> (e f) p", p=P)).then_inc(s_b, 16)
                def slots(q, e):
                    sp.dma_start(xin[:, q, :, :], m.slots[ds(CAP * e, 4 * P), :].rearrange("(s p) d -> p s d", p=P)).then_inc(s_in[q], 16)

                def store(q, e):
                    sp.wait_ge(s_y, 4 * e + 8)
                    sp.sem_inc(s_turn, 1)
                    sp.dma_start(m.yslots[ds(CAP * e, 3 * P), :].rearrange("(s p) d -> p s d", p=P), Y[:, q, 0:3, :]).then_inc(s_st[q], 16)
                    sp.dma_start(m.yslots[ds(CAP * e + 3 * P, last), :], Y[0:last, q, 3, :]).then_inc(s_st[q], 16)

                for q in range(2):
                    sp.sem_inc(s_w[q], 16)
                    sp.sem_inc(s_st[q], 16)
                for q in range(2):
                    slots(q, q)
                with sp.Fori(0, NEXP // 2 - 1) as i:
                    for q in range(2):
                        e = 2 * i + q
                        sp.wait_ge(s_dn, 4 * e + 5)
                        sp.sem_inc(s_turn, 1)
                        slots(q, e + 2)
                        load_expert(sp, A, w, q, e + 2, s_w[q])
                        store(q, e)
                for q in range(2):
                    store(q, NEXP - 2 + q)
                for q in range(2):
                    sp.wait_ge(s_st[q], 32 * (NEXP // 2) + 16)

            @block.tensor
            def _(pe):
                pe.wait_ge(s_b, 32)
                pe.transpose(m.ps[:, 7, 0:NEXP * FT], b1r[:], m.ident[0:NEXP * FT, 0:NEXP * FT]).then_inc(s_bt, 1)
                pe.sem_inc(s_up, 2)

                def turn(e, q, i):
                    pe.wait_ge(s_in[q], 16 * (i + 1))
                    pe.wait_ge(s_xt, 2 * e)
                    for k in range(2):
                        for s in range(4):
                            ins = pe.transpose(m.ps[:, k, s * P:(s + 1) * P], xin[:, q, s, k * P:(k + 1) * P], m.ident[:])
                        ins.then_inc(s_tr, 1)

                def up(e, q, i):
                    pe.wait_ge(s_w[q], 32 * i + 16)
                    pe.wait_ge(s_xt, 2 * e + 2)
                    for g in range(FT):
                        pe.wait_ge(s_h, FT * e + g + 1)
                        for k in range(2):
                            ins = pe.matmul(m.ps[:, 2 + g % 2, 0:CAP], w1[:, q, k, g * P:(g + 1) * P], xt[:, q, k, 0:CAP],
                                            start=(k == 0), stop=(k == 1))
                        ins.then_inc(s_up, 1)

                def down(e, q):
                    pe.wait_ge(s_h, FT * e + FT + 2)
                    for s in range(4):
                        pe.wait_ge(s_y, 4 * e + s + 1)
                        for g in range(FT):
                            ins = pe.matmul(m.ps[:, 4 + s, 0:D], hid[:, g, s * P:(s + 1) * P], w2[:, q, g, :],
                                            start=(g == 0), stop=(g == FT - 1))
                        ins.then_inc(s_dn, 1)

                pe.sem_inc(s_dn, 1)
                turn(0, 0, 0)
                with pe.Fori(0, NEXP // 2 - 1) as i:
                    for q in range(2):
                        e = 2 * i + q
                        up(e, q, i)
                        turn(e + 1, 1 - q, i + q)
                        down(e, q)
                up(NEXP - 2, 0, NEXP // 2 - 1)
                turn(NEXP - 1, 1, NEXP // 2 - 1)
                down(NEXP - 2, 0)
                up(NEXP - 1, 1, NEXP // 2 - 1)
                down(NEXP - 1, 1)

            @block.scalar
            def _(act):
                act.wait_ge(s_bt, 1)
                act.copy(b1[:], m.ps[:, 7, 0:NEXP * FT]).then_inc(s_bc, 1)
                act.wait_ge(s_bc, 1)
                act.sem_inc(s_h, 2)

                def turned(e, q):
                    for k in range(2):
                        act.wait_ge(s_tr, 2 * e + k + 1)
                        act.copy(xt[:, q, k, :], m.ps[:, k, :]).then_inc(s_xt, 1)

                def hidden(e):
                    act.wait_ge(s_dn, 4 * e + 1)
                    for g in range(FT):
                        act.wait_ge(s_up, FT * e + g + 3)
                        act.activation(hid[:, g, 0:CAP], m.ps[:, 2 + g % 2, 0:CAP], ACT.Relu,
                                       bias=b1[:, ds(FT * e + g, 1)]).then_inc(s_h, 1)

                turned(0, 0)
                with act.Fori(0, NEXP // 2 - 1) as i:
                    for q in range(2):
                        hidden(2 * i + q)
                        turned(2 * i + q + 1, 1 - q)
                hidden(NEXP - 2)
                turned(NEXP - 1, 1)
                hidden(NEXP - 1)

            @block.vector
            def _(v):
                v.wait_ge(s_b, 32)
                v.sem_inc(s_y, 4)
                with v.Fori(0, NEXP // 2) as i:
                    for q in range(2):
                        e = 2 * i + q
                        v.wait_ge(s_st[q], 32 * i + 16)
                        for s in range(4):
                            v.wait_ge(s_dn, 4 * e + s + 2)
                            v.tensor_tensor(Y[:, q, s, :], m.ps[:, 4 + s, 0:D], b2[:, ds(D * e, D)], ALU.add).then_inc(s_y, 1)


def gate_attend_and_experts(nc, m, A):
    H, HC = GH, 16
    W = HC + H
    RING = 4
    FT = HID2 // P
    CW = U * P
    HW = CW // 2
    NU = 2 * FT
    assert FNBLK == TURNS * KEXP and KEXP % 2 == 0
    with Phase(nc, "ga") as f:
        G = f.sb("G", [P, KEXP, FB, W])
        DD = f.sb("DD", [P, KEXP, FB, 2 * H])
        z = f.sb("z", [P, FB, H])
        ixs = f.sb("ixs", [P, KEXP, FB], U32)
        ixd = f.sb("ixd", [P, KEXP, FB], U32)
        lo = f.sb("lo", [P, KEXP, FB])
        hi = f.sb("hi", [P, KEXP, FB])
        S = f.sb("S", [P, FB, P])
        hot = f.sb("hot", [P, FB, T])
        R = f.sb("R", [P, RING, T, W])
        zz = f.sb("zz", [P, T * W])
        w1 = f.sb("w1", [P, KEXP, 2, HID2])
        w2 = f.sb("w2", [P, KEXP, FT, D])
        b2 = f.sb("b2", [P, KEXP, D])
        b1r = f.sb("b1r", [KEXP * FT, P])
        b1 = f.sb("b1", [P, KEXP * FT])
        hid = f.sb("hid", [P, 2, FT, CW])
        y = f.sb("y", [P, 2, U, D])
        s_stage = f.sem("stage")
        s_rows = [f.sem(f"rows{q}") for q in range(KEXP)]
        s_z = f.sem("z")
        s_w = f.sem("w")
        s_m = f.sem("m")
        s_S = f.sem("S")
        s_R = f.sem("R")
        s_mm = f.sem("mm")
        s_turn = f.sem("turn")
        s_v = f.sem("v")
        s_zero = f.sem("zero")
        s_end = f.sem("end")
        s_in = f.sem("in")
        s_bt = f.sem("bt")
        s_bc = f.sem("bc")
        s_up = f.sem("up")
        s_h = f.sem("h")
        s_dn = f.sem("dn")
        s_y = f.sem("y")
        s_st = [f.sem(f"st{q}") for q in range(2)]
        with nc.Block() as block:

            @block.sync
            def _(sp):
                sp.dma_start(b1r[:], A["L1_ffn_b1"].rearrange("e (f p) -> (e f) p", p=P)).then_inc(s_in, 16)
                for e in range(KEXP):
                    sp.dma_start(w1[:, e, :, :], A["L1_ffn_W1"][e].rearrange("(k p) n -> p k n", p=P)).then_inc(s_in, 16)
                    sp.dma_start(w2[:, e, :, :], A["L1_ffn_W2"][e].rearrange("(k p) n -> p k n", p=P)).then_inc(s_in, 16)
                    sp.dma_start(b2[:, e, :], A["L1_ffn_b2"][e].partition_broadcast(P)).then_inc(s_in, 16)
                for q in range(2):
                    sp.sem_inc(s_st[q], 16)
                with sp.Fori(0, TURNS) as i:
                    for e in range(KEXP):
                        n = KEXP * i + e
                        sp.wait_ge(s_y, U * n + 2 * U)
                        sp.sem_inc(s_turn, 1)
                        sp.dma_start(m.ymix[e][ds(CW * i, CW), :].rearrange("(t p) d -> p t d", p=P),
                                     y[:, e % 2, :, :]).then_inc(s_st[e % 2], 16)
                for q in range(2):
                    sp.wait_ge(s_st[q], 16 * (FNBLK // 2) + 16)

            @block.scalar
            def _(act):
                def stage(b, q, waits=True):
                    if waits:
                        act.wait_ge(s_mm, FB * b - FB)
                    act.copy(ixs[:, q, :], m.fsrc[:, :, ds(b, 1)]).then_inc(s_stage, 1)
                    act.copy(ixd[:, q, :], m.fdst[:, :, ds(b, 1)]).then_inc(s_stage, 1)
                    act.copy(lo[:, q, :], m.flo[:, :, ds(b, 1)]).then_inc(s_stage, 1)
                    act.copy(hi[:, q, :], m.fhi[:, :, ds(b, 1)]).then_inc(s_stage, 1)

                def first_layer(n, e):
                    for k in range(NU):
                        act.wait_ge(s_up, NU * n + k + 3)
                        g_, hf = k // 2, k % 2
                        act.activation(hid[:, e % 2, g_, hf * HW:(hf + 1) * HW], m.ps[:, 1 + k % 2, 0:HW], ACT.Gelu,
                                       bias=b1[:, FT * e + g_:FT * e + g_ + 1]).then_inc(s_h, 1)

                def weights(b, q):
                    act.wait_ge(s_z, b + 1)
                    act.activation(G[:, q, :, HC:W], z[:], ACT.Exp).then_inc(s_w, 1)

                for b in range(KEXP - 1):
                    stage(b, b, waits=False)
                act.wait_ge(s_bt, 1)
                act.copy(b1[:], m.ps[:, 7, 0:KEXP * FT]).then_inc(s_bc, 1)
                act.wait_ge(s_bc, 1)
                act.sem_inc(s_h, 2)

                def step(n, e):
                    first_layer(n, e)
                    stage(n + 2, (e + 2) % KEXP)
                    weights(n, e)

                first_layer(0, 0)
                weights(0, 0)
                for e in range(1, KEXP):
                    step(e, e)
                with act.Fori(1, TURNS - 1) as i:
                    for e in range(KEXP):
                        step(KEXP * i + e, e)
                for e in range(KEXP):
                    n = FNBLK - KEXP + e
                    if n + 2 < FNBLK:
                        step(n, e)
                    else:
                        first_layer(n, e)
                        weights(n, e)

            @block.gpsimd
            def _(pool):
                with pool.Fori(0, TURNS) as i:
                    for q in range(KEXP):
                        pool.wait_ge(s_stage, 4 * (KEXP * i + q) + 4)
                        pool.sem_inc(s_turn, 1)
                        for j in range(FB):
                            pool.indirect_dma_start(
                                out=G[:, q, j, :], out_offset=None, in_=m.gtable[:, :],
                                in_offset=bass.IndirectOffsetOnAxis(ap=ixs[:, q, j:j + 1], axis=0),
                            ).then_inc(s_rows[q], 16)
                            pool.indirect_dma_start(
                                out=DD[:, q, j, :], out_offset=None, in_=m.gedu[:, :],
                                in_offset=bass.IndirectOffsetOnAxis(ap=ixd[:, q, j:j + 1], axis=0),
                            ).then_inc(s_rows[q], 16)

            @block.vector
            def _(v):
                v.memset(zz[:], 0.0).then_inc(s_zero, 1)
                v.sem_inc(s_y, U)

                def scores(b, q, turn):
                    v.wait_ge(s_rows[q], 32 * FB * (turn + 1))
                    edge_weights(v, s_z, s_w, Steps(v, s_v, 2 * b), z[:], G[:, q, :, HC:W],
                                 DD[:, q, :, 0:H], DD[:, q, :, H:2 * H])

                def edges(b, q):
                    v.wait_ge(s_stage, 4 * b + 4)
                    v.wait_ge(s_mm, FB * b + 2 * FB)
                    io = m.iota[:, 0:P].rearrange("p (o c) -> p o c", o=1).broadcast_to([P, FB, P])
                    v.tensor_tensor(S[:], io, dup(lo[:, q, :], P), ALU.is_equal).then_inc(s_S, 1)
                    io = m.iota[:, 0:T].rearrange("p (o c) -> p o c", o=1).broadcast_to([P, FB, T])
                    v.tensor_tensor(hot[:], io, dup(hi[:, q, :], T), ALU.is_equal).then_inc(s_S, 1)
                    v.wait_ge(s_w, b + 1)
                    g4 = G[:, q, :, 0:HC].rearrange("p j (h c) -> p j h c", h=H)
                    w4 = G[:, q, :, HC:W].rearrange("p j (h o) -> p j h o", o=1).broadcast_to([P, FB, H, HC // H])
                    v.tensor_tensor(g4, g4, w4, ALU.mult).then_inc(s_m, 1)
                    v.wait_ge(s_m, b + 1)
                    v.wait_ge(s_S, 2 * b + 2)
                    for j in range(FB):
                        if j >= RING:
                            v.wait_ge(s_mm, FB * b + 2 * FB + j - RING + 1)
                        val = G[:, q, j:j + 1, :].broadcast_to([P, T, W])
                        v.tensor_tensor(R[:, j % RING, :, :], dup(hot[:, j, :], W), val, ALU.mult).then_inc(s_R, 1)

                def second_layer(n, e, turn):
                    if e >= 2:
                        v.wait_ge(s_st[e % 2], 16 * (2 * turn + 2))
                    else:
                        v.wait_ge(s_st[e % 2], 32 * turn + 16)
                    for j in range(U):
                        v.wait_ge(s_dn, U * n + j + 1)
                        v.tensor_tensor(y[:, e % 2, j, :], m.ps[:, 3 + j, 0:D], b2[:, e, :], ALU.add).then_inc(s_y, 1)

                v.wait_ge(s_in, 16 * (1 + 3 * KEXP))
                v.wait_ge(s_bc, 1)

                def step(n, e, turn):
                    edges(n - 1, (e - 1) % KEXP)
                    scores(n, e, turn)
                    second_layer(n, e, turn)

                second_layer(0, 0, 0)
                scores(0, 0, 0)
                for e in range(1, KEXP):
                    step(e, e, 0)
                with v.Fori(1, TURNS) as i:
                    for e in range(KEXP):
                        step(KEXP * i + e, e, i)
                edges(FNBLK - 1, KEXP - 1)

            @block.tensor
            def _(pe):
                pe.sem_inc(s_mm, 2 * FB)
                pe.sem_inc(s_up, 2)
                pe.wait_ge(s_zero, 1)
                pe.matmul(m.ps[:, 0, 0:T * W], zz[:, 0:P], zz[:], start=True, stop=False)
                pe.wait_ge(s_in, 16 * (1 + 3 * KEXP))
                pe.transpose(m.ps[:, 7, 0:KEXP * FT], b1r[:], m.ident[0:KEXP * FT, 0:KEXP * FT]).then_inc(s_bt, 1)

                def first_layer(n, e, i):
                    for k_ in range(NU):
                        g_, hf = k_ // 2, k_ % 2
                        pe.wait_ge(s_h, NU * n + k_ + 1)
                        for k in range(2):
                            ins = pe.matmul(m.ps[:, 1 + k_ % 2, 0:HW], w1[:, e, k, g_ * P:(g_ + 1) * P],
                                            m.XT[:, k, ds(CW * i + HW * hf, HW)], start=(k == 0), stop=(k == 1))
                        ins.then_inc(s_up, 1)

                def edges(b):
                    for j in range(FB):
                        pe.wait_ge(s_R, FB * b + j + 1)
                        pe.matmul(m.ps[:, 0, 0:T * W], S[:, j, :], R[:, j % RING, :, :].rearrange("p t w -> p (t w)"),
                                  start=False, stop=False).then_inc(s_mm, 1)

                def second_layer(n, e):
                    pe.wait_ge(s_h, NU * n + NU + 2)
                    for j in range(U):
                        pe.wait_ge(s_y, U * n + j + 1)
                        for g_ in range(FT):
                            ins = pe.matmul(m.ps[:, 3 + j, 0:D], hid[:, e % 2, g_, j * P:(j + 1) * P], w2[:, e, g_, :],
                                            start=(g_ == 0), stop=(g_ == FT - 1))
                        ins.then_inc(s_dn, 1)

                def step(n, e, i):
                    first_layer(n, e, i)
                    edges(n - 1)
                    second_layer(n, e)

                first_layer(0, 0, 0)
                second_layer(0, 0)
                for e in range(1, KEXP):
                    step(e, e, 0)
                with pe.Fori(1, TURNS) as i:
                    for e in range(KEXP):
                        step(KEXP * i + e, e, i)
                edges(FNBLK - 1)
                pe.matmul(m.ps[:, 0, 0:T * W], zz[:, 0:P], zz[:], start=False, stop=True).then_inc(s_end, 1)
        with nc.Block() as block:

            @block.vector
            def _(v):
                a = m.ACC[:, :, 0:W]
                v.tensor_tensor(a, a, m.ps[:, 0, 0:T * W].rearrange("p (t w) -> p t w", w=W), ALU.add).then_inc(s_v, 1)


def load_results(eng, m, y, i, sem):
    for e in range(KEXP):
        eng.dma_start(y[:, i % 2, e, :, :], m.ymix[e][U * P * i:U * P * (i + 1), :].rearrange("(t p) d -> p t d", p=P)).then_inc(sem, 16)


def gates(nc, m, A, y):
    C = 16
    with Phase(nc, "gt") as f:
        vec = f.sb("vec", [P, 3, C])
        a = f.sb("a", [P, T, C])
        b = f.sb("b", [P, T, C])
        mu = f.sb("mu", [P, T])
        sd = f.sb("sd", [P, T])
        den = f.sb("den", [P, T, GH])
        sc = f.sb("sc", [P, T, KEXP])
        o1 = f.sb("o1", [P, T, KEXP])
        o2 = f.sb("o2", [P, T, KEXP])
        m1 = f.sb("m1", [P, T])
        m2 = f.sb("m2", [P, T])
        k1 = f.sb("k1", [P, T])
        s_dma = f.sem("dma")
        s_v = f.sem("v")
        s_var = f.sem("var")
        s_sd = f.sem("sd")
        s_d = f.sem("d")
        s_e = f.sem("e")
        s_y = f.sem("y")
        with nc.Block() as block:

            @block.sync
            def _(sp):
                for k, name in enumerate(("L1_ffn_b_gat", "L1_ffn_ln_gamma", "L1_ffn_ln_beta")):
                    sp.dma_start(vec[:, k, :], A[name].partition_broadcast(P)).then_inc(s_dma, 16)
                for i in range(2):
                    load_results(sp, m, y, i, s_y)
                sp.wait_ge(s_y, 2 * KEXP * 16)

            @block.scalar
            def _(act):
                act.wait_ge(s_var, 1)
                act.activation(sd[:], sd[:], ACT.Sqrt).then_inc(s_sd, 1)
                act.wait_ge(s_d, 1)
                act.activation(m2[:], m2[:], ACT.Exp).then_inc(s_e, 1)

            @block.vector
            def _(v):
                step = Steps(v, s_v)

                def row(k):
                    return vec[:, k:k + 1, :].broadcast_to([P, T, C])

                step(v.tensor_scalar(den[:], m.ACC[:, :, C:C + GH], 1e-16, None, ALU.add))
                step(v.reciprocal(den[:], den[:]))
                step(v.tensor_tensor(a[:].rearrange("p t (h c) -> p t h c", h=GH),
                                     m.ACC[:, :, 0:C].rearrange("p t (h c) -> p t h c", h=GH),
                                     den[:].rearrange("p t (h o) -> p t h o", o=1).broadcast_to([P, T, GH, C // GH]), ALU.mult))
                v.wait_ge(s_dma, 48)
                step(v.tensor_tensor(a[:], a[:], row(0), ALU.add))
                step(v.tensor_reduce(mu[:], a[:], X_, ALU.add))
                step(v.tensor_scalar(mu[:], mu[:], 1.0 / C, None, ALU.mult))
                step(v.tensor_tensor(a[:], a[:], dup(mu[:], C), ALU.subtract))
                step(v.tensor_tensor(b[:], a[:], a[:], ALU.mult))
                step(v.tensor_reduce(sd[:], b[:], X_, ALU.add))
                step(v.tensor_scalar(sd[:], sd[:], 1.0 / C, EPS, ALU.mult, ALU.add))
                v.sem_inc(s_var, 1)
                v.wait_ge(s_sd, 1)
                step(v.reciprocal(sd[:], sd[:]))
                step(v.tensor_tensor(a[:], a[:], dup(sd[:], C), ALU.mult))
                step(v.tensor_tensor(a[:], a[:], row(1), ALU.mult))
                step(v.tensor_tensor(a[:], a[:], row(2), ALU.add))
                step(v.tensor_reduce(sc[:], a[:].rearrange("p t (h e) -> p t e h", h=GH), X_, ALU.add))
                step(v.tensor_scalar(sc[:], sc[:], 1.0 / GH, None, ALU.mult))
                io4 = m.iota[:, 0:KEXP].rearrange("p (o e) -> p o e", o=1).broadcast_to([P, T, KEXP])

                def first_best(o, best):
                    step(v.tensor_reduce(best[:], sc[:], X_, ALU.max))
                    step(v.tensor_tensor(o[:], sc[:], dup(best[:], KEXP), ALU.is_equal))
                    step(v.scalar_tensor_tensor(out=o[:], in0=o[:], scalar=-float(KEXP), in1=io4, op0=ALU.mult, op1=ALU.add))
                    step(v.tensor_reduce(k1[:], o[:], X_, ALU.min))
                    step(v.tensor_tensor(o[:], o[:], dup(k1[:], KEXP), ALU.is_equal))

                first_best(o1, m1)
                step(v.scalar_tensor_tensor(out=sc[:], in0=o1[:], scalar=NEG, in1=sc[:], op0=ALU.mult, op1=ALU.add))
                first_best(o2, m2)
                step(v.tensor_tensor(m2[:], m2[:], m1[:], ALU.subtract))
                v.sem_inc(s_d, 1)
                v.wait_ge(s_e, 1)
                step(v.tensor_scalar(m1[:], m2[:], 1.0, None, ALU.add))
                step(v.reciprocal(m1[:], m1[:]))
                step(v.tensor_tensor(m2[:], m2[:], m1[:], ALU.mult))
                step(v.tensor_tensor(o1[:], o1[:], dup(m1[:], KEXP), ALU.mult))
                step(v.tensor_tensor(o2[:], o2[:], dup(m2[:], KEXP), ALU.mult))
                step(v.tensor_tensor(m.gate[:], o1[:], o2[:], ALU.add))


def mix_experts(nc, m, y, out):
    CW = U * P
    with Phase(nc, "mx") as f:
        s_in = [f.sem(f"in{q}") for q in range(2)]
        s_x = f.sem("x")
        s_out = f.sem("out")
        with nc.Block() as block:

            @block.scalar
            def _(act):
                for i in range(2, TURNS):
                    act.wait_ge(s_x, KEXP * U * (i - 1))
                    load_results(act, m, y, i, s_in[i % 2])

            @block.vector
            def _(v):
                for i in range(TURNS):
                    if i >= 2:
                        v.wait_ge(s_in[i % 2], 16 * KEXP * (i // 2))
                    for e in range(KEXP):
                        for j in range(U):
                            t = U * i + j
                            if e:
                                v.wait_ge(s_x, KEXP * U * i + U * (e - 1) + j + 1)
                            v.scalar_tensor_tensor(out=m.X[:, t, :], in0=y[:, i % 2, e, j, :], scalar=m.gate[:, t, e:e + 1],
                                                   in1=m.X[:, t, :], op0=ALU.mult, op1=ALU.add).then_inc(s_x, 1)

            @block.sync
            def _(sp):
                for i in range(TURNS - 1):
                    sp.wait_ge(s_x, KEXP * U * (i + 1))
                    sp.dma_start(out[CW * i:CW * (i + 1), :].rearrange("(t p) d -> p t d", p=P), m.X[:, U * i:U * (i + 1), :]).then_inc(s_out, 16)
                sp.wait_ge(s_x, KEXP * T)
                sp.dma_start(out[(TURNS - 1) * CW:(T - 1) * P, :].rearrange("(t p) d -> p t d", p=P), m.X[:, (TURNS - 1) * U:T - 1, :]).then_inc(s_out, 16)
                sp.dma_start(out[(T - 1) * P:N, :], m.X[0:TAIL, T - 1, :]).then_inc(s_out, 16)
                sp.wait_ge(s_out, 16 * (TURNS + 1))


def store_x(nc, m, out):
    with Phase(nc, "end") as f:
        s = f.sem("s")
        with nc.Block() as block:

            @block.sync
            def _(sp):
                sp.dma_start(out[0:(T - 1) * P, :].rearrange("(t p) d -> p t d", p=P), m.X[:, 0:T - 1, :]).then_inc(s, 16)
                sp.dma_start(out[(T - 1) * P:N, :], m.X[0:TAIL, T - 1, :]).then_inc(s, 16)
                sp.wait_ge(s, 32)


def program(nc, A, out, upto=99):
    ctx = ExitStack()
    m = Memory()
    m.support = [nc.dram_tensor(f"support{k}", (NP_, D), F32).ap() for k in range(2)]
    m.drows = nc.dram_tensor("drows", (NBLK, ROWE), U16).ap()
    m.slots = nc.dram_tensor("slots", (NEXP * CAP + NP_, D), F32).ap()
    m.yslots = nc.dram_tensor("yslots", (NEXP * CAP, D), F32).ap()
    m.atable = [nc.dram_tensor(f"atable{k}", (NP_, D + h), F32).ap() for k, h in ((0, 4), (1, 2))]
    m.ymix = nc.dram_tensor("ymix", (KEXP, NP_, D), F32).ap()
    m.gtable = nc.dram_tensor("gtable", (NP_, 20), F32).ap()
    m.gedu = nc.dram_tensor("gedu", (NP_, 8), F32).ap()
    with ctx:
        alloc(nc, ctx, m)
        prepare(nc, m, A)
        project(nc, m, "p0", "ln", m.W["c1"], D, table=m.support[0])
        convolve(nc, m, "c0", m.support[0], A)
        project(nc, m, "p1", "acc", m.W["c2"], D, table=m.support[1])
        convolve(nc, m, "c1", m.support[1])
        project(nc, m, "route", "ln", m.W["gate"], NEXP, first="add")
        with nc.sbuf_tensor("ew1", [P, 2, 2, HID], F32) as ew1, nc.sbuf_tensor("ew2", [P, 2, HID // P, D], F32) as ew2:
            route(nc, m, A, (ew1, ew2))
            experts(nc, m, A, (ew1, ew2))
        project(nc, m, "p2", "ln", m.W["g1"], D + 4, heads=4, table=m.atable[0], first="combine")
        if upto == 2:
            return store_x(nc, m, out)
        self_loops(nc, m, "s2", D, 4, None, LOOPS)
        attend(nc, m, "t2", 4, m.atable[0])
        project(nc, m, "p3", "relu", m.W["g2"], D + 1, heads=1, table=m.atable[1], first="attention", gat=4,
                params=(A["L1_gnn_b1"], A["L1_gnn_ln_g"], A["L1_gnn_ln_b"]))
        self_loops(nc, m, "s3", D, 1, None, LOOPS, at=D + 1)
        attend(nc, m, "t3", 1, m.atable[1])
        project(nc, m, "gatep", "ln", m.W["gat"], 20, heads=4, table=m.gtable, first="both", gat=1,
                params=(A["L1_gnn_b2"],))
        if upto == 3:
            return store_x(nc, m, out)
        self_loops(nc, m, "s4", 16, 4, m.gedu, N)
        gate_attend_and_experts(nc, m, A)
        with nc.sbuf_tensor("results", [P, 2, KEXP, U, D], F32) as y:
            gates(nc, m, A, y)
            mix_experts(nc, m, y, out)


_INS = ['x', 'src', 'dst', 'edge_weight', 'L0_gnn_W1', 'L0_gnn_W2', 'L0_ffn_gate_w', 'L0_ffn_gate_b', 'L0_ffn_w1',
        'L0_ffn_b1', 'L0_ffn_w2', 'L0_ffn_b2', 'L1_gnn_W1', 'L1_gnn_a1_src', 'L1_gnn_a1_dst', 'L1_gnn_b1',
        'L1_gnn_ln_g', 'L1_gnn_ln_b', 'L1_gnn_W2', 'L1_gnn_a2_src', 'L1_gnn_a2_dst', 'L1_gnn_b2', 'L1_ffn_W_gat',
        'L1_ffn_att_src', 'L1_ffn_att_dst', 'L1_ffn_b_gat', 'L1_ffn_ln_gamma', 'L1_ffn_ln_beta', 'L1_ffn_W1',
        'L1_ffn_b1', 'L1_ffn_W2', 'L1_ffn_b2', 'L1_ffn_edge_index']


def kernel(**inputs):
    import numpy as _np
    import concourse.bacc as _bacc
    from concourse import mybir as _mybir
    from concourse.bass_utils import run_bass_kernel_spmd as _run

    nc = _bacc.Bacc("TRN2", target_bir_lowering=False, num_devices=1)
    arrays, args = {}, {}
    for name in _INS:
        a = _np.ascontiguousarray(inputs[name])
        arrays[f"in_{name}_dram"] = a
        args[name] = nc.dram_tensor(f"in_{name}_dram", a.shape, _mybir.dt.from_np(a.dtype), kind="ExternalInput").ap()
    out = nc.dram_tensor("out_0_dram", (N, D), _mybir.dt.float32, kind="ExternalOutput").ap()
    program(nc, args, out)
    r = _run(nc, [arrays], core_ids=[0])
    return r.results[0]["out_0_dram"]
```
